# Optimizing a Trainium2 kernel written in Bass

```python
import numpy as np
import jax
import jax.numpy as jnp

def _softmax(x, axis=-1):
    return jax.nn.softmax(x, axis=axis)

def _gelu(x):
    return jax.nn.gelu(x, approximate=True)

def _silu(x):
    return jax.nn.silu(x)

def _sigmoid(x):
    return jax.nn.sigmoid(x)

def _layernorm(x, axis=-1, eps=1e-05):
    m = jnp.mean(x, axis=axis, keepdims=True)
    v = jnp.var(x, axis=axis, keepdims=True)
    return (x - m) / jnp.sqrt(v + eps)

def _scatter_add(tgt, idx, src, axis=0):
    return tgt.at[idx].add(src)

def _segment_sum(src, seg, n):
    return jax.ops.segment_sum(src, seg, n)
kernel_name = 'mk_hybrid_d1_jaxref_r8_83f3b5'

def setup_inputs(seed: int=0):
    np.random.seed(seed)
    _w = jnp.asarray

    def _L0_attn_a_setup():
        import jax, jax.numpy as jnp
        import numpy as np
        D_MODEL = 128
        N_HEADS = 16
        D_HEAD = D_MODEL // N_HEADS
        BATCH = 2
        SEQ = 256
        key = jax.random.key(seed)
        ks = jax.random.split(key, 5)
        s = 1.0 / np.sqrt(D_MODEL)
        return {'x': jax.random.normal(ks[0], (BATCH, SEQ, D_MODEL), dtype=jnp.float32), 'W_qkv': jax.random.normal(ks[1], (3 * D_MODEL, D_MODEL), dtype=jnp.float32) * s, 'b_qkv': jax.random.normal(ks[2], (3 * D_MODEL,), dtype=jnp.float32) * 0.01, 'W_out': jax.random.normal(ks[3], (D_MODEL, D_MODEL), dtype=jnp.float32) * s, 'b_out': jax.random.normal(ks[4], (D_MODEL,), dtype=jnp.float32) * 0.01}
    _L0_attn_a_in = _L0_attn_a_setup()

    def _L0_attn_b_setup():
        import jax, jax.numpy as jnp
        import numpy as np
        NHEADS = 16
        SCALE_BASE = 64
        GN_EPS = 1e-05

        def rotate_every_two(x):
            x1 = x[..., ::2]
            x2 = x[..., 1::2]
            return jnp.stack((-x2, x1), axis=-1).reshape(x.shape)

        def xpos_apply(x, downscale, offset=0):
            B, T, C = x.shape
            half = C // 2
            scale_vec = (jnp.arange(0, C, 2, dtype=jnp.float32) + 0.4 * C) / (1.4 * C)
            min_pos = -(T + offset) // 2
            max_pos = T + offset + min_pos
            power = jnp.arange(min_pos, max_pos, dtype=jnp.float32) / SCALE_BASE
            scale = scale_vec[None, :] ** power[:, None]
            L = scale.shape[0]
            inv_freq = 1.0 / 10000.0 ** (jnp.arange(half, dtype=jnp.float32) / half)
            sinusoid = jnp.arange(L, dtype=jnp.float32)[:, None] * inv_freq[None, :]
            sin, cos = (jnp.sin(sinusoid), jnp.cos(sinusoid))
            if L > T:
                scale, sin, cos = (scale[-T:], sin[-T:], cos[-T:])
            if downscale:
                scale = 1.0 / scale
            sin = jnp.repeat(sin * scale, 2, axis=-1)
            cos = jnp.repeat(cos * scale, 2, axis=-1)
            return x * cos + rotate_every_two(x) * sin

        def decay_mask(nheads, T):
            gamma = 1.0 - 2.0 ** (-5.0 - jnp.arange(nheads, dtype=jnp.float32))
            idx = jnp.arange(T)
            diff = idx[:, None] - idx[None, :]
            keep = diff >= 0
            m = gamma[:, None, None] ** jnp.where(keep, diff, 0).astype(jnp.float32)
            return jnp.where(keep[None, :, :], m, 0.0)
        key = jax.random.key(seed)
        ks = jax.random.split(key, 6)
        B, T, C = (2, 256, 128)
        w_std = 0.02
        return {'x': jax.random.normal(ks[0], (B, T, C), jnp.float32), 'w_qkvff': jax.random.normal(ks[1], (5 * C, C), jnp.float32) * w_std, 'w_gated': jax.random.normal(ks[2], (C, C), jnp.float32) * w_std, 'b_gated': jnp.zeros((C,), jnp.float32), 'w_proj': jax.random.normal(ks[3], (C, C), jnp.float32) * w_std, 'b_proj': jnp.zeros((C,), jnp.float32), 'gn_w': jnp.ones((C,), jnp.float32), 'gn_b': jnp.zeros((C,), jnp.float32), 'w_ff': jax.random.normal(ks[4], (C, 2 * C), jnp.float32) * w_std, 'rms_w': jnp.ones((C,), jnp.float32)}
    _L0_attn_b_in = _L0_attn_b_setup()

    def _L0_ffn_setup():
        import math
        import jax, jax.numpy as jnp
        import numpy as np
        H = 128
        F = 512
        E = 8
        TOP_K = 2
        CAP_FACTOR = 1.25
        MIN_CAP = 4
        SHARED_SCALE = 0.1

        def _top2_gating(logits, capacity):
            N, nE = logits.shape
            gates = jax.nn.softmax(logits, axis=-1)
            idx1 = jnp.argmax(gates, axis=-1)
            mask1 = jax.nn.one_hot(idx1, nE, dtype=gates.dtype)
            idx2 = jnp.argmax(gates * (1.0 - mask1), axis=-1)
            mask2 = jax.nn.one_hot(idx2, nE, dtype=gates.dtype)
            pos1 = jnp.cumsum(mask1, axis=0) - mask1
            mask1 = mask1 * (pos1 < capacity)
            pos2 = jnp.cumsum(mask2, axis=0) - mask2 + jnp.sum(mask1, axis=0, keepdims=True)
            mask2 = mask2 * (pos2 < capacity)
            g1 = jnp.sum(gates * mask1, axis=-1)
            g2 = jnp.sum(gates * mask2, axis=-1)
            denom = jnp.maximum(g1 + g2, jnp.finfo(gates.dtype).eps)
            g1, g2 = (g1 / denom, g2 / denom)
            loc1 = jnp.sum(pos1 * mask1, axis=-1).astype(jnp.int32)
            loc2 = jnp.sum(pos2 * mask2, axis=-1).astype(jnp.int32)
            oh1 = jax.nn.one_hot(loc1, capacity, dtype=gates.dtype)
            oh2 = jax.nn.one_hot(loc2, capacity, dtype=gates.dtype)
            combine = (g1[:, None] * mask1)[:, :, None] * oh1[:, None, :] + (g2[:, None] * mask2)[:, :, None] * oh2[:, None, :]
            dispatch = (combine > 0).astype(gates.dtype)
            return (combine, dispatch)
        key = jax.random.key(seed)
        ks = jax.random.split(key, 10)
        s_h = 1.0 / math.sqrt(H)
        s_f = 1.0 / math.sqrt(F)
        return {'hidden_states': jax.random.normal(ks[0], (2, 256, H), jnp.float32), 'router_w': jax.random.uniform(ks[1], (H, E), jnp.float32, -s_h, s_h), 'w1': jax.random.uniform(ks[2], (E, H, F), jnp.float32, -s_h, s_h), 'b1': jax.random.uniform(ks[3], (E, F), jnp.float32, -s_h, s_h), 'w2': jax.random.uniform(ks[4], (E, F, H), jnp.float32, -s_f, s_f), 'b2': jax.random.uniform(ks[5], (E, H), jnp.float32, -s_f, s_f), 'sw1': jax.random.uniform(ks[6], (H, F), jnp.float32, -s_h, s_h), 'sb1': jax.random.uniform(ks[7], (F,), jnp.float32, -s_h, s_h), 'sw2': jax.random.uniform(ks[8], (F, H), jnp.float32, -s_f, s_f), 'sb2': jax.random.uniform(ks[9], (H,), jnp.float32, -s_f, s_f)}
    _L0_ffn_in = _L0_ffn_setup()
    _d = {'L0_attn_a_x': _L0_attn_a_in['x'], 'L0_attn_a_W_qkv': _L0_attn_a_in['W_qkv'], 'L0_attn_a_b_qkv': _L0_attn_a_in['b_qkv'], 'L0_attn_a_W_out': _L0_attn_a_in['W_out'], 'L0_attn_a_b_out': _L0_attn_a_in['b_out'], 'L0_attn_b_w_qkvff': _L0_attn_b_in['w_qkvff'], 'L0_attn_b_w_gated': _L0_attn_b_in['w_gated'], 'L0_attn_b_b_gated': _L0_attn_b_in['b_gated'], 'L0_attn_b_w_proj': _L0_attn_b_in['w_proj'], 'L0_attn_b_b_proj': _L0_attn_b_in['b_proj'], 'L0_attn_b_gn_w': _L0_attn_b_in['gn_w'], 'L0_attn_b_gn_b': _L0_attn_b_in['gn_b'], 'L0_attn_b_w_ff': _L0_attn_b_in['w_ff'], 'L0_attn_b_rms_w': _L0_attn_b_in['rms_w'], 'L0_ffn_router_w': _L0_ffn_in['router_w'], 'L0_ffn_w1': _L0_ffn_in['w1'], 'L0_ffn_b1': _L0_ffn_in['b1'], 'L0_ffn_w2': _L0_ffn_in['w2'], 'L0_ffn_b2': _L0_ffn_in['b2'], 'L0_ffn_sw1': _L0_ffn_in['sw1'], 'L0_ffn_sb1': _L0_ffn_in['sb1'], 'L0_ffn_sw2': _L0_ffn_in['sw2'], 'L0_ffn_sb2': _L0_ffn_in['sb2']}
    _x0 = _d['L0_attn_a_x']
    _d['L0_attn_a_x'] = jax.random.normal(jax.random.fold_in(jax.random.key(seed), 1), (4, 1024, 128), dtype=_x0.dtype)
    del _x0
    return _d

def reference(L0_attn_a_x, L0_attn_a_W_qkv, L0_attn_a_b_qkv, L0_attn_a_W_out, L0_attn_a_b_out, L0_attn_b_w_qkvff, L0_attn_b_w_gated, L0_attn_b_b_gated, L0_attn_b_w_proj, L0_attn_b_b_proj, L0_attn_b_gn_w, L0_attn_b_gn_b, L0_attn_b_w_ff, L0_attn_b_rms_w, L0_ffn_router_w, L0_ffn_w1, L0_ffn_b1, L0_ffn_w2, L0_ffn_b2, L0_ffn_sw1, L0_ffn_sb1, L0_ffn_sw2, L0_ffn_sb2):

    def _L0_attn_a_ref(x, W_qkv, b_qkv, W_out, b_out):
        import jax, jax.numpy as jnp
        import numpy as np
        D_MODEL = 128
        N_HEADS = 16
        D_HEAD = D_MODEL // N_HEADS
        BATCH = 2
        SEQ = 256
        b, s, d = x.shape
        qkv = x @ W_qkv.T + b_qkv
        qkv = qkv.reshape(b, s, N_HEADS, 3 * D_HEAD)
        q = qkv[..., :D_HEAD]
        k = qkv[..., D_HEAD:2 * D_HEAD]
        v = qkv[..., 2 * D_HEAD:]
        scale = np.sqrt(D_HEAD).astype(np.float32)
        scores = jnp.einsum('bqhd,bkhd->bhqk', q, k) / scale
        attn = jax.nn.softmax(scores, axis=-1)
        out = jnp.einsum('bhqk,bkhd->bqhd', attn, v)
        out = out.reshape(b, s, d)
        return out @ W_out.T + b_out

    def _L0_attn_b_ref(x, w_qkvff, w_gated, b_gated, w_proj, b_proj, gn_w, gn_b, w_ff, rms_w):
        import jax, jax.numpy as jnp
        import numpy as np
        NHEADS = 16
        SCALE_BASE = 64
        GN_EPS = 1e-05

        def rotate_every_two(x):
            x1 = x[..., ::2]
            x2 = x[..., 1::2]
            return jnp.stack((-x2, x1), axis=-1).reshape(x.shape)

        def xpos_apply(x, downscale, offset=0):
            B, T, C = x.shape
            half = C // 2
            scale_vec = (jnp.arange(0, C, 2, dtype=jnp.float32) + 0.4 * C) / (1.4 * C)
            min_pos = -(T + offset) // 2
            max_pos = T + offset + min_pos
            power = jnp.arange(min_pos, max_pos, dtype=jnp.float32) / SCALE_BASE
            scale = scale_vec[None, :] ** power[:, None]
            L = scale.shape[0]
            inv_freq = 1.0 / 10000.0 ** (jnp.arange(half, dtype=jnp.float32) / half)
            sinusoid = jnp.arange(L, dtype=jnp.float32)[:, None] * inv_freq[None, :]
            sin, cos = (jnp.sin(sinusoid), jnp.cos(sinusoid))
            if L > T:
                scale, sin, cos = (scale[-T:], sin[-T:], cos[-T:])
            if downscale:
                scale = 1.0 / scale
            sin = jnp.repeat(sin * scale, 2, axis=-1)
            cos = jnp.repeat(cos * scale, 2, axis=-1)
            return x * cos + rotate_every_two(x) * sin

        def decay_mask(nheads, T):
            gamma = 1.0 - 2.0 ** (-5.0 - jnp.arange(nheads, dtype=jnp.float32))
            idx = jnp.arange(T)
            diff = idx[:, None] - idx[None, :]
            keep = diff >= 0
            m = gamma[:, None, None] ** jnp.where(keep, diff, 0).astype(jnp.float32)
            return jnp.where(keep[None, :, :], m, 0.0)
        B, T, C = x.shape
        H = NHEADS
        hd = C // H
        nrm = jnp.sqrt(jnp.sum(x * x, axis=-1, keepdims=True)) * C ** (-0.5)
        x_ = x / jnp.maximum(nrm, 1e-08) * rms_w
        qkvff = jnp.einsum('btc,oc->bto', x_, w_qkvff)
        q, k, v, ff = jnp.split(qkvff, [C, 2 * C, 3 * C], axis=-1)
        q = xpos_apply(q, downscale=False)
        k = xpos_apply(k, downscale=True)
        q = q.reshape(B, T, H, hd).transpose(0, 2, 1, 3)
        k = k.reshape(B, T, H, hd).transpose(0, 2, 1, 3)
        v = v.reshape(B, T, H, hd).transpose(0, 2, 1, 3)
        scores = jnp.einsum('bhtd,bhsd->bhts', q, k) * hd ** (-0.5)
        scores = scores * decay_mask(H, T)[None]
        y = jnp.einsum('bhts,bhsd->bhtd', scores, v)
        yg = y.transpose(0, 2, 1, 3).reshape(B * T, H, hd)
        mu = jnp.mean(yg, axis=-1, keepdims=True)
        var = jnp.mean((yg - mu) ** 2, axis=-1, keepdims=True)
        yg = (yg - mu) / jnp.sqrt(var + GN_EPS)
        y = yg.reshape(B * T, C) * gn_w + gn_b
        y = y.reshape(B, T, C)
        y = jax.nn.silu(jnp.einsum('btc,oc->bto', x, w_gated) + b_gated) * y
        y = jnp.einsum('btc,oc->bto', y, w_proj) + b_proj
        ff_out = jnp.einsum('bte,ce->btc', jax.nn.gelu(ff, approximate=False), w_ff)
        return x + ff_out + y

    def _L0_ffn_ref(hidden_states, router_w, w1, b1, w2, b2, sw1, sb1, sw2, sb2):
        import math
        import jax, jax.numpy as jnp
        import numpy as np
        H = 128
        F = 512
        E = 8
        TOP_K = 2
        CAP_FACTOR = 1.25
        MIN_CAP = 4
        SHARED_SCALE = 0.1

        def _top2_gating(logits, capacity):
            N, nE = logits.shape
            gates = jax.nn.softmax(logits, axis=-1)
            idx1 = jnp.argmax(gates, axis=-1)
            mask1 = jax.nn.one_hot(idx1, nE, dtype=gates.dtype)
            idx2 = jnp.argmax(gates * (1.0 - mask1), axis=-1)
            mask2 = jax.nn.one_hot(idx2, nE, dtype=gates.dtype)
            pos1 = jnp.cumsum(mask1, axis=0) - mask1
            mask1 = mask1 * (pos1 < capacity)
            pos2 = jnp.cumsum(mask2, axis=0) - mask2 + jnp.sum(mask1, axis=0, keepdims=True)
            mask2 = mask2 * (pos2 < capacity)
            g1 = jnp.sum(gates * mask1, axis=-1)
            g2 = jnp.sum(gates * mask2, axis=-1)
            denom = jnp.maximum(g1 + g2, jnp.finfo(gates.dtype).eps)
            g1, g2 = (g1 / denom, g2 / denom)
            loc1 = jnp.sum(pos1 * mask1, axis=-1).astype(jnp.int32)
            loc2 = jnp.sum(pos2 * mask2, axis=-1).astype(jnp.int32)
            oh1 = jax.nn.one_hot(loc1, capacity, dtype=gates.dtype)
            oh2 = jax.nn.one_hot(loc2, capacity, dtype=gates.dtype)
            combine = (g1[:, None] * mask1)[:, :, None] * oh1[:, None, :] + (g2[:, None] * mask2)[:, :, None] * oh2[:, None, :]
            dispatch = (combine > 0).astype(gates.dtype)
            return (combine, dispatch)
        B, S, h = hidden_states.shape
        x = hidden_states.reshape(-1, h)
        N = x.shape[0]
        capacity = min(max(MIN_CAP, math.ceil(TOP_K * CAP_FACTOR * N / E)), N)
        logits = x @ router_w
        combine, dispatch = _top2_gating(logits, capacity)
        expert_in = jnp.einsum('nec,nh->ech', dispatch, x)
        hmid = jax.nn.silu(jnp.einsum('ech,ehf->ecf', expert_in, w1) + b1[:, None, :])
        expert_out = jnp.einsum('ecf,efh->ech', hmid, w2) + b2[:, None, :]
        y = jnp.einsum('nec,ech->nh', combine, expert_out)
        shared = jax.nn.silu(x @ sw1 + sb1) @ sw2 + sb2
        out = y + SHARED_SCALE * shared
        return out.reshape(B, S, h)
    x = L0_attn_a_x
    x = x + _L0_attn_a_ref(_layernorm(x, axis=-1), L0_attn_a_W_qkv, L0_attn_a_b_qkv, L0_attn_a_W_out, L0_attn_a_b_out)
    x = x + _L0_ffn_ref(_layernorm(x, axis=-1), L0_ffn_router_w, L0_ffn_w1, L0_ffn_b1, L0_ffn_w2, L0_ffn_b2, L0_ffn_sw1, L0_ffn_sb1, L0_ffn_sw2, L0_ffn_sb2)
    x = x + _L0_attn_b_ref(_layernorm(x, axis=-1), L0_attn_b_w_qkvff, L0_attn_b_w_gated, L0_attn_b_b_gated, L0_attn_b_w_proj, L0_attn_b_b_proj, L0_attn_b_gn_w, L0_attn_b_gn_b, L0_attn_b_w_ff, L0_attn_b_rms_w)
    x = x + _L0_ffn_ref(_layernorm(x, axis=-1), L0_ffn_router_w, L0_ffn_w1, L0_ffn_b1, L0_ffn_w2, L0_ffn_b2, L0_ffn_sw1, L0_ffn_sb1, L0_ffn_sw2, L0_ffn_sb2)
    return x

_drawn_inputs = setup_inputs


def setup_inputs(seed=0):
    import zlib

    import numpy as np

    out = dict(_drawn_inputs(seed))
    spreads = {'L0_attn_b_b_gated': (0.0, 0.8),
     'L0_attn_b_b_proj': (0.0, 0.1),
     'L0_attn_b_gn_w': (1.0, 0.6),
     'L0_attn_b_gn_b': (0.0, 0.8),
     'L0_attn_b_rms_w': (1.0, 0.6)}
    factors = {'L0_attn_a_b_qkv': 4.187,
     'L0_attn_a_b_out': 3.637,
     'L0_attn_b_w_gated': 3.872,
     'L0_attn_b_w_proj': 3.479,
     'L0_ffn_b1': 3.072,
     'L0_ffn_sb1': 22.672,
     'L0_ffn_sb2': 8.0}
    for name, (base, spread) in spreads.items():
        noise = np.random.default_rng([zlib.crc32(name.encode()), seed]).standard_normal(out[name].shape)
        drawn = base * np.exp(spread * noise) if base else spread * noise
        out[name] = jnp.asarray(drawn.astype(out[name].dtype))
    for name, factor in factors.items():
        out[name] = (out[name] * factor).astype(out[name].dtype)
    return out
```

```python
from contextlib import ExitStack

import concourse.bass as bass
from concourse import mybir

F32 = mybir.dt.float32
BF16 = mybir.dt.bfloat16
ALU = mybir.AluOpType
ACT = mybir.ActivationFunctionType
AX = mybir.AxisListType

P = 128
D = 128
BATCH, SEQ = 4, 1024
TOKENS = BATCH * SEQ
TILES = TOKENS // P
CH = 512
CT = CH // P
CHUNKS = TOKENS // CH
HEADS = 16
HD = D // HEADS
LN_EPS = 1e-5

JH = 4
GROUPS = BATCH * HEADS // JH
QROWS = 6 * HD
AROWS = QROWS + 3
KT = SEQ // P
VW = 32

EXPERTS = 8
FF = 512
FT = FF // P
CAP = 1280
FLOOR = -103.0
GATE_EPS = 1.1920929e-07
SHARED = 0.1

RL = 128
GN_EPS = 1e-5


class Count:

    def __init__(self, eng, sem, turn=0, each=0):
        self.eng, self.sem, self.turn, self.each, self.n = eng, sem, turn, each, 0

    def mark(self, ins, by=1):
        ins.then_inc(self.sem, by)
        self.n += by

    def settle(self, eng=None):
        (eng or self.eng).wait_ge(self.sem, self.turn * self.each + self.n)


class Buffers:
    pass


def ring(stack, make, name, n, shape, dt):
    return [stack.enter_context(make(f"{name}{i}", shape, dt)) for i in range(n)]


def load_stage(nc, T, I):
    with ExitStack() as st:
        loaded = st.enter_context(nc.semaphore("ld_loaded"))
        weights = st.enter_context(nc.semaphore("ld_weights"))
        blank = st.enter_context(nc.semaphore("ld_blank"))
        block = st.enter_context(nc.Block())
        xt = I["x"].rearrange("b (t p) d -> p (b t) d", p=P)

        @block.sync
        def _(sp):
            for c in range(CHUNKS):
                sp.dma_start(T.X[:, CT * c:CT * (c + 1), :], xt[:, CT * c:CT * (c + 1), :]).then_inc(loaded, 16)
            sp.dma_start(T.upper[:, :], I["upper"]).then_inc(loaded, 16)
            sp.dma_start(T.rank[:, :], I["rank"].partition_broadcast(P)).then_inc(loaded, 16)
            sp.dma_start(T.bo[:, :], I["b_out"].partition_broadcast(P)).then_inc(loaded, 16)
            sp.wait_ge(loaded, 16 * (CHUNKS + 3))

        @block.scalar
        def _(act):
            act.dma_start(T.w1[:, :, :], I["w1"].rearrange("e h f -> h e f")).then_inc(weights, 16)
            act.dma_start(T.w2[:, :, :, :], I["w2"].rearrange("e (c p) h -> p e c h", p=P)).then_inc(weights, 16)
            act.dma_start(T.sw1[:, :], I["sw1"]).then_inc(weights, 16)
            act.dma_start(T.sw2[:, :, :], I["sw2"].rearrange("(c p) h -> p c h", p=P)).then_inc(weights, 16)
            act.dma_start(T.rw[:, :], I["rw"]).then_inc(weights, 16)
            act.dma_start(T.b1[:, :], I["b1cols"]).then_inc(weights, 16)
            act.dma_start(T.b2[:, :], I["b2cols"]).then_inc(weights, 16)
            act.wait_ge(weights, 16 * 7)

        @block.gpsimd
        def _(pool):
            pool.memset(T.ident[:, :], 0.0).then_inc(blank, 1)
            pool.memset(T.ones[:, :], 1.0)
            pool.wait_ge(blank, 1)
            pool.affine_select(out=T.ident[:, :], in_=T.ident[:, :], compare_op=ALU.not_equal, fill=1.0,
                               base=0, pattern=[[-1, P]], channel_multiplier=1).then_inc(blank, 1)


def norm_stage(nc, T, tag, turn=True):
    with ExitStack() as st:
        sem = lambda n: st.enter_context(nc.semaphore(f"{tag}_{n}"))
        stats, spread, root, xh_ready, turned, copied = map(
            sem, ("stats", "spread", "root", "xh_ready", "turned", "copied"))
        XH = ring(st, nc.sbuf_tensor, f"{tag}_xh", 2, [P, CT, D], F32)
        pst = ring(st, nc.psum_tensor, f"{tag}_ps", 2, [P, CH], F32)
        bn = st.enter_context(nc.sbuf_tensor(f"{tag}_bn", [P, TILES, 6], F32))
        block = st.enter_context(nc.Block())

        @block.vector
        def _(dve):
            with dve.Fori(0, TILES // CT) as i:
                t = i * CT
                for k in range(CT):
                    nc.vector.bn_stats(bn[:, bass.ds(t + k, 1), :].rearrange("p t s -> p (t s)"),
                                       T.X[:, bass.ds(t + k, 1), :].rearrange("p t d -> p (t d)")).then_inc(stats, 1)
            dve.wait_ge(stats, TILES)
            mean, var, dif, sq = T.mv[:, :, 0], T.mv[:, :, 1], T.sd[:, :], T.rs[:, :]
            nc.vector.tensor_tensor(mean, bn[:, :, 1], bn[:, :, 4], ALU.add).then_inc(spread, 1)
            nc.vector.tensor_tensor(dif, bn[:, :, 1], bn[:, :, 4], ALU.subtract).then_inc(spread, 1)
            nc.vector.tensor_tensor(var, bn[:, :, 2], bn[:, :, 5], ALU.add).then_inc(spread, 1)
            dve.wait_ge(spread, 3)
            nc.vector.tensor_scalar(mean, mean, 0.5, None, ALU.mult).then_inc(spread, 1)
            nc.vector.tensor_tensor(sq, dif, dif, ALU.mult).then_inc(spread, 1)
            nc.vector.tensor_scalar(var, var, 1.0 / D, None, ALU.mult).then_inc(spread, 1)
            dve.wait_ge(spread, 6)
            nc.vector.scalar_tensor_tensor(out=var, in0=sq, scalar=0.25, in1=var, op0=ALU.mult, op1=ALU.add).then_inc(spread, 1)
            dve.wait_ge(spread, 7)
            nc.vector.tensor_scalar(T.sd[:, :], var, LN_EPS, None, ALU.add).then_inc(spread, 1)
            dve.wait_ge(root, 1)
            nc.vector.reciprocal(T.rs[:, :], T.sd[:, :]).then_inc(root, 1)
            dve.wait_ge(root, 2)
            if not turn:
                nc.vector.tensor_tensor(T.ri[:, :], T.ri[:, :], T.rs[:, :], ALU.mult).then_inc(root, 1)
                dve.wait_ge(root, 3)
                nc.vector.tensor_scalar(T.ri[:, :], T.ri[:, :], 1e-8, None, ALU.max).then_inc(root, 1)
                dve.wait_ge(root, 4)
                nc.vector.reciprocal(T.ri[:, :], T.ri[:, :]).then_inc(root, 1)
                dve.wait_ge(root, 5)
                nc.vector.tensor_tensor(T.ri[:, :], T.ri[:, :], T.rs[:, :], ALU.mult)
                return
            with dve.Fori(0, CHUNKS // 2) as i:
                for a in range(2):
                    dve.wait_ge(turned, 2 * i + a + 1)
                    for k in range(CT):
                        t = i * (2 * CT) + (a * CT + k)
                        ins = nc.vector.tensor_scalar(XH[a][:, k, :], T.X[:, bass.ds(t, 1), :].rearrange("p t d -> p (t d)"),
                                                      T.mv[:, bass.ds(t, 1), 0:1].rearrange("p t s -> p (t s)"),
                                                      T.rs[:, bass.ds(t, 1)], ALU.subtract, ALU.mult)
                    ins.then_inc(xh_ready, 1)

        @block.tensor
        def _(pe):
            if not turn:
                return
            pe.sem_inc(turned, 2)
            with pe.Fori(0, CHUNKS // 2) as i:
                for a in range(2):
                    pe.wait_ge(xh_ready, 2 * i + a + 1)
                    pe.wait_ge(copied, 2 * i + a + 1)
                    for k in range(CT):
                        ins = nc.tensor.transpose(pst[a][:, k * P:(k + 1) * P], XH[a][:, k, :], T.ident[:, :])
                    ins.then_inc(turned, 1)

        @block.scalar
        def _(act):
            act.sem_inc(copied, 2)
            act.wait_ge(spread, 8)
            if not turn:
                nc.scalar.activation(T.ri[:, :], T.mv[:, :, 1], ACT.Sqrt)
            nc.scalar.activation(T.sd[:, :], T.sd[:, :], ACT.Sqrt).then_inc(root, 1)
            if not turn:
                return
            with act.Fori(0, CHUNKS // 2) as i:
                for a in range(2):
                    act.wait_ge(turned, 2 * i + a + 3)
                    nc.scalar.copy(T.XT[:, bass.ds(i * (2 * CH) + a * CH, CH)], pst[a][:, :]).then_inc(copied, 1)


def qkv_stage(nc, T, I, S):
    with ExitStack() as st:
        sem = lambda n: st.enter_context(nc.semaphore(f"qkv_{n}"))
        weights, projected, evacuated, vturned, vkept, split, cleared = map(
            sem, ("weights", "projected", "evacuated", "vturned", "vkept", "split", "cleared"))
        stored = [sem("stored0"), sem("stored1")]
        chain = sem("chain")
        wqkv = st.enter_context(nc.sbuf_tensor("qkv_w", [P, 3, D], F32))
        bqkv = st.enter_context(nc.sbuf_tensor("qkv_b", [P, 3], F32))
        zero = st.enter_context(nc.sbuf_tensor("qkv_zero", [QROWS, 8, SEQ], BF16))
        QK = ring(st, nc.sbuf_tensor, "qkv_qk", 2, [P, 2, CH], F32)
        R = ring(st, nc.sbuf_tensor, "qkv_r", 2, [P, 2, CH], F32)
        VT = ring(st, nc.sbuf_tensor, "qkv_vt", 2, [P, CH], F32)
        part = ring(st, nc.sbuf_tensor, "qkv_part", 2, [P, 3, 2, CH], BF16)
        ps = [ring(st, nc.psum_tensor, f"qkv_ps{w}", 2, [P, CH], F32) for w in range(3)]
        pvt = ring(st, nc.psum_tensor, "qkv_pvt", 2, [P, CH], F32)
        block = st.enter_context(nc.Block())
        QP, KP = (0, 0, 0, 1, 1, 2), (0, 1, 2, 0, 1, 0)
        sq = S.q.rearrange("g j (r d) t -> (g j) r d t", d=HD)
        sk = S.k.rearrange("g j (r d) t -> (g j) r d t", d=HD)

        @block.sync
        def _(sp):
            sp.dma_start(wqkv[:, :, :], I["w_qkv"]).then_inc(weights, 16)
            sp.dma_start(bqkv[:, :], I["b_qkv"]).then_inc(weights, 16)
            for a in range(2):
                sp.sem_inc(stored[a], 16)
            with sp.Fori(0, BATCH) as b:
                for a in range(2):
                    sp.wait_ge(split, 2 * b + a + 1)
                    for r in range(6):
                        for s, w, n in ((sq, 0, QP[r]), (sk, 1, KP[r])):
                            sp.dma_start(s[bass.ds(b * HEADS, HEADS), r, :, a * CH:(a + 1) * CH],
                                         part[a][:, n, w, :]).then_inc(stored[a], 16)
            sp.wait_ge(cleared, 1)
            for s in (S.q, S.k):
                sp.dma_start(s[GROUPS:GROUPS + 2, :, :, :].rearrange("g j r t -> r (g j) t"), zero[:, :, :]).then_inc(weights, 16)
            sp.wait_ge(weights, 64)
            for a in range(2):
                sp.wait_ge(stored[a], BATCH * 12 * 16 + 16)

        @block.tensor
        def _(pe):
            pe.wait_ge(weights, 32)
            with pe.Fori(0, BATCH) as b:
                for a in range(2):
                    c = 2 * b + a
                    pe.wait_ge(evacuated, 3 * c + 3)
                    for w in (2, 0, 1):
                        nc.tensor.matmul(ps[w][a][:, :], wqkv[:, w, :], T.XT[:, bass.ds(b * SEQ + a * CH, CH)],
                                         start=True, stop=True).then_inc(projected, 1)
                    pe.wait_ge(evacuated, 3 * c + 7)
                    pe.wait_ge(vkept, c + 1)
                    for k in range(CT):
                        ins = nc.tensor.transpose(pvt[a][:, k * P:(k + 1) * P], VT[a][:, k * P:(k + 1) * P], T.ident[:, :])
                    ins.then_inc(vturned, 1)

        @block.scalar
        def _(act):
            act.sem_inc(evacuated, 6)
            act.sem_inc(vkept, 2)
            act.wait_ge(weights, 32)
            with act.Fori(0, BATCH) as b:
                for a in range(2):
                    c = 2 * b + a
                    act.wait_ge(projected, 3 * c + 1)
                    nc.scalar.activation(VT[a][:, :], ps[2][a][:, :], ACT.Identity, bias=bqkv[:, 2:3]).then_inc(evacuated, 1)
                    act.wait_ge(chain, 6 * b + 3 * a + 2)
                    for w in range(2):
                        act.wait_ge(projected, 3 * c + 2 + w)
                        nc.scalar.activation(QK[a][:, w, :], ps[w][a][:, :], ACT.Identity,
                                             bias=bqkv[:, w:w + 1]).then_inc(evacuated, 1)
                    act.wait_ge(vturned, c + 1)
                    nc.scalar.copy(T.V[:, bass.ds(b * 4, 4), CT * a:CT * (a + 1), :],
                                   pvt[a][:, :].rearrange("p (t g e) -> p g t e", t=CT, g=4)).then_inc(vkept, 1)

        @block.vector
        def _(dve):
            dve.sem_inc(chain, 6)
            with dve.Fori(0, BATCH) as b:
                link = Count(dve, chain, b, 6)
                link.n = 6
                for a in range(2):
                    dve.wait_ge(evacuated, 6 * b + 3 * a + 9)
                    dve.wait_ge(stored[a], 12 * 16 * b + 16)
                    q, r, p = QK[a][:, :, :], R[a][:, :, :], part[a]
                    link.mark(nc.vector.tensor_copy(p[:, 0, :, :], q))
                    link.settle()
                    link.mark(nc.vector.tensor_tensor(r, q, p[:, 0, :, :], ALU.subtract))
                    link.settle()
                    link.mark(nc.vector.tensor_copy(p[:, 1, :, :], r))
                    link.settle()
                    nc.vector.tensor_tensor(p[:, 2, :, :], r, p[:, 1, :, :], ALU.subtract).then_inc(split, 1)

        @block.gpsimd
        def _(pool):
            pool.memset(zero[:, :, :], 0.0).then_inc(cleared, 1)
            pool.memset(T.V[:, GROUPS, :, :], 0.0)
            with pool.Fori(0, TILES // CT) as i:
                xs = T.X[:, bass.ds(i * CT, CT), :]
                pool.tensor_tensor(xs, xs, T.bo[:, :].unsqueeze(1).to_broadcast([P, CT, D]), ALU.add)


def attention_stage(nc, T, S):
    STEPS = 16
    EXPS = 2 * STEPS
    HIGHS = JH * KT * 2
    HALF = HIGHS // 2
    with ExitStack() as st:
        sem = lambda n: st.enter_context(nc.semaphore(f"at_{n}"))
        (scored, exped, multiplied, o_kept, high_scored, high_kept, low_ready, low_turned, low_split,
         v_staged, chain, blanked) = map(sem, (
             "scored", "exped", "multiplied", "o_kept", "high_scored", "high_kept", "low_ready",
             "low_turned", "low_split", "v_staged", "chain", "blanked"))
        high_loaded = [sem("high_loaded0"), sem("high_loaded1")]
        loaded = [sem("loaded0"), sem("loaded1")]
        rows_stored, rows_loaded = sem("rows_stored"), [sem("rows_loaded0"), sem("rows_loaded1")]
        o_stored = [sem("o_stored0"), sem("o_stored1")]
        hq = ring(st, nc.sbuf_tensor, "at_hq", 2, [P, 2, SEQ], BF16)
        hk = ring(st, nc.sbuf_tensor, "at_hk", 2, [P, 2, SEQ], BF16)
        eq = ring(st, nc.sbuf_tensor, "at_eq", 2, [P, 2, SEQ], BF16)
        ek = ring(st, nc.sbuf_tensor, "at_ek", 2, [P, 2, SEQ], BF16)
        prob = ring(st, nc.sbuf_tensor, "at_prob", 2, [P, JH, 2, CH], F32)
        vst = ring(st, nc.sbuf_tensor, "at_v", 2, [P, KT, JH, VW], F32)
        osb = ring(st, nc.sbuf_tensor, "at_o", 2, [P, CH], F32)
        hmax = ring(st, nc.sbuf_tensor, "at_hmax", 2, [P, JH * KT, 2], F32)
        low = ring(st, nc.sbuf_tensor, "at_low", 2, [P, JH * KT], F32)
        rest = ring(st, nc.sbuf_tensor, "at_rest", 2, [JH * KT, P], F32)
        lparts = ring(st, nc.sbuf_tensor, "at_lparts", 2, [JH * KT, 3, P], BF16)
        ps = ring(st, nc.psum_tensor, "at_ps", 2, [P, 2, CH], F32)
        pso = ring(st, nc.psum_tensor, "at_pso", 2, [P, CH], F32)
        psh = ring(st, nc.psum_tensor, "at_psh", 2, [P, CH], F32)
        block = st.enter_context(nc.Block())

        def high_units(first, last):
            for n in range(first, last):
                yield n % JH, n // (2 * JH), n // JH % 2

        @block.sync
        def _(sp):
            def load_high(g, e):
                for s, d in ((S.q, hq[e]), (S.k, hk[e])):
                    for h in range(2):
                        sp.dma_start(d[64 * h:64 * h + QROWS, :, :],
                                     s[bass.ds(g, 1), h:JH:2, 0:QROWS, :].rearrange("g j r t -> (g r) j t")
                                     ).then_inc(high_loaded[e], 16)

            def load_group(g, e):
                for s, d in ((S.q, eq[e]), (S.k, ek[e])):
                    for h in range(2):
                        sp.dma_start(d[64 * h:64 * h + QROWS, :, :],
                                     s[bass.ds(g, 1), h:JH:2, 0:QROWS, :].rearrange("g j r t -> (g r) j t")
                                     ).then_inc(loaded[e], 16)

            def load_rows(g, e, nth):
                sp.wait_ge(low_split, nth)
                for j in range(JH):
                    sp.dma_start(S.low[bass.ds(g, 1), j, :, :].rearrange("g r (t c) -> (g t) r c", c=P),
                                 lparts[e][KT * j:KT * (j + 1), :, :]).then_inc(rows_stored, 16)
                sp.wait_ge(rows_stored, nth * JH * 16)
                for h in range(2):
                    sp.dma_start(eq[e][64 * h + QROWS:64 * h + AROWS, :, :],
                                 S.low[bass.ds(g, 1), h:JH:2, :, :].rearrange("g j r t -> (g r) j t")
                                 ).then_inc(rows_loaded[e], 16)

            def store_o(g, qc):
                for j in range(JH):
                    sp.dma_start(S.o[bass.ds(g, 1), j, :, qc * CH:(qc + 1) * CH].rearrange("g r t -> (g r) t"),
                                 osb[qc][VW * j:VW * j + HD + 1, :]).then_inc(o_stored[qc], 16)

            for qc in range(2):
                sp.sem_inc(o_stored[qc], 16)
            load_high(0, 0)
            load_high(1, 1)
            sp.wait_ge(blanked, 4)
            load_group(0, 0)
            load_rows(0, 0, 1)
            with sp.Fori(0, GROUPS // 2) as turn:
                g0 = turn * 2
                for a in range(2):
                    g = g0 + a
                    sp.wait_ge(high_kept, 2 + HIGHS * g + HIGHS)
                    load_high(g + 2, a)
                    sp.wait_ge(exped, EXPS * g + 2)
                    load_group(g + 1, 1 - a)
                    sp.wait_ge(o_kept, 2 * g + 3)
                    store_o(g, 1)
                    load_rows(g + 1, 1 - a, g + 2)
                    sp.wait_ge(o_kept, 2 * g + 4)
                    store_o(g + 1, 0)
            sp.wait_ge(o_kept, 2 * GROUPS + 3)
            store_o(GROUPS, 1)
            for qc in range(2):
                sp.wait_ge(o_stored[qc], JH * 16 * (GROUPS + qc) + 16)
            for e in range(2):
                sp.wait_ge(high_loaded[e], 64 * (GROUPS // 2 + 1))
                sp.wait_ge(loaded[e], 64 * (GROUPS // 2 + 1 - e))
                sp.wait_ge(rows_loaded[e], 32 * (GROUPS // 2 + 1 - e))

        @block.gpsimd
        def _(pool):
            for e in range(2):
                pool.memset(eq[e][:, :, :], 1.0).then_inc(blanked, 1)
                pool.memset(ek[e][:, :, :], 1.0).then_inc(blanked, 1)
            for e in range(2):
                pool.memset(vst[e][:, :, :, :], 1.0).then_inc(blanked, 1)
            pool.memset(prob[1][:, :, :, :], 0.0).then_inc(blanked, 1)

            def stage_v(g, e):
                pool.tensor_copy(vst[e][:, :, :, 0:HD],
                                 T.V[:, bass.ds(g, 1), :, :].rearrange("p g t (j e) -> p (g t) j e", e=HD)
                                 ).then_inc(v_staged, 1)

            pool.wait_ge(blanked, 7)
            stage_v(0, 0)
            with pool.Fori(0, GROUPS // 2) as turn:
                g0 = turn * 2
                for a in range(2):
                    g = g0 + a
                    pool.wait_ge(multiplied, 4 + 16 * g + 2)
                    stage_v(g + 1, 1 - a)

        @block.tensor
        def _(pe):
            used = [0]

            def high(e, unit):
                j, qt, kh = unit
                h, pair = 64 * (j % 2), j // 2
                nc.tensor.matmul(psh[used[0] % 2][:, :], hq[e][h:h + QROWS, pair, qt * P:(qt + 1) * P],
                                 hk[e][h:h + QROWS, pair, kh * CH:(kh + 1) * CH],
                                 start=True, stop=True).then_inc(high_scored, 1)
                used[0] += 1

            def turn_low(e, nth):
                pe.wait_ge(low_ready, nth)
                nc.tensor.transpose(psh[used[0] % 2][0:JH * KT, 0:P], low[e][:, :], T.ident[:, :]).then_inc(low_turned, 1)
                used[0] += 1

            def score(g, e, n):
                qc, kp, jp = n // 8, n % 8 // 2, n % 2
                for i in range(2):
                    h = 64 * i
                    pe.wait_ge(exped, EXPS * g + 2 * n + i + 1)
                    for k in range(2):
                        ins = nc.tensor.matmul(ps[i][:, k, :], ek[e][h:h + AROWS, jp, (2 * kp + k) * P:(2 * kp + k + 1) * P],
                                               eq[e][h:h + AROWS, jp, qc * CH:(qc + 1) * CH], start=True, stop=True)
                        if k == 1:
                            ins.then_inc(scored, 1)

            def multiply(e, c, k):
                qc, kt = c // 4, 2 * (c % 4) + k
                for j in range(JH):
                    ins = nc.tensor.matmul(pso[qc][VW * j:VW * (j + 1), :], vst[e][:, kt, j, :],
                                           prob[c % 2][:, j, k, :], start=(kt == 0), stop=(kt == KT - 1))
                ins.then_inc(multiplied, 1)

            pe.sem_inc(multiplied, 4)
            pe.wait_ge(blanked, 7)
            for j in range(JH):
                nc.tensor.matmul(pso[1][VW * j:VW * (j + 1), :], vst[1][:, 0, j, :], prob[1][:, j, 0, :],
                                 start=True, stop=False)
            pe.wait_ge(high_loaded[0], 64)
            for n, unit in enumerate(high_units(0, HIGHS)):
                pe.wait_ge(high_kept, n + 1)
                high(0, unit)
            pe.wait_ge(high_loaded[1], 64)
            for n, unit in enumerate(high_units(0, HALF)):
                pe.wait_ge(high_kept, HIGHS + n + 1 + (n == 4))
                if n == 5:
                    pe.wait_ge(chain, 2)
                high(1, unit)
                if n == 3:
                    pe.wait_ge(high_kept, HIGHS + n + 2)
                    turn_low(0, 1)
            start = HIGHS + HALF
            with pe.Fori(0, GROUPS // 2) as turn:
                g0 = turn * 2
                for a in range(2):
                    g, e = g0 + a, a
                    todo = [(1 - e, u) for u in high_units(HALF, HIGHS)] + [(e, u) for u in high_units(0, HALF)]
                    for n in range(STEPS):
                        if n == 0:
                            pe.wait_ge(loaded[e], g0 * 32 + 64)
                            pe.wait_ge(rows_loaded[e], g0 * 16 + 32)
                        score(g, e, n)
                        if n == STEPS // 2:
                            pe.wait_ge(high_loaded[e], g0 * 32 + 128)
                        for u in range(4):
                            m = 4 * n + u
                            pe.wait_ge(high_kept, start + HIGHS * g + m + 1 + (m == HALF + 4))
                            if m == HALF + 5:
                                pe.wait_ge(chain, 3 * g + 5)
                            high(*todo[m])
                        if n == STEPS // 2:
                            pe.wait_ge(high_kept, start + HIGHS * g + 4 * n + 4 + 1)
                            turn_low(1 - e, g + 2)
                        if n == 2:
                            pe.wait_ge(v_staged, g + 1)
                        if n in (2, 10):
                            pe.wait_ge(o_kept, 2 * g + (n == 10) + 1)
                        if n < 2:
                            multiply(1 - e, 7, n)
                        else:
                            multiply(e, (n - 2) // 2, n % 2)
            pe.wait_ge(exped, 2 + EXPS * GROUPS)
            for k in range(2):
                multiply(1, 7, k)

        @block.scalar
        def _(act):
            act.sem_inc(exped, 2)
            act.sem_inc(o_kept, 2)

            def keep(qc, before, done):
                act.wait_ge(multiplied, done)
                act.wait_ge(o_stored[qc], before + 16)
                nc.scalar.copy(osb[qc][:, :], pso[qc][:, :]).then_inc(o_kept, 1)

            act.wait_ge(blanked, 7)
            with act.Fori(0, GROUPS // 2) as turn:
                g0 = turn * 2
                for a in range(2):
                    g = g0 + a
                    for n in range(STEPS):
                        c = n // 2
                        if n % 2 == 0:
                            act.wait_ge(multiplied, 16 * g + 2 * c + 4)
                        for i in range(2):
                            act.wait_ge(scored, EXPS * g + 2 * n + i + 1)
                            nc.scalar.activation(prob[c % 2][:, 2 * (n % 2) + i, :, :], ps[i][:, :, :], ACT.Exp,
                                                 scale=HD ** -0.5).then_inc(exped, 1)
                        if n == 2:
                            keep(1, g * (JH * 16), 16 * g + 6)
                        if n == 10:
                            keep(0, g * (JH * 16), 16 * g + 14)
            keep(1, GROUPS * JH * 16, 16 * GROUPS + 6)

        @block.vector
        def _(dve):
            dve.sem_inc(high_kept, 2)
            used = [0]

            def take(e, unit, nth):
                j, qt, kh = unit
                dve.wait_ge(high_scored, nth)
                nc.vector.tensor_reduce(hmax[e][:, KT * j + qt, kh:kh + 1], psh[used[0] % 2][:, :], AX.X,
                                        ALU.max).then_inc(high_kept, 1)
                used[0] += 1

            def lowest(e, kept):
                dve.wait_ge(high_kept, kept)
                nc.vector.tensor_reduce(low[e][:, :], hmax[e][:, :, :], AX.X, ALU.max, negate=True).then_inc(low_ready, 1)

            def split_low(e, nth, links, rows):
                bank = psh[used[0] % 2][0:JH * KT, 0:P]
                dve.wait_ge(low_turned, nth)
                if rows is not None:
                    dve.wait_ge(rows_stored, rows)
                nc.vector.tensor_copy(lparts[e][:, 0, :], bank).then_inc(chain, 1)
                dve.wait_ge(chain, links + 1)
                nc.vector.tensor_tensor(rest[e][:, :], bank, lparts[e][:, 0, :], ALU.subtract).then_inc(chain, 1)
                dve.wait_ge(chain, links + 2)
                nc.vector.tensor_copy(lparts[e][:, 1, :], rest[e][:, :]).then_inc(chain, 1)
                dve.wait_ge(chain, links + 3)
                nc.vector.tensor_tensor(lparts[e][:, 2, :], rest[e][:, :], lparts[e][:, 1, :],
                                        ALU.subtract).then_inc(low_split, 1)
                used[0] += 1

            for n, unit in enumerate(high_units(0, HIGHS)):
                take(0, unit, n + 1)
            lowest(0, 2 + HIGHS)
            for n, unit in enumerate(high_units(0, HALF)):
                take(1, unit, HIGHS + n + 1)
                if n == 3:
                    split_low(0, 1, 0, None)
            start = HIGHS + HALF
            with dve.Fori(0, GROUPS // 2) as turn:
                g0 = turn * 2
                for a in range(2):
                    g, e = g0 + a, a
                    todo = [(1 - e, u) for u in high_units(HALF, HIGHS)] + [(e, u) for u in high_units(0, HALF)]
                    for m in range(HIGHS):
                        if m == HALF:
                            lowest(1 - e, 2 + start + HIGHS * g + HALF)
                        take(*todo[m], start + HIGHS * g + m + 1)
                        if m == HALF + 3:
                            split_low(1 - e, g + 2, 3 * g + 3, g * (JH * 16) + JH * 16)


def output_stage(nc, T, I, S):
    with ExitStack() as st:
        sem = lambda n: st.enter_context(nc.semaphore(f"out_{n}"))
        weights, inverted, divided, projected, added = map(
            sem, ("weights", "inverted", "divided", "projected", "added"))
        loaded = [sem("loaded0"), sem("loaded1")]
        wo = st.enter_context(nc.sbuf_tensor("out_w", [P, D], F32))
        OT = ring(st, nc.sbuf_tensor, "out_o", 2, [P, CH], F32)
        DN = ring(st, nc.sbuf_tensor, "out_dn", 2, [P, CH], F32)
        ps = ring(st, nc.psum_tensor, "out_ps", 2, [P, CH], F32)
        block = st.enter_context(nc.Block())
        so = S.o.rearrange("g j r t -> (g j) r t")

        @block.sync
        def _(sp):
            sp.dma_start(wo[:, :], I["w_out"]).then_inc(weights, 16)
            sp.wait_ge(weights, 16)
            with sp.Fori(0, BATCH) as b:
                for a in range(2):
                    sp.wait_ge(added, 2 * b + a + 1)
                    heads = so[bass.ds(b * HEADS + JH, HEADS), :, a * CH:(a + 1) * CH]
                    sp.dma_start(OT[a][:, :], heads[:, 0:HD, :]).then_inc(loaded[a], 16)
                    for r in range(HD):
                        sp.dma_start(DN[a][r:P:HD, :], heads[:, HD, :]).then_inc(loaded[a], 16)

        @block.vector
        def _(dve):
            dve.sem_inc(added, 2)
            with dve.Fori(0, BATCH) as b:
                for a in range(2):
                    c = 2 * b + a
                    dve.wait_ge(loaded[a], b * (16 * (HD + 1)) + 16 * (HD + 1))
                    nc.vector.reciprocal(DN[a][:, :], DN[a][:, :]).then_inc(inverted, 1)
                    dve.wait_ge(inverted, c + 1)
                    nc.vector.tensor_tensor(OT[a][:, :], OT[a][:, :], DN[a][:, :], ALU.mult).then_inc(divided, 1)
                    dve.wait_ge(projected, c + 1)
                    xs = T.X[:, bass.ds(c * CT, CT), :]
                    nc.vector.tensor_tensor(xs, ps[a][:, :].rearrange("p (t d) -> p t d", d=D), xs, ALU.add).then_inc(added, 1)

        @block.tensor
        def _(pe):
            pe.wait_ge(weights, 16)
            with pe.Fori(0, BATCH) as b:
                for a in range(2):
                    c = 2 * b + a
                    pe.wait_ge(divided, c + 1)
                    for k in range(CT):
                        ins = nc.tensor.matmul(ps[a][:, k * D:(k + 1) * D], OT[a][:, k * P:(k + 1) * P], wo[:, :],
                                               start=(k == 0), stop=(k == CT - 1), skip_group_check=True)
                    ins.then_inc(projected, 1)


def gate_stage(nc, T, I, S):
    N, E = TILES, EXPERTS
    with ExitStack() as st:
        gate_no[0] += 1
        tag = f"gate{gate_no[0]}"
        sem = lambda n: st.enter_context(nc.semaphore(f"{tag}_{n}"))
        logged, copied, turned, unturned, shifted, exped, masked, placed, weighed, chain, wdone, stored = map(
            sem, ("logged", "copied", "turned", "unturned", "shifted", "exped", "masked", "placed", "weighed",
                  "chain", "wdone", "stored"))
        sb = lambda n, shape: st.enter_context(nc.sbuf_tensor(f"{tag}_{n}", shape, F32))
        LG = sb("lg", [E, TOKENS])
        L, G, K2, EQ, W = (sb(n, [P, N, E]) for n in ("l", "g", "k2", "eq", "w"))
        M = sb("m", [P, N, 2, E])
        KEEP = sb("keep", [P, N, 2, E])
        A, B, POS = (sb(n, [P, N, 2, E]) for n in ("a", "b", "pos"))
        top, tot, den = sb("top", [P, N]), sb("tot", [P, N]), sb("den", [P, N])
        cnt = sb("cnt", [P, E])
        psl = ring(st, nc.psum_tensor, f"{tag}_psl", 4, [P, CH], F32)
        pst, psa, psb = (st.enter_context(nc.psum_tensor(f"{tag}_{n}", [P, CH], F32)) for n in ("pst", "psa", "psb"))
        block = st.enter_context(nc.Block())

        @block.tensor
        def _(pe):
            for c in range(CHUNKS):
                if c >= 4:
                    pe.wait_ge(copied, c - 3)
                nc.tensor.matmul(psl[c % 4][0:E, :], T.rw[:, :], T.XT[:, c * CH:(c + 1) * CH],
                                 start=True, stop=True).then_inc(logged, 1)
            pe.wait_ge(copied, CHUNKS)
            for t in range(N):
                ins = nc.tensor.transpose(pst[:, t * E:(t + 1) * E], LG[:, t * P:(t + 1) * P], T.ident[0:E, 0:E])
            ins.then_inc(turned, 1)
            pe.wait_ge(masked, 1)
            m = M[:, :, :, :].rearrange("p t k e -> p (t k e)")
            nc.tensor.matmul(psa[:, :], T.upper[:, :], m, start=True, stop=True)
            nc.tensor.matmul(psb[:, :], T.ones[:, :], m, start=True, stop=True).then_inc(placed, 1)
            pe.wait_ge(weighed, 1)
            for c in range(CHUNKS):
                if c >= 4:
                    pe.wait_ge(wdone, c - 3)
                for k in range(CT):
                    ins = nc.tensor.transpose(psl[c % 4][0:E, k * P:(k + 1) * P], W[:, c * CT + k, :], T.ident[:, :])
                ins.then_inc(unturned, 1)

        @block.scalar
        def _(act):
            for c in range(CHUNKS):
                act.wait_ge(logged, c + 1)
                nc.scalar.copy(LG[:, c * CH:(c + 1) * CH], psl[c % 4][0:E, :]).then_inc(copied, 1)
            act.wait_ge(shifted, 1)
            nc.scalar.activation(G[:, :, :], L[:, :, :], ACT.Exp).then_inc(exped, 1)
            for c in range(CHUNKS):
                act.wait_ge(unturned, c + 1)
                nc.scalar.copy(T.WT[:, c * CH:(c + 1) * CH], psl[c % 4][0:E, :]).then_inc(wdone, 1)
            act.wait_ge(wdone, CHUNKS)
            act.dma_start(S.wt, T.WT[:, :]).then_inc(stored, 16)
            act.wait_ge(stored, 16)

        @block.vector
        def _(dve):
            link = Count(dve, chain)
            wide = lambda a: a.unsqueeze(2).to_broadcast([P, N, E])
            rank = T.rank[:, :].unsqueeze(1).to_broadcast([P, N, E])

            def step(ins):
                link.mark(ins)
                link.settle()

            def first_best(out, key, best):
                step(nc.vector.tensor_tensor(EQ[:, :, :], key, wide(best), ALU.is_equal))
                step(nc.vector.tensor_tensor(EQ[:, :, :], EQ[:, :, :], rank, ALU.mult))
                step(nc.vector.tensor_reduce(top[:, :], EQ[:, :, :], AX.X, ALU.max))
                step(nc.vector.tensor_tensor(out, EQ[:, :, :], wide(top[:, :]), ALU.is_equal))

            dve.wait_ge(turned, 1)
            lg = pst[:, 0:N * E].rearrange("p (t e) -> p t e", e=E)
            step(nc.vector.tensor_reduce(top[:, :], lg, AX.X, ALU.max))
            nc.vector.tensor_tensor(L[:, :, :], lg, wide(top[:, :]), ALU.subtract).then_inc(shifted, 1)
            dve.wait_ge(shifted, 1)
            step(nc.vector.memset(den[:, :], 0.0))
            first_best(M[:, :, 0, :], L[:, :, :], den[:, :])
            step(nc.vector.tensor_scalar(K2[:, :, :], L[:, :, :], FLOOR, None, ALU.max))
            step(nc.vector.tensor_scalar(EQ[:, :, :], M[:, :, 0, :], FLOOR, None, ALU.mult))
            step(nc.vector.tensor_tensor(K2[:, :, :], K2[:, :, :], EQ[:, :, :], ALU.add))
            step(nc.vector.tensor_reduce(den[:, :], K2[:, :, :], AX.X, ALU.max))
            first_best(M[:, :, 1, :], K2[:, :, :], den[:, :])
            nc.vector.tensor_copy(EQ[:, :, :], M[:, :, 1, :]).then_inc(masked, 1)
            dve.wait_ge(exped, 1)
            step(nc.vector.tensor_reduce(tot[:, :], G[:, :, :], AX.X, ALU.add))
            step(nc.vector.reciprocal(tot[:, :], tot[:, :]))
            step(nc.vector.tensor_tensor(G[:, :, :], G[:, :, :], wide(tot[:, :]), ALU.mult))
            dve.wait_ge(placed, 1)
            a3 = lambda x: x[:, :, :, :].rearrange("p t k e -> p t (k e)")
            pb = psb[:, :].rearrange("p (t q) -> p t q", q=2 * E)
            step(nc.vector.tensor_copy(a3(A), pb))
            src, dst, s = A, B, 1
            while s < N:
                step(nc.vector.tensor_tensor(a3(dst)[:, s:N, :], a3(src)[:, s:N, :], a3(src)[:, 0:N - s, :], ALU.add))
                step(nc.vector.tensor_copy(a3(dst)[:, 0:s, :], a3(src)[:, 0:s, :]))
                src, dst, s = dst, src, 2 * s
            step(nc.vector.tensor_scalar(cnt[:, :], src[:, N - 1, 0, :], float(CAP), None, ALU.min))
            step(nc.vector.tensor_tensor(a3(POS), a3(src), pb, ALU.subtract))
            step(nc.vector.tensor_tensor(a3(POS), psa[:, :].rearrange("p (t q) -> p t q", q=2 * E), a3(POS), ALU.add))
            step(nc.vector.tensor_tensor(POS[:, :, 1, :], POS[:, :, 1, :],
                                         cnt[:, :].unsqueeze(1).to_broadcast([P, N, E]), ALU.add))
            step(nc.vector.tensor_scalar(a3(KEEP), a3(POS), float(CAP), None, ALU.is_lt))
            step(nc.vector.tensor_tensor(a3(KEEP), a3(KEEP), a3(M), ALU.mult))
            step(nc.vector.tensor_tensor(EQ[:, :, :], KEEP[:, :, 0, :], KEEP[:, :, 1, :], ALU.add))
            step(nc.vector.tensor_tensor(G[:, :, :], G[:, :, :], EQ[:, :, :], ALU.mult))
            step(nc.vector.tensor_reduce(tot[:, :], G[:, :, :], AX.X, ALU.add))
            step(nc.vector.tensor_scalar(tot[:, :], tot[:, :], GATE_EPS, None, ALU.max))
            step(nc.vector.reciprocal(tot[:, :], tot[:, :]))
            nc.vector.tensor_tensor(W[:, :, :], G[:, :, :], wide(tot[:, :]), ALU.mult).then_inc(weighed, 1)


gate_no = [0]


def experts_stage(nc, T, S, tag):
    NE = EXPERTS + 1
    NS = EXPERTS - 1
    with ExitStack() as st:
        sem = lambda n: st.enter_context(nc.semaphore(f"{tag}_{n}"))
        first, silued, second, scaled, summed, finished = map(
            sem, ("first", "silued", "second", "scaled", "summed", "finished"))
        wloaded = [sem("wloaded0"), sem("wloaded1")]
        WB = ring(st, nc.sbuf_tensor, f"{tag}_wb", 2, [P, EXPERTS, CH], F32)
        hid = ring(st, nc.sbuf_tensor, f"{tag}_hid", 2, [P, FT, CH], F32)
        tmp = ring(st, nc.sbuf_tensor, f"{tag}_tmp", 2, [P, CH], F32)
        acc = ring(st, nc.sbuf_tensor, f"{tag}_acc", 2, [P, CH], F32)
        ps1 = ring(st, nc.psum_tensor, f"{tag}_ps1", 4, [P, CH], F32)
        ps2 = ring(st, nc.psum_tensor, f"{tag}_ps2", 2, [P, CH], F32)
        block = st.enter_context(nc.Block())

        @block.sync
        def _(sp):
            with sp.Fori(0, CHUNKS // 2) as i:
                for a in range(2):
                    sp.wait_ge(scaled, NE * (2 * i + a) + NE)
                    sp.dma_start(WB[a][:, :, :], S.wt[:, bass.ds(i * (2 * CH) + a * CH, CH)].partition_broadcast(P)
                                 ).then_inc(wloaded[a], 16)

        @block.tensor
        def _(pe):
            def up(c, e, cols):
                for f in range(FT):
                    pe.wait_ge(silued, (c * NE + e) * FT + f + 1)
                    w = T.w1[:, e, f * P:(f + 1) * P] if e < EXPERTS else T.sw1[:, f * P:(f + 1) * P]
                    nc.tensor.matmul(ps1[f][:, :], w, T.XT[:, cols], start=True, stop=True).then_inc(first, 1)

            def down(c, a, e):
                k = (a * NE + e) % 2
                pe.wait_ge(scaled, c * NE + e + 2 * NE - 1)
                for f in range(FT):
                    pe.wait_ge(silued, (c * NE + e) * FT + f + 1 + FT)
                    w = T.w2[:, e, f, :] if e < EXPERTS else T.sw2[:, f, :]
                    ins = nc.tensor.matmul(ps2[k][:, :], w, hid[k][:, f, :], start=(f == 0), stop=(f == FT - 1))
                ins.then_inc(second, 1)

            with pe.Fori(0, CHUNKS // 2) as i:
                for a in range(2):
                    c = 2 * i + a
                    cols = bass.ds(i * (2 * CH) + a * CH, CH)
                    up(c, 0, cols)
                    for e in range(1, NE):
                        up(c, e, cols)
                        down(c, a, e - 1)
                    down(c, a, NE - 1)

        @block.scalar
        def _(act):
            act.sem_inc(silued, FT)
            act.sem_inc(second, 2)
            with act.Fori(0, CHUNKS // 2) as i:
                for a in range(2):
                    c = 2 * i + a
                    for e in range(NE):
                        k = (a * NE + e) % 2
                        act.wait_ge(second, c * NE + e + 1)
                        for f in range(FT):
                            act.wait_ge(first, (c * NE + e) * FT + f + 1)
                            nc.scalar.activation(hid[k][:, f, :], ps1[f][:, :], ACT.Silu,
                                                 bias=T.b1[:, e * FT + f:e * FT + f + 1]).then_inc(silued, 1)

        @block.vector
        def _(dve):
            dve.sem_inc(scaled, 2 * NE)
            dve.sem_inc(finished, 1)
            with dve.Fori(0, CHUNKS // 2) as i:
                for a in range(2):
                    c = 2 * i + a
                    dve.wait_ge(wloaded[a], 16 * i + 16)
                    for e in range(NE):
                        k = (a * NE + e) % 2
                        dve.wait_ge(second, c * NE + e + 3)
                        if e >= 2:
                            dve.wait_ge(summed, c * NS + max(e - 2, 1) + 2)
                        elif e == 0:
                            dve.wait_ge(finished, c + 1)
                        if e < EXPERTS:
                            nc.vector.scalar_tensor_tensor(out=tmp[k][:, :], in0=ps2[k][:, :], scalar=T.b2[:, e:e + 1],
                                                           in1=WB[a][:, e, :], op0=ALU.add, op1=ALU.mult).then_inc(scaled, 1)
                        else:
                            nc.vector.tensor_scalar(tmp[k][:, :], ps2[k][:, :], T.b2[:, e:e + 1], SHARED,
                                                    ALU.add, ALU.mult).then_inc(scaled, 1)
                    dve.wait_ge(scaled, (c + 1) * NE + 2 * NE)
                    dve.wait_ge(summed, c * NS + NS + 2)
                    nc.vector.tensor_tensor(T.ACC[:, bass.ds(i * (2 * CH) + a * CH, CH)], acc[a][:, :], tmp[k][:, :],
                                            ALU.add).then_inc(finished, 1)

        @block.gpsimd
        def _(pool):
            pool.sem_inc(summed, 2)
            with pool.Fori(0, CHUNKS // 2) as i:
                for a in range(2):
                    c = 2 * i + a
                    for e in range(1, EXPERTS):
                        k = (a * NE + e) % 2
                        pool.wait_ge(scaled, c * NE + e + 1 + 2 * NE)
                        if e > 1:
                            pool.wait_ge(summed, c * NS + e + 1)
                        pool.tensor_tensor(acc[a][:, :], tmp[1 - k][:, :] if e == 1 else acc[a][:, :], tmp[k][:, :],
                                           ALU.add).then_inc(summed, 1)


def add_back_stage(nc, T, tag):
    with ExitStack() as st:
        sem = lambda n: st.enter_context(nc.semaphore(f"{tag}_{n}"))
        fetched, turned, added = map(sem, ("fetched", "turned", "added"))
        buf = ring(st, nc.sbuf_tensor, f"{tag}_buf", 2, [P, CH], F32)
        ps = ring(st, nc.psum_tensor, f"{tag}_ps", 2, [P, CH], F32)
        block = st.enter_context(nc.Block())

        @block.scalar
        def _(act):
            act.sem_inc(turned, 2)
            with act.Fori(0, CHUNKS // 2) as i:
                for a in range(2):
                    act.wait_ge(turned, 2 * i + a + 1)
                    nc.scalar.copy(buf[a][:, :], T.ACC[:, bass.ds(i * (2 * CH) + a * CH, CH)]).then_inc(fetched, 1)

        @block.tensor
        def _(pe):
            with pe.Fori(0, CHUNKS // 2) as i:
                for a in range(2):
                    pe.wait_ge(fetched, 2 * i + a + 1)
                    pe.wait_ge(added, 2 * i + a + 1)
                    for k in range(CT):
                        ins = nc.tensor.transpose(ps[a][:, k * P:(k + 1) * P], buf[a][:, k * P:(k + 1) * P], T.ident[:, :])
                    ins.then_inc(turned, 1)

        @block.vector
        def _(dve):
            dve.sem_inc(added, 2)
            with dve.Fori(0, CHUNKS // 2) as i:
                for a in range(2):
                    dve.wait_ge(turned, 2 * i + a + 3)
                    xs = T.X[:, bass.ds(i * (2 * CT) + a * CT, CT), :]
                    nc.vector.tensor_tensor(xs, ps[a][:, :].rearrange("p (t d) -> p t d", d=D), xs, ALU.add).then_inc(added, 1)


def retention_stage(nc, T, I):
    NT = SEQ // RL
    HT = NT // 2
    TURNS = 4 + 3 * NT + 2
    with ExitStack() as st:
        sem = lambda n: st.enter_context(nc.semaphore(f"rt_{n}"))
        (x_ready, turned, t_kept, projected, q_read, v_kept, decayed_qk, scored, masked, y_done, y_read,
         outered, m_free, wide, wide_kept, var_ready, rooted, yn_ready, gated, x_plus, chain, blank) = map(sem, (
             "x_ready", "turned", "t_kept", "projected", "q_read", "v_kept", "decayed_qk", "scored", "masked",
             "y_done", "y_read", "outered", "m_free", "wide", "wide_kept", "var_ready", "rooted", "yn_ready",
             "gated", "x_plus", "chain", "blank"))
        rotated = sem("rotated")
        loaded = sem("loaded")
        sb = lambda n, shape: st.enter_context(nc.sbuf_tensor(f"rt_{n}", shape, F32))
        wqkv, wff1, wg, wp, wff2 = sb("wqkv", [P, 3 * D]), sb("wff1", [P, 2, D]), sb("wg", [P, D]), sb("wp", [P, D]), sb("wff2", [P, 2, D])
        cols, bp = sb("cols", [P, 5]), sb("bp", [P, D])
        cosn, sinn = sb("cos", [P, NT, 2, D]), sb("sin", [P, NT, 2, D])
        mask = sb("mask", [P, 4, 4, RL])
        qg, kg, diag = sb("qg", [P, D]), sb("kg", [P, D]), sb("diag", [P, D])
        XH, XR = sb("xh", [P, NT, D]), sb("xr", [P, NT, D])
        XHT, XRT = sb("xht", [P, SEQ]), sb("xrt", [P, SEQ])
        GATE, GT = sb("gate", [P, SEQ]), sb("gt", [P, 2, SEQ])
        T1, T2 = sb("t1", [P, 2, D]), sb("t2", [P, 2, D])
        PAD = ring(st, nc.sbuf_tensor, "rt_pad", 2, [P, 2, HEADS, 32], F32)
        QD, KD, VS = (ring(st, nc.sbuf_tensor, f"rt_{n}", 2, [P, D], F32) for n in ("qd", "kd", "vs"))
        QT, KTr = (ring(st, nc.sbuf_tensor, f"rt_{n}", 2, [P, 4, RL], F32) for n in ("qt", "kt"))
        QDT = ring(st, nc.sbuf_tensor, "rt_qdt", 2, [P, RL], F32)
        SM = ring(st, nc.sbuf_tensor, "rt_sm", 2, [P, 4, 4, RL], F32)
        STATE, UM = sb("state", [P, D]), sb("um", [P, D])
        YC, YN = sb("yc", [P, HT * HEADS, HD]), sb("yn", [P, HT * HEADS, HD])
        YT, GY = sb("yt", [P, CH]), sb("gy", [P, CH])
        mu, var = sb("mu", [P, HT * HEADS]), sb("var", [P, HT * HEADS])
        pt = ring(st, nc.psum_tensor, "rt_pt", 2, [P, CH], F32)
        pss = ring(st, nc.psum_tensor, "rt_ps", 2, [P, CH], F32)
        pq, py, pw, pm = (st.enter_context(nc.psum_tensor(f"rt_{n}", [P, CH], F32)) for n in ("pq", "py", "pw", "pm"))
        block = st.enter_context(nc.Block())
        LOADS = 13

        def kept_after_tile(k):
            return 4 + 3 * (k + 1) + (1 if k >= 7 else 0)

        @block.sync
        def _(sp):
            for d, s in ((wqkv[:, :], I["r_wqkv"]), (wff1[:, :, :], I["r_wff1"]), (wg[:, :], I["r_wg"]), (wp[:, :], I["r_wp"]),
                         (wff2[:, :, :], I["r_wff2"]), (cols[:, :], I["r_cols"]), (bp[:, :], I["r_bp"].partition_broadcast(P)),
                         (cosn[:, :, :, :], I["r_cos"]), (sinn[:, :, :, :], I["r_sin"]), (mask[:, :, :, :], I["r_mask"]),
                         (qg[:, :], I["r_qg"]), (kg[:, :], I["r_kg"]), (diag[:, :], I["r_diag"])):
                sp.dma_start(d, s).then_inc(loaded, 16)
            sp.wait_ge(loaded, 16 * LOADS)

        @block.tensor
        def _(pe):
            pe.wait_ge(loaded, 16 * LOADS)
            with pe.Fori(0, BATCH) as b:
                uses = [0]

                def turn_into(rows, src):
                    n = uses[0]
                    pe.wait_ge(t_kept, b * TURNS + n + 1)
                    for k, piece in enumerate(src):
                        ins = nc.tensor.transpose(pt[n % 2][0:rows, k * P:(k + 1) * P], piece, T.ident[:, :])
                    ins.then_inc(turned, 1)
                    uses[0] += 1

                def project(k):
                    pe.wait_ge(q_read, b * NT + k + 1)
                    pe.wait_ge(v_kept, b * NT + k + 1)
                    pe.wait_ge(t_kept, b * TURNS + 2 + (2 if k < HT else 4))
                    nc.tensor.matmul(pq[:, 0:3 * D], XRT[:, k * RL:(k + 1) * RL], wqkv[:, :],
                                     start=True, stop=True).then_inc(projected, 1)

                def turn_qk(k):
                    pe.wait_ge(rotated, b * NT + k + 1)
                    for w in range(2):
                        turn_into(P, [PAD[k % 2][:, w, 4 * i:4 * i + 4, :].rearrange("p h d -> p (h d)") for i in range(4)])
                    pe.wait_ge(decayed_qk, b * NT + k + 1)
                    turn_into(P, [QD[k % 2][:, :]])

                def score(k):
                    for j in range(4):
                        pe.wait_ge(masked, (b * NT + k) * 4 + j + 1)
                        if j == 0:
                            pe.wait_ge(t_kept, b * TURNS + 2 + kept_after_tile(k))
                        for i in range(4):
                            ins = nc.tensor.matmul(pss[j % 2][:, i * RL:(i + 1) * RL], KTr[k % 2][32 * j:32 * j + HD, i, :],
                                                   QT[k % 2][32 * j:32 * j + HD, i, :], start=True, stop=True)
                        ins.then_inc(scored, 1)

                def values(k):
                    o = k % HT * D
                    if k == 0:
                        pe.wait_ge(y_read, b * 2 + 1)
                    if k == HT:
                        pe.wait_ge(y_read, b * 2 + 2)
                    pe.wait_ge(v_kept, b * NT + k + 2)
                    if k:
                        pe.wait_ge(m_free, b * (NT + 1) + k + 1)
                        nc.tensor.matmul(py[:, o:o + D], QDT[k % 2][:, :], STATE[:, :], start=True, stop=False,
                                         skip_group_check=True)
                    for j in range(4):
                        pe.wait_ge(masked, (b * NT + k) * 4 + j + 3)
                        for i in range(4):
                            h = 4 * i + j
                            ins = nc.tensor.matmul(py[:, o + h * HD:o + (h + 1) * HD], SM[k % 2][:, j, i, :],
                                                   VS[k % 2][:, h * HD:(h + 1) * HD], start=(k == 0 and j == 0 and i == 0),
                                                   stop=(j == 3 and i == 3), skip_group_check=True)
                    ins.then_inc(y_done, 1)

                def outer(k):
                    pe.wait_ge(m_free, b * (NT + 1) + k + 1)
                    pe.wait_ge(decayed_qk, b * NT + k + 1)
                    nc.tensor.matmul(pm[:, 0:D], KD[k % 2][:, :], VS[k % 2][:, :], start=True, stop=True).then_inc(outered, 1)

                def widen(n):
                    pe.wait_ge(wide_kept, b * 6 + n + 1)
                    w, x = (wg[:, :], XHT) if n < 2 else (wff1[:, (n - 2) // 2, :], XRT)
                    pe.wait_ge(t_kept, b * TURNS + 6)
                    nc.tensor.matmul(pw[:, :], w, x[:, n % 2 * CH:(n % 2 + 1) * CH], start=True, stop=True).then_inc(wide, 1)

                def finish(half):
                    pe.wait_ge(gated, b * 2 + half + 1)
                    pe.wait_ge(wide_kept, b * 6 + 7)
                    pe.wait_ge(m_free, b * (NT + 1) + NT + half)
                    for k in range(HT):
                        out = pm[:, k * D:(k + 1) * D]
                        for f in range(2):
                            nc.tensor.matmul(out, GT[:, f, half * CH + k * P:half * CH + (k + 1) * P], wff2[:, f, :],
                                             start=(k == 0 and f == 0), stop=False, skip_group_check=True)
                        ins = nc.tensor.matmul(out, GY[:, k * P:(k + 1) * P], wp[:, :], start=False, stop=(k == HT - 1),
                                               skip_group_check=True)
                    ins.then_inc(outered, 1)

                def turn_y(half):
                    pe.wait_ge(yn_ready, b * 2 + half + 1)
                    turn_into(P, [YN[:, k * HEADS:(k + 1) * HEADS, :].rearrange("p h d -> p (h d)") for k in range(HT)])

                for n in range(4):
                    pe.wait_ge(x_ready, b * 4 + n + 1)
                    src = (XH, XR)[n % 2]
                    turn_into(P, [src[:, n // 2 * HT + k, :] for k in range(HT)])
                project(0)
                turn_qk(0)
                for k in range(NT):
                    if k < 6:
                        widen(k)
                    if k + 1 < NT:
                        project(k + 1)
                    score(k)
                    if k + 1 < NT:
                        turn_qk(k + 1)
                    values(k)
                    if k + 1 < NT:
                        outer(k)
                    if k == 5:
                        turn_y(0)
                    if k == 6:
                        finish(0)
                turn_y(1)
                finish(1)
                assert uses[0] == TURNS

        @block.scalar
        def _(act):
            act.sem_inc(t_kept, 2)
            act.sem_inc(v_kept, 1)
            act.sem_inc(wide_kept, 1)
            act.wait_ge(loaded, 16 * LOADS)
            with act.Fori(0, BATCH) as b:
                uses = [0]

                def keep(out, cols=CH, **how):
                    n = uses[0]
                    act.wait_ge(turned, b * TURNS + n + 1)
                    nc.scalar.activation(out, pt[n % 2][:, 0:cols], ACT.Identity, **how).then_inc(t_kept, 1)
                    uses[0] += 1

                def keep_v(k):
                    act.wait_ge(q_read, b * NT + k + 2)
                    nc.scalar.copy(VS[k % 2][:, :], pq[:, 2 * D:3 * D]).then_inc(v_kept, 1)

                def keep_qk(k):
                    for buf in (QT, KTr):
                        keep(buf[k % 2][:, :, :].rearrange("p i t -> p (i t)"))
                    keep(QDT[k % 2][:, :], RL)

                def keep_wide(n):
                    act.wait_ge(wide, b * 6 + n + 1)
                    if n < 2:
                        nc.scalar.activation(GATE[:, n * CH:(n + 1) * CH], pw[:, :], ACT.Silu, bias=cols[:, 3:4]).then_inc(wide_kept, 1)
                    else:
                        nc.scalar.activation(GT[:, (n - 2) // 2, n % 2 * CH:(n % 2 + 1) * CH], pw[:, :], ACT.Gelu).then_inc(wide_kept, 1)

                def root(half):
                    act.wait_ge(var_ready, b * 2 + half + 1)
                    nc.scalar.activation(var[:, :], var[:, :], ACT.Sqrt).then_inc(rooted, 1)

                def keep_y():
                    keep(YT[:, :], scale=cols[:, 1:2], bias=cols[:, 2:3])

                for n in range(4):
                    half = slice(n // 2 * CH, (n // 2 + 1) * CH)
                    if n % 2:
                        keep(XRT[:, half], scale=cols[:, 0:1])
                    else:
                        keep(XHT[:, half])
                keep_v(0)
                keep_qk(0)
                for k in range(NT):
                    if k < 6:
                        keep_wide(k)
                    if k + 1 < NT:
                        keep_v(k + 1)
                        keep_qk(k + 1)
                    if k == HT:
                        root(0)
                    if k == 5:
                        keep_y()
                root(1)
                keep_y()

        @block.vector
        def _(dve):
            dve.sem_inc(q_read, 1)
            dve.sem_inc(masked, 2)
            dve.sem_inc(y_read, 1)
            dve.sem_inc(m_free, 1)
            dve.wait_ge(loaded, 16 * LOADS)
            dve.wait_ge(blank, 3)
            with dve.Fori(0, BATCH) as b:
                CHAIN = NT * 2 + (NT - 2) + 2 * 6
                link = Count(dve, chain, b, CHAIN)

                def step(ins):
                    link.mark(ins)
                    link.settle()

                def normalise(n):
                    half, dst, inv = n // 2, (XH, XR)[n % 2], (T.rs, T.ri)[n % 2]
                    for k in range(half * HT, (half + 1) * HT):
                        t = b * NT + k
                        ins = nc.vector.tensor_scalar(dst[:, k, :], T.X[:, bass.ds(t, 1), :].rearrange("p t d -> p (t d)"),
                                                      T.mv[:, bass.ds(t, 1), 0:1].rearrange("p t s -> p (t s)"),
                                                      inv[:, bass.ds(t, 1)], ALU.subtract, ALU.mult)
                    ins.then_inc(x_ready, 1)

                def rotate(k):
                    dve.wait_ge(projected, b * NT + k + 1)
                    if k >= 2:
                        dve.wait_ge(decayed_qk, b * NT + k - 1)
                    qk = pq[:, 0:2 * D].rearrange("p (w d) -> p w d", w=2)
                    link.mark(nc.vector.tensor_tensor(T1[:, :, :], qk, cosn[:, k, :, :], ALU.mult))
                    link.mark(nc.vector.tensor_tensor(T2[:, :, 0:D:2], qk[:, :, 1:D:2], sinn[:, k, :, 0:D:2], ALU.mult))
                    nc.vector.tensor_tensor(T2[:, :, 1:D:2], qk[:, :, 0:D:2], sinn[:, k, :, 1:D:2], ALU.mult).then_inc(q_read, 1)
                    link.settle()
                    dve.wait_ge(q_read, b * NT + k + 2)
                    v = lambda a: a[:, :, :].rearrange("p w (h d) -> p w h d", d=HD)
                    nc.vector.tensor_tensor(PAD[k % 2][:, :, :, 0:HD], v(T1), v(T2), ALU.add).then_inc(rotated, 1)
                    dve.wait_ge(rotated, b * NT + k + 1)

                def decay_scores(k):
                    for j in range(4):
                        dve.wait_ge(scored, (b * NT + k) * 4 + j + 1)
                        nc.vector.tensor_tensor(SM[k % 2][:, j, :, :], pss[j % 2][:, :].rearrange("p (i t) -> p i t", t=RL),
                                                mask[:, j, :, :], ALU.mult).then_inc(masked, 1)

                def carry(k):
                    dve.wait_ge(outered, b * (NT + 1) + k + 1)
                    if k == 0:
                        nc.vector.tensor_tensor(STATE[:, :], pm[:, 0:D], diag[:, :], ALU.mult).then_inc(m_free, 1)
                        return
                    step(nc.vector.tensor_tensor(UM[:, :], pm[:, 0:D], diag[:, :], ALU.mult))
                    dve.wait_ge(m_free, b * (NT + 1) + k + 1)
                    nc.vector.scalar_tensor_tensor(out=STATE[:, :], in0=STATE[:, :], scalar=cols[:, 4:5], in1=UM[:, :],
                                                   op0=ALU.mult, op1=ALU.add).then_inc(m_free, 1)

                def group_norm_a(half):
                    dve.wait_ge(y_done, b * NT + (half + 1) * HT)
                    y = py[:, :].rearrange("p (h d) -> p h d", d=HD)
                    step(nc.vector.tensor_reduce(mu[:, :], y, AX.X, ALU.add))
                    step(nc.vector.tensor_scalar(mu[:, :], mu[:, :], 1.0 / HD, None, ALU.mult))
                    nc.vector.tensor_tensor(YC[:, :, :], y, mu[:, :].unsqueeze(2).to_broadcast([P, HT * HEADS, HD]),
                                            ALU.subtract).then_inc(y_read, 1)
                    dve.wait_ge(y_read, b * 2 + half + 2)
                    step(nc.vector.tensor_tensor(YN[:, :, :], YC[:, :, :], YC[:, :, :], ALU.mult))
                    step(nc.vector.tensor_reduce(var[:, :], YN[:, :, :], AX.X, ALU.add))
                    nc.vector.tensor_scalar(var[:, :], var[:, :], 1.0 / HD, GN_EPS, ALU.mult, ALU.add).then_inc(var_ready, 1)

                def group_norm_b(half):
                    dve.wait_ge(rooted, b * 2 + half + 1)
                    step(nc.vector.reciprocal(mu[:, :], var[:, :]))
                    nc.vector.tensor_tensor(YN[:, :, :], YC[:, :, :], mu[:, :].unsqueeze(2).to_broadcast([P, HT * HEADS, HD]),
                                            ALU.mult).then_inc(yn_ready, 1)

                def add(half):
                    dve.wait_ge(x_plus, b * 2 + half + 1)
                    xs = T.X[:, bass.ds(b * NT + half * HT, HT), :]
                    step(nc.vector.tensor_tensor(xs, xs, XH[:, half * HT:(half + 1) * HT, :], ALU.add))
                    dve.wait_ge(outered, b * (NT + 1) + NT + half)
                    nc.vector.tensor_tensor(xs, pm[:, :].rearrange("p (t d) -> p t d", d=D), xs, ALU.add).then_inc(m_free, 1)

                for n in range(4):
                    normalise(n)
                rotate(0)
                for k in range(NT):
                    if k + 1 < NT:
                        rotate(k + 1)
                    decay_scores(k)
                    if k == HT:
                        group_norm_a(0)
                    if k + 1 < NT:
                        carry(k)
                    if k == HT:
                        group_norm_b(0)
                    if k == NT - 1:
                        add(0)
                group_norm_a(1)
                group_norm_b(1)
                add(1)
                assert link.n == CHAIN

        @block.gpsimd
        def _(pool):
            for e in range(2):
                pool.memset(PAD[e][:, :, :, :], 0.0).then_inc(blank, 1)
            pool.memset(STATE[:, :], 0.0).then_inc(blank, 1)
            pool.wait_ge(loaded, 16 * LOADS)
            with pool.Fori(0, BATCH) as b:
                def decay_qk(k):
                    pool.wait_ge(rotated, b * NT + k + 1)
                    h = lambda a: a[:, :].rearrange("p (h d) -> p h d", d=HD)
                    pool.tensor_tensor(h(KD[k % 2]), PAD[k % 2][:, 1, :, 0:HD], h(kg), ALU.mult)
                    pool.tensor_tensor(h(QD[k % 2]), PAD[k % 2][:, 0, :, 0:HD], h(qg), ALU.mult).then_inc(decayed_qk, 1)

                def plus(half):
                    pool.wait_ge(turned, b * TURNS + 2 * half + 1)
                    xs = XH[:, half * HT:(half + 1) * HT, :]
                    pool.tensor_tensor(xs, xs, bp[:, :].unsqueeze(1).to_broadcast([P, HT, D]), ALU.add).then_inc(x_plus, 1)

                def gate(half):
                    pool.wait_ge(t_kept, b * TURNS + 2 + (4 + 3 * 7 + 1 if half == 0 else TURNS))
                    pool.wait_ge(wide_kept, b * 6 + 2 + half + 0)
                    pool.tensor_tensor(GY[:, :], YT[:, :], GATE[:, half * CH:(half + 1) * CH], ALU.mult).then_inc(gated, 1)

                decay_qk(0)
                for k in range(NT):
                    if k + 1 < NT:
                        decay_qk(k + 1)
                    if k in (1, 2):
                        plus(k - 1)
                    if k == 5:
                        gate(0)
                gate(1)


def block_kernel(nc, I, out, upto=99):
    T, S = Buffers(), Buffers()
    with ExitStack() as st:
        sb = lambda n, shape, dt=F32: st.enter_context(nc.sbuf_tensor(n, shape, dt))
        T.X, T.XT = sb("X", [P, TILES, D]), sb("XT", [P, TOKENS])
        T.V = sb("V", [P, GROUPS + 1, KT, JH * HD])
        T.ACC = T.V[:, 0:GROUPS, :, :].rearrange("p g t e -> p (g t e)")
        T.ident, T.ones, T.upper, T.bo = (sb(n, [P, P]) for n in ("ident", "ones", "upper", "bo"))
        T.rank = sb("rank", [P, EXPERTS])
        T.mv, T.sd, T.rs, T.ri = sb("mv", [P, TILES, 2]), sb("sd", [P, TILES]), sb("rs", [P, TILES]), sb("ri", [P, TILES])
        T.w1, T.w2 = sb("w1", [P, EXPERTS, FF]), sb("w2", [P, EXPERTS, FT, D])
        T.sw1, T.sw2, T.rw = sb("sw1", [P, FF]), sb("sw2", [P, FT, D]), sb("rw", [P, EXPERTS])
        T.b1, T.b2 = sb("b1", [P, (EXPERTS + 1) * FT]), sb("b2", [P, EXPERTS + 1])
        dr = lambda n, shape, dt=F32: nc.dram_tensor(n, shape, dt, kind="Internal").ap()
        S.q, S.k = (dr(n, [GROUPS + 2, JH, QROWS, SEQ], BF16) for n in ("s_q", "s_k"))
        S.low = dr("s_low", [GROUPS + 1, JH, 3, SEQ], BF16)
        S.o = dr("s_o", [GROUPS + 1, JH, HD + 1, SEQ])
        S.wt = dr("s_wt", [EXPERTS, TOKENS])

        load_stage(nc, T, I)
        if upto >= 1:
            norm_stage(nc, T, "ln1")
            qkv_stage(nc, T, I, S)
            attention_stage(nc, T, S)
            output_stage(nc, T, I, S)

        def mixture(n):
            norm_stage(nc, T, f"ln{n}")
            with nc.sbuf_tensor(f"WT{n}", [EXPERTS, TOKENS], F32) as T.WT:
                gate_stage(nc, T, I, S)
            experts_stage(nc, T, S, f"ex{n}")
            add_back_stage(nc, T, f"ab{n}")
        if upto >= 2:
            mixture(2)
        if upto >= 3:
            norm_stage(nc, T, "ln3", turn=False)
            retention_stage(nc, T, I)
        if upto >= 4:
            mixture(4)
        with nc.semaphore("written") as written, nc.Block() as block:
            @block.sync
            def _(sp):
                xo = out.rearrange("b (t p) d -> p (b t) d", p=P)
                for c in range(CHUNKS):
                    sp.dma_start(xo[:, CT * c:CT * (c + 1), :], T.X[:, CT * c:CT * (c + 1), :]).then_inc(written, 16)
                sp.wait_ge(written, 16 * CHUNKS)


def _arrange(v):
    import numpy as np
    g = {k: np.asarray(a) for k, a in v.items()}
    a, b, f = "L0_attn_a_", "L0_attn_b_", "L0_ffn_"
    w = g[a + "W_qkv"].reshape(HEADS, 3, HD, D)
    o = {
        "x": g[a + "x"],
        "w_qkv": w.transpose(3, 1, 0, 2).reshape(D, 3, D),
        "b_qkv": g[a + "b_qkv"].reshape(HEADS, 3, HD).transpose(0, 2, 1).reshape(D, 3),
        "w_out": g[a + "W_out"].T, "b_out": g[a + "b_out"],
        "rw": g[f + "router_w"], "w1": g[f + "w1"], "w2": g[f + "w2"], "sw1": g[f + "sw1"], "sw2": g[f + "sw2"],
        "b1cols": np.concatenate([g[f + "b1"], g[f + "sb1"][None]]).reshape(-1, P).T,
        "b2cols": np.concatenate([g[f + "b2"], g[f + "sb2"][None]]).T,
        "upper": np.triu(np.ones((P, P), np.float32), 1),
        "rank": np.arange(EXPERTS, 0, -1).astype(np.float32),
    }
    wq = g[b + "w_qkvff"]
    half = D // 2
    f32 = np.float32
    scale_vec = (np.arange(0, D, 2, dtype=f32) + f32(0.4 * D)) / f32(1.4 * D)
    power = np.arange(-(SEQ // 2), SEQ // 2, dtype=f32) / f32(64)
    scale = (scale_vec[None, :] ** power[:, None]).astype(f32)
    inv_freq = (f32(1.0) / f32(10000.0) ** (np.arange(half, dtype=f32) / f32(half))).astype(f32)
    angle = (np.arange(SEQ, dtype=f32)[:, None] * inv_freq[None, :]).astype(f32)
    sin, cos = np.sin(angle), np.cos(angle)
    both = np.stack([scale, f32(1.0) / scale])
    sign = np.tile(np.array([-1.0, 1.0], f32), half)
    cosn = np.repeat(cos * both, 2, axis=-1)
    sinn = np.repeat(sin * both, 2, axis=-1) * sign
    lay = lambda t: t.reshape(2, SEQ // P, P, D).transpose(2, 1, 0, 3)
    gamma = 1.0 - 2.0 ** (-5.0 - np.arange(HEADS, dtype=np.float64))
    at = np.arange(RL)
    diff = at[None, :] - at[:, None]
    mask = np.where(diff >= 0, gamma[:, None, None] ** np.maximum(diff, 0), 0.0) * HD ** -0.5
    head = np.repeat(np.arange(HEADS), HD)
    o.update({
        "r_wqkv": wq[:3 * D].T, "r_wff1": wq[3 * D:].T.reshape(D, 2, D), "r_wg": g[b + "w_gated"].T,
        "r_wp": g[b + "w_proj"].T, "r_wff2": g[b + "w_ff"].T.reshape(2, D, D).transpose(1, 0, 2),
        "r_cols": np.stack([g[b + "rms_w"], g[b + "gn_w"], g[b + "gn_b"], g[b + "b_gated"],
                            (gamma[head] ** RL).astype(f32)], axis=1),
        "r_bp": g[b + "b_proj"], "r_cos": lay(cosn), "r_sin": lay(sinn),
        "r_mask": mask.astype(f32).reshape(4, 4, RL, RL).transpose(2, 1, 0, 3),
        "r_qg": (gamma[head][None, :] ** at[:, None] * HD ** -0.5).astype(f32),
        "r_kg": (gamma[head][None, :] ** (RL - at)[:, None]).astype(f32),
        "r_diag": (head[:, None] == head[None, :]).astype(f32),
    })
    return {k: np.ascontiguousarray(x) for k, x in o.items()}


def build(nc, arrays, upto=99):
    I = {}
    for name, x in arrays.items():
        I[name] = nc.dram_tensor(f"in_{name}", x.shape, mybir.dt.from_np(x.dtype), kind="ExternalInput").ap()
    out = nc.dram_tensor("out_x", (BATCH, SEQ, D), F32, kind="ExternalOutput").ap()
    block_kernel(nc, I, out, upto)


def kernel(**inputs):
    import concourse.bacc as bacc
    from concourse.bass_utils import run_bass_kernel_spmd

    arrays = _arrange(inputs)
    nc = bacc.Bacc("TRN2", target_bir_lowering=False, num_devices=1)
    build(nc, arrays)
    r = run_bass_kernel_spmd(nc, [{f"in_{k}": v for k, v in arrays.items()}], core_ids=[0])
    return r.results[0]["out_x"]
```

```python
from contextlib import ExitStack

import concourse.bass as bass
from concourse import mybir

F32 = mybir.dt.float32
BF16 = mybir.dt.bfloat16
ALU = mybir.AluOpType
ACT = mybir.ActivationFunctionType
AX = mybir.AxisListType

P = 128
D = 128
BATCH, SEQ = 4, 1024
TOKENS = BATCH * SEQ
TILES = TOKENS // P
CH = 512
CT = CH // P
CHUNKS = TOKENS // CH
HEADS = 16
HD = D // HEADS
LN_EPS = 1e-5

JH = 4
GROUPS = BATCH * HEADS // JH
QROWS = 6 * HD
AROWS = QROWS + 3
KT = SEQ // P
VW = 32

EXPERTS = 8
FF = 512
FT = FF // P
CAP = 1280
FLOOR = -103.0
GATE_EPS = 1.1920929e-07
SHARED = 0.1

RL = 128
GN_EPS = 1e-5


class Count:

    def __init__(self, eng, sem, turn=0, each=0):
        self.eng, self.sem, self.turn, self.each, self.n = eng, sem, turn, each, 0

    def mark(self, ins, by=1):
        ins.then_inc(self.sem, by)
        self.n += by

    def settle(self, eng=None):
        (eng or self.eng).wait_ge(self.sem, self.turn * self.each + self.n)


class Buffers:
    pass


def ring(stack, make, name, n, shape, dt):
    return [stack.enter_context(make(f"{name}{i}", shape, dt)) for i in range(n)]


def load_stage(nc, T, I):
    with ExitStack() as st:
        loaded = st.enter_context(nc.semaphore("ld_loaded"))
        weights = st.enter_context(nc.semaphore("ld_weights"))
        blank = st.enter_context(nc.semaphore("ld_blank"))
        block = st.enter_context(nc.Block())
        xt = I["x"].rearrange("b (t p) d -> p (b t) d", p=P)

        @block.sync
        def _(sp):
            for c in range(CHUNKS):
                sp.dma_start(T.X[:, CT * c:CT * (c + 1), :], xt[:, CT * c:CT * (c + 1), :]).then_inc(loaded, 16)
            sp.dma_start(T.upper[:, :], I["upper"]).then_inc(loaded, 16)
            sp.dma_start(T.rank[:, :], I["rank"].partition_broadcast(P)).then_inc(loaded, 16)
            sp.dma_start(T.bo[:, :], I["b_out"].partition_broadcast(P)).then_inc(loaded, 16)
            sp.wait_ge(loaded, 16 * (CHUNKS + 3))

        @block.scalar
        def _(act):
            act.dma_start(T.sw1[:, :], I["sw1"]).then_inc(weights, 16)
            act.dma_start(T.sw2[:, :, :], I["sw2"].rearrange("(c p) h -> p c h", p=P)).then_inc(weights, 16)
            act.dma_start(T.rw[:, :], I["rw"]).then_inc(weights, 16)
            act.dma_start(T.b1[:, :], I["b1cols"]).then_inc(weights, 16)
            act.dma_start(T.b2[:, :], I["b2cols"]).then_inc(weights, 16)
            act.wait_ge(weights, 16 * 5)

        @block.gpsimd
        def _(pool):
            pool.memset(T.ident[:, :], 0.0).then_inc(blank, 1)
            pool.memset(T.ones[:, :], 1.0)
            pool.wait_ge(blank, 1)
            pool.affine_select(out=T.ident[:, :], in_=T.ident[:, :], compare_op=ALU.not_equal, fill=1.0,
                               base=0, pattern=[[-1, P]], channel_multiplier=1).then_inc(blank, 1)


def norm_stage(nc, T, tag, turn=True):
    with ExitStack() as st:
        sem = lambda n: st.enter_context(nc.semaphore(f"{tag}_{n}"))
        stats, spread, root, xh_ready, turned, copied = map(
            sem, ("stats", "spread", "root", "xh_ready", "turned", "copied"))
        XH = ring(st, nc.sbuf_tensor, f"{tag}_xh", 2, [P, CT, D], F32)
        pst = ring(st, nc.psum_tensor, f"{tag}_ps", 2, [P, CH], F32)
        bn = st.enter_context(nc.sbuf_tensor(f"{tag}_bn", [P, TILES, 6], F32))
        block = st.enter_context(nc.Block())

        @block.vector
        def _(dve):
            with dve.Fori(0, TILES // CT) as i:
                t = i * CT
                for k in range(CT):
                    nc.vector.bn_stats(bn[:, bass.ds(t + k, 1), :].rearrange("p t s -> p (t s)"),
                                       T.X[:, bass.ds(t + k, 1), :].rearrange("p t d -> p (t d)")).then_inc(stats, 1)
            dve.wait_ge(stats, TILES)
            mean, var, dif, sq = T.mv[:, :, 0], T.mv[:, :, 1], T.sd[:, :], T.rs[:, :]
            nc.vector.tensor_tensor(mean, bn[:, :, 1], bn[:, :, 4], ALU.add).then_inc(spread, 1)
            nc.vector.tensor_tensor(dif, bn[:, :, 1], bn[:, :, 4], ALU.subtract).then_inc(spread, 1)
            nc.vector.tensor_tensor(var, bn[:, :, 2], bn[:, :, 5], ALU.add).then_inc(spread, 1)
            dve.wait_ge(spread, 3)
            nc.vector.tensor_scalar(mean, mean, 0.5, None, ALU.mult).then_inc(spread, 1)
            nc.vector.tensor_tensor(sq, dif, dif, ALU.mult).then_inc(spread, 1)
            nc.vector.tensor_scalar(var, var, 1.0 / D, None, ALU.mult).then_inc(spread, 1)
            dve.wait_ge(spread, 6)
            nc.vector.scalar_tensor_tensor(out=var, in0=sq, scalar=0.25, in1=var, op0=ALU.mult, op1=ALU.add).then_inc(spread, 1)
            dve.wait_ge(spread, 7)
            nc.vector.tensor_scalar(T.sd[:, :], var, LN_EPS, None, ALU.add).then_inc(spread, 1)
            dve.wait_ge(root, 1)
            nc.vector.reciprocal(T.rs[:, :], T.sd[:, :]).then_inc(root, 1)
            dve.wait_ge(root, 2)
            if not turn:
                nc.vector.tensor_tensor(T.ri[:, :], T.ri[:, :], T.rs[:, :], ALU.mult).then_inc(root, 1)
                dve.wait_ge(root, 3)
                nc.vector.tensor_scalar(T.ri[:, :], T.ri[:, :], 1e-8, None, ALU.max).then_inc(root, 1)
                dve.wait_ge(root, 4)
                nc.vector.reciprocal(T.ri[:, :], T.ri[:, :]).then_inc(root, 1)
                dve.wait_ge(root, 5)
                nc.vector.tensor_tensor(T.ri[:, :], T.ri[:, :], T.rs[:, :], ALU.mult)
                return
            with dve.Fori(0, CHUNKS // 2) as i:
                for a in range(2):
                    dve.wait_ge(turned, 2 * i + a + 1)
                    for k in range(CT):
                        t = i * (2 * CT) + (a * CT + k)
                        ins = nc.vector.tensor_scalar(XH[a][:, k, :], T.X[:, bass.ds(t, 1), :].rearrange("p t d -> p (t d)"),
                                                      T.mv[:, bass.ds(t, 1), 0:1].rearrange("p t s -> p (t s)"),
                                                      T.rs[:, bass.ds(t, 1)], ALU.subtract, ALU.mult)
                    ins.then_inc(xh_ready, 1)

        @block.tensor
        def _(pe):
            if not turn:
                return
            pe.sem_inc(turned, 2)
            with pe.Fori(0, CHUNKS // 2) as i:
                for a in range(2):
                    pe.wait_ge(xh_ready, 2 * i + a + 1)
                    pe.wait_ge(copied, 2 * i + a + 1)
                    for k in range(CT):
                        ins = nc.tensor.transpose(pst[a][:, k * P:(k + 1) * P], XH[a][:, k, :], T.ident[:, :])
                    ins.then_inc(turned, 1)

        @block.scalar
        def _(act):
            act.sem_inc(copied, 2)
            act.wait_ge(spread, 8)
            if not turn:
                nc.scalar.activation(T.ri[:, :], T.mv[:, :, 1], ACT.Sqrt)
            nc.scalar.activation(T.sd[:, :], T.sd[:, :], ACT.Sqrt).then_inc(root, 1)
            if not turn:
                return
            with act.Fori(0, CHUNKS // 2) as i:
                for a in range(2):
                    act.wait_ge(turned, 2 * i + a + 3)
                    nc.scalar.copy(T.XT[:, bass.ds(i * (2 * CH) + a * CH, CH)], pst[a][:, :]).then_inc(copied, 1)


def qkv_stage(nc, T, I, S):
    with ExitStack() as st:
        sem = lambda n: st.enter_context(nc.semaphore(f"qkv_{n}"))
        weights, projected, evacuated, vturned, vkept, split, cleared = map(
            sem, ("weights", "projected", "evacuated", "vturned", "vkept", "split", "cleared"))
        stored = [sem("stored0"), sem("stored1")]
        chain = sem("chain")
        wqkv = st.enter_context(nc.sbuf_tensor("qkv_w", [P, 3, D], F32))
        bqkv = st.enter_context(nc.sbuf_tensor("qkv_b", [P, 3], F32))
        zero = st.enter_context(nc.sbuf_tensor("qkv_zero", [QROWS, 8, SEQ], BF16))
        QK = ring(st, nc.sbuf_tensor, "qkv_qk", 2, [P, 2, CH], F32)
        R = ring(st, nc.sbuf_tensor, "qkv_r", 2, [P, 2, CH], F32)
        VT = ring(st, nc.sbuf_tensor, "qkv_vt", 2, [P, CH], F32)
        part = ring(st, nc.sbuf_tensor, "qkv_part", 2, [P, 3, 2, CH], BF16)
        ps = [ring(st, nc.psum_tensor, f"qkv_ps{w}", 2, [P, CH], F32) for w in range(3)]
        pvt = ring(st, nc.psum_tensor, "qkv_pvt", 2, [P, CH], F32)
        block = st.enter_context(nc.Block())
        QP, KP = (0, 0, 0, 1, 1, 2), (0, 1, 2, 0, 1, 0)
        sq = S.q.rearrange("g j (r d) t -> (g j) r d t", d=HD)
        sk = S.k.rearrange("g j (r d) t -> (g j) r d t", d=HD)

        @block.sync
        def _(sp):
            sp.dma_start(wqkv[:, :, :], I["w_qkv"]).then_inc(weights, 16)
            sp.dma_start(bqkv[:, :], I["b_qkv"]).then_inc(weights, 16)
            for a in range(2):
                sp.sem_inc(stored[a], 16)
            with sp.Fori(0, BATCH) as b:
                for a in range(2):
                    sp.wait_ge(split, 2 * b + a + 1)
                    for r in range(6):
                        for s, w, n in ((sq, 0, QP[r]), (sk, 1, KP[r])):
                            sp.dma_start(s[bass.ds(b * HEADS, HEADS), r, :, a * CH:(a + 1) * CH],
                                         part[a][:, n, w, :]).then_inc(stored[a], 16)
            sp.wait_ge(cleared, 1)
            for s in (S.q, S.k):
                sp.dma_start(s[GROUPS:GROUPS + 2, :, :, :].rearrange("g j r t -> r (g j) t"), zero[:, :, :]).then_inc(weights, 16)
            sp.wait_ge(weights, 64)
            for a in range(2):
                sp.wait_ge(stored[a], BATCH * 12 * 16 + 16)

        @block.tensor
        def _(pe):
            pe.wait_ge(weights, 32)
            with pe.Fori(0, BATCH) as b:
                for a in range(2):
                    c = 2 * b + a
                    pe.wait_ge(evacuated, 3 * c + 3)
                    for w in (2, 0, 1):
                        nc.tensor.matmul(ps[w][a][:, :], wqkv[:, w, :], T.XT[:, bass.ds(b * SEQ + a * CH, CH)],
                                         start=True, stop=True).then_inc(projected, 1)
                    pe.wait_ge(evacuated, 3 * c + 7)
                    pe.wait_ge(vkept, c + 1)
                    for k in range(CT):
                        ins = nc.tensor.transpose(pvt[a][:, k * P:(k + 1) * P], VT[a][:, k * P:(k + 1) * P], T.ident[:, :])
                    ins.then_inc(vturned, 1)

        @block.scalar
        def _(act):
            act.sem_inc(evacuated, 6)
            act.sem_inc(vkept, 2)
            act.wait_ge(weights, 32)
            with act.Fori(0, BATCH) as b:
                for a in range(2):
                    c = 2 * b + a
                    act.wait_ge(projected, 3 * c + 1)
                    nc.scalar.activation(VT[a][:, :], ps[2][a][:, :], ACT.Identity, bias=bqkv[:, 2:3]).then_inc(evacuated, 1)
                    act.wait_ge(chain, 6 * b + 3 * a + 2)
                    for w in range(2):
                        act.wait_ge(projected, 3 * c + 2 + w)
                        nc.scalar.activation(QK[a][:, w, :], ps[w][a][:, :], ACT.Identity,
                                             bias=bqkv[:, w:w + 1]).then_inc(evacuated, 1)
                    act.wait_ge(vturned, c + 1)
                    nc.scalar.copy(T.V[:, bass.ds(b * 4, 4), CT * a:CT * (a + 1), :],
                                   pvt[a][:, :].rearrange("p (t g e) -> p g t e", t=CT, g=4)).then_inc(vkept, 1)

        @block.vector
        def _(dve):
            dve.sem_inc(chain, 6)
            with dve.Fori(0, BATCH) as b:
                link = Count(dve, chain, b, 6)
                link.n = 6
                for a in range(2):
                    dve.wait_ge(evacuated, 6 * b + 3 * a + 9)
                    dve.wait_ge(stored[a], 12 * 16 * b + 16)
                    q, r, p = QK[a][:, :, :], R[a][:, :, :], part[a]
                    link.mark(nc.vector.tensor_copy(p[:, 0, :, :], q))
                    link.settle()
                    link.mark(nc.vector.tensor_tensor(r, q, p[:, 0, :, :], ALU.subtract))
                    link.settle()
                    link.mark(nc.vector.tensor_copy(p[:, 1, :, :], r))
                    link.settle()
                    nc.vector.tensor_tensor(p[:, 2, :, :], r, p[:, 1, :, :], ALU.subtract).then_inc(split, 1)

        @block.gpsimd
        def _(pool):
            pool.memset(zero[:, :, :], 0.0).then_inc(cleared, 1)
            pool.memset(T.V[:, GROUPS, :, :], 0.0)
            with pool.Fori(0, TILES // CT) as i:
                xs = T.X[:, bass.ds(i * CT, CT), :]
                pool.tensor_tensor(xs, xs, T.bo[:, :].unsqueeze(1).to_broadcast([P, CT, D]), ALU.add)


def attention_stage(nc, T, S):
    STEPS = 16
    EXPS = 2 * STEPS
    HIGHS = JH * KT * 2
    HALF = HIGHS // 2
    with ExitStack() as st:
        sem = lambda n: st.enter_context(nc.semaphore(f"at_{n}"))
        (scored, exped, multiplied, o_kept, high_scored, high_kept, low_ready, low_turned, low_split,
         v_staged, chain, blanked) = map(sem, (
             "scored", "exped", "multiplied", "o_kept", "high_scored", "high_kept", "low_ready",
             "low_turned", "low_split", "v_staged", "chain", "blanked"))
        high_loaded = [sem("high_loaded0"), sem("high_loaded1")]
        loaded = [sem("loaded0"), sem("loaded1")]
        rows_stored, rows_loaded = sem("rows_stored"), [sem("rows_loaded0"), sem("rows_loaded1")]
        o_stored = [sem("o_stored0"), sem("o_stored1")]
        free = T.XT[:, :].bitcast(BF16)
        hq = [free[:, e * JH * SEQ:(e + 1) * JH * SEQ].rearrange("p (j t) -> p j t", j=JH) for e in range(2)]
        hk = ring(st, nc.sbuf_tensor, "at_hk", 2, [P, 2, SEQ], BF16)
        eq = ring(st, nc.sbuf_tensor, "at_eq", 2, [P, JH, SEQ], BF16)
        ek = ring(st, nc.sbuf_tensor, "at_ek", 2, [P, 2, SEQ], BF16)
        prob = ring(st, nc.sbuf_tensor, "at_prob", 2, [P, JH, 2, CH], F32)
        prob += [T.w1[:, :, :].rearrange("p (j k) q -> p j k q", k=2),
                 T.w2[:, :, :, :].rearrange("p (j k) c h -> p j k (c h)", k=2)]
        vst = ring(st, nc.sbuf_tensor, "at_v", 2, [P, KT, JH, VW], F32)
        osb = ring(st, nc.sbuf_tensor, "at_o", 2, [P, CH], F32)
        hmax = ring(st, nc.sbuf_tensor, "at_hmax", 2, [P, JH * KT, 2], F32)
        low = ring(st, nc.sbuf_tensor, "at_low", 2, [P, JH * KT], F32)
        rest = ring(st, nc.sbuf_tensor, "at_rest", 2, [JH * KT, P], F32)
        lparts = ring(st, nc.sbuf_tensor, "at_lparts", 2, [JH * KT, 3, P], BF16)
        ps = ring(st, nc.psum_tensor, "at_ps", 2, [P, 2, CH], F32)
        pso = ring(st, nc.psum_tensor, "at_pso", 2, [P, CH], F32)
        psh = ring(st, nc.psum_tensor, "at_psh", 2, [P, CH], F32)
        block = st.enter_context(nc.Block())

        def high_units(first, last):
            for n in range(first, last):
                yield n % JH, n // (2 * JH), n // JH % 2

        @block.sync
        def _(sp):
            def load_high(g, e):
                for s, d in ((S.q, hq[e]), (S.k, hk[e])):
                    for h in range(2):
                        sp.dma_start(d[64 * h:64 * h + QROWS, h:JH:2, :] if d is hq[e] else d[64 * h:64 * h + QROWS, :, :],
                                     s[bass.ds(g, 1), h:JH:2, 0:QROWS, :].rearrange("g j r t -> (g r) j t")
                                     ).then_inc(high_loaded[e], 16)

            def load_group(g, e):
                for s, d in ((S.q, eq[e]), (S.k, ek[e])):
                    for h in range(2):
                        sp.dma_start(d[64 * h:64 * h + QROWS, h:JH:2, :] if d is eq[e] else d[64 * h:64 * h + QROWS, :, :],
                                     s[bass.ds(g, 1), h:JH:2, 0:QROWS, :].rearrange("g j r t -> (g r) j t")
                                     ).then_inc(loaded[e], 16)

            def load_rows(g, e, nth):
                sp.wait_ge(low_split, nth)
                for j in range(JH):
                    sp.dma_start(S.low[bass.ds(g, 1), j, :, :].rearrange("g r (t c) -> (g t) r c", c=P),
                                 lparts[e][KT * j:KT * (j + 1), :, :]).then_inc(rows_stored, 16)
                sp.wait_ge(rows_stored, nth * JH * 16)
                for h in range(2):
                    sp.dma_start(eq[e][64 * h + QROWS:64 * h + AROWS, h:JH:2, :],
                                 S.low[bass.ds(g, 1), h:JH:2, :, :].rearrange("g j r t -> (g r) j t")
                                 ).then_inc(rows_loaded[e], 16)

            def store_o(g, qc):
                for j in range(JH):
                    sp.dma_start(S.o[bass.ds(g, 1), j, :, qc * CH:(qc + 1) * CH].rearrange("g r t -> (g r) t"),
                                 osb[qc][VW * j:VW * j + HD + 1, :]).then_inc(o_stored[qc], 16)

            for qc in range(2):
                sp.sem_inc(o_stored[qc], 16)
            sp.wait_ge(blanked, 4)
            load_high(0, 0)
            load_high(1, 1)
            sp.wait_ge(blanked, 8)
            load_group(0, 0)
            load_rows(0, 0, 1)
            with sp.Fori(0, GROUPS // 2) as turn:
                g0 = turn * 2
                for a in range(2):
                    g = g0 + a
                    sp.wait_ge(high_kept, 2 + HIGHS * g + HIGHS)
                    load_high(g + 2, a)
                    sp.wait_ge(exped, EXPS * g + 2)
                    load_group(g + 1, 1 - a)
                    sp.wait_ge(o_kept, 2 * g + 3)
                    store_o(g, 1)
                    load_rows(g + 1, 1 - a, g + 2)
                    sp.wait_ge(o_kept, 2 * g + 4)
                    store_o(g + 1, 0)
            sp.wait_ge(o_kept, 2 * GROUPS + 3)
            store_o(GROUPS, 1)
            for qc in range(2):
                sp.wait_ge(o_stored[qc], JH * 16 * (GROUPS + qc) + 16)
            for e in range(2):
                sp.wait_ge(high_loaded[e], 64 * (GROUPS // 2 + 1))
                sp.wait_ge(loaded[e], 64 * (GROUPS // 2 + 1 - e))
                sp.wait_ge(rows_loaded[e], 32 * (GROUPS // 2 + 1 - e))

        @block.gpsimd
        def _(pool):
            for e in range(2):
                pool.memset(hq[e].bitcast(F32), 0.0).then_inc(blanked, 1)
                pool.memset(hk[e][:, :, :].bitcast(F32), 0.0).then_inc(blanked, 1)
            for e in range(2):
                pool.memset(eq[e][:, :, :].bitcast(F32), 0.0).then_inc(blanked, 1)
                pool.memset(ek[e][:, :, :], 1.0).then_inc(blanked, 1)
            for e in range(2):
                pool.memset(vst[e][:, :, :, :], 1.0).then_inc(blanked, 1)
            for e in range(2, 4):
                pool.memset(prob[e], 0.0).then_inc(blanked, 1)

            def stage_v(g, e):
                pool.tensor_copy(vst[e][:, :, :, 0:HD],
                                 T.V[:, bass.ds(g, 1), :, :].rearrange("p g t (j e) -> p (g t) j e", e=HD)
                                 ).then_inc(v_staged, 1)

            pool.wait_ge(blanked, 12)
            stage_v(0, 0)
            with pool.Fori(0, GROUPS // 2) as turn:
                g0 = turn * 2
                for a in range(2):
                    g = g0 + a
                    pool.wait_ge(multiplied, 4 + 16 * g + 3)
                    stage_v(g + 1, 1 - a)

        @block.tensor
        def _(pe):
            used = [0]

            def high(e, unit):
                j, qt, kh = unit
                nc.tensor.matmul(psh[used[0] % 2][:, :], hq[e][:, j, qt * P:(qt + 1) * P],
                                 hk[e][:, j // 2, kh * CH:(kh + 1) * CH],
                                 start=True, stop=True).then_inc(high_scored, 1)
                used[0] += 1

            def turn_low(e, nth):
                pe.wait_ge(low_ready, nth)
                nc.tensor.transpose(psh[used[0] % 2][0:JH * KT, 0:P], low[e][:, :], T.ident[:, :]).then_inc(low_turned, 1)
                used[0] += 1

            def score(e, n, i, k):
                qc, kp, jp = n // 8, n % 8 // 2, n % 2
                ins = nc.tensor.matmul(ps[i][:, k, :], ek[e][:, jp, (2 * kp + k) * P:(2 * kp + k + 1) * P],
                                       eq[e][:, 2 * jp + i, qc * CH:(qc + 1) * CH], start=True, stop=True)
                if k == 1:
                    ins.then_inc(scored, 1)

            def multiply(e, c, k):
                qc, kt = c // 4, 2 * (c % 4) + k
                for j in range(JH):
                    ins = nc.tensor.matmul(pso[qc][VW * j:VW * (j + 1), :], vst[e][:, kt, j, :],
                                           prob[c % 4][:, j, k, :], start=(kt == 0), stop=(kt == KT - 1))
                ins.then_inc(multiplied, 1)

            pe.sem_inc(multiplied, 4)
            pe.wait_ge(blanked, 12)
            for j in range(JH):
                nc.tensor.matmul(pso[1][VW * j:VW * (j + 1), :], vst[1][:, 0, j, :], prob[3][:, j, 0, :],
                                 start=True, stop=False)
            pe.wait_ge(high_loaded[0], 64)
            for n, unit in enumerate(high_units(0, HIGHS)):
                pe.wait_ge(high_kept, n + 1)
                high(0, unit)
            pe.wait_ge(high_loaded[1], 64)
            for n, unit in enumerate(high_units(0, HALF)):
                pe.wait_ge(high_kept, HIGHS + n + 1 + (n == 4))
                if n == 5:
                    pe.wait_ge(chain, 2)
                high(1, unit)
                if n == 3:
                    pe.wait_ge(high_kept, HIGHS + n + 2)
                    turn_low(0, 1)
            start = HIGHS + HALF
            with pe.Fori(0, GROUPS // 2) as turn:
                g0 = turn * 2
                for a in range(2):
                    g, e = g0 + a, a
                    todo = [(1 - e, u) for u in high_units(HALF, HIGHS)] + [(e, u) for u in high_units(0, HALF)]
                    for n in range(STEPS):
                        if n == 0:
                            pe.wait_ge(loaded[e], g0 * 32 + 64)
                            pe.wait_ge(rows_loaded[e], g0 * 16 + 32)
                        if n == STEPS // 2:
                            pe.wait_ge(high_loaded[e], g0 * 32 + 128)
                        for i in range(2):
                            pe.wait_ge(exped, EXPS * g + 2 * n + i + 1)
                            for k in range(2):
                                score(e, n, i, k)
                                m = 4 * n + 2 * i + k
                                pe.wait_ge(high_kept, start + HIGHS * g + m + 1 + (m == HALF + 4))
                                if m == HALF + 5:
                                    pe.wait_ge(chain, 3 * g + 5)
                                high(*todo[m])
                            if i == 0:
                                if n == 3:
                                    pe.wait_ge(v_staged, g + 1)
                                if n in (3, 11):
                                    pe.wait_ge(o_kept, 2 * g + 2 + (n == 11))
                                if n < 3:
                                    multiply(1 - e, (6, 7, 7)[n], (1, 0, 1)[n])
                                else:
                                    multiply(e, (n - 3) // 2, (n - 3) % 2)
                        if n == STEPS // 2:
                            pe.wait_ge(high_kept, start + HIGHS * g + 4 * n + 4 + 1)
                            turn_low(1 - e, g + 2)
            pe.wait_ge(exped, 2 + EXPS * GROUPS)
            for c, k in ((6, 1), (7, 0), (7, 1)):
                multiply(1, c, k)

        @block.scalar
        def _(act):
            act.sem_inc(exped, 2)
            act.sem_inc(o_kept, 2)

            def keep(qc, before, done):
                act.wait_ge(multiplied, done)
                act.wait_ge(o_stored[qc], before + 16)
                nc.scalar.copy(osb[qc][:, :], pso[qc][:, :]).then_inc(o_kept, 1)

            act.wait_ge(blanked, 12)
            with act.Fori(0, GROUPS // 2) as turn:
                g0 = turn * 2
                for a in range(2):
                    g = g0 + a
                    for n in range(STEPS):
                        c = n // 2
                        if n % 2 == 0:
                            act.wait_ge(multiplied, 16 * g + 2 * c + 1)
                        for i in range(2):
                            act.wait_ge(scored, EXPS * g + 2 * n + i + 1)
                            nc.scalar.activation(prob[c % 4][:, 2 * (n % 2) + i, :, :], ps[i][:, :, :], ACT.Exp,
                                                 scale=HD ** -0.5).then_inc(exped, 1)
                        if n == 3:
                            keep(1, g * (JH * 16), 16 * g + 7)
                        if n == 11:
                            keep(0, g * (JH * 16), 16 * g + 15)
            keep(1, GROUPS * JH * 16, 16 * GROUPS + 7)

        @block.vector
        def _(dve):
            dve.sem_inc(high_kept, 2)
            used = [0]

            def take(e, unit, nth):
                j, qt, kh = unit
                dve.wait_ge(high_scored, nth)
                nc.vector.tensor_reduce(hmax[e][:, KT * j + qt, kh:kh + 1], psh[used[0] % 2][:, :], AX.X,
                                        ALU.max).then_inc(high_kept, 1)
                used[0] += 1

            def lowest(e, kept):
                dve.wait_ge(high_kept, kept)
                nc.vector.tensor_reduce(low[e][:, :], hmax[e][:, :, :], AX.X, ALU.max, negate=True).then_inc(low_ready, 1)

            def split_low(e, nth, links, rows):
                bank = psh[used[0] % 2][0:JH * KT, 0:P]
                dve.wait_ge(low_turned, nth)
                if rows is not None:
                    dve.wait_ge(rows_stored, rows)
                nc.vector.tensor_copy(lparts[e][:, 0, :], bank).then_inc(chain, 1)
                dve.wait_ge(chain, links + 1)
                nc.vector.tensor_tensor(rest[e][:, :], bank, lparts[e][:, 0, :], ALU.subtract).then_inc(chain, 1)
                dve.wait_ge(chain, links + 2)
                nc.vector.tensor_copy(lparts[e][:, 1, :], rest[e][:, :]).then_inc(chain, 1)
                dve.wait_ge(chain, links + 3)
                nc.vector.tensor_tensor(lparts[e][:, 2, :], rest[e][:, :], lparts[e][:, 1, :],
                                        ALU.subtract).then_inc(low_split, 1)
                used[0] += 1

            for n, unit in enumerate(high_units(0, HIGHS)):
                take(0, unit, n + 1)
            lowest(0, 2 + HIGHS)
            for n, unit in enumerate(high_units(0, HALF)):
                take(1, unit, HIGHS + n + 1)
                if n == 3:
                    split_low(0, 1, 0, None)
            start = HIGHS + HALF
            with dve.Fori(0, GROUPS // 2) as turn:
                g0 = turn * 2
                for a in range(2):
                    g, e = g0 + a, a
                    todo = [(1 - e, u) for u in high_units(HALF, HIGHS)] + [(e, u) for u in high_units(0, HALF)]
                    for m in range(HIGHS):
                        if m == HALF:
                            lowest(1 - e, 2 + start + HIGHS * g + HALF)
                        take(*todo[m], start + HIGHS * g + m + 1)
                        if m == HALF + 3:
                            split_low(1 - e, g + 2, 3 * g + 3, g * (JH * 16) + JH * 16)


def output_stage(nc, T, I, S):
    with ExitStack() as st:
        sem = lambda n: st.enter_context(nc.semaphore(f"out_{n}"))
        weights, experts, inverted, divided, projected, added = map(
            sem, ("weights", "experts", "inverted", "divided", "projected", "added"))
        loaded = [sem("loaded0"), sem("loaded1")]
        wo = st.enter_context(nc.sbuf_tensor("out_w", [P, D], F32))
        OT = ring(st, nc.sbuf_tensor, "out_o", 2, [P, CH], F32)
        DN = ring(st, nc.sbuf_tensor, "out_dn", 2, [P, CH], F32)
        ps = ring(st, nc.psum_tensor, "out_ps", 2, [P, CH], F32)
        block = st.enter_context(nc.Block())
        so = S.o.rearrange("g j r t -> (g j) r t")

        @block.scalar
        def _(act):
            act.dma_start(T.w1[:, :, :], I["w1"].rearrange("e h f -> h e f")).then_inc(experts, 16)
            act.dma_start(T.w2[:, :, :, :], I["w2"].rearrange("e (c p) h -> p e c h", p=P)).then_inc(experts, 16)
            act.wait_ge(experts, 32)

        @block.sync
        def _(sp):
            sp.dma_start(wo[:, :], I["w_out"]).then_inc(weights, 16)
            sp.wait_ge(weights, 16)
            with sp.Fori(0, BATCH) as b:
                for a in range(2):
                    sp.wait_ge(added, 2 * b + a + 1)
                    heads = so[bass.ds(b * HEADS + JH, HEADS), :, a * CH:(a + 1) * CH]
                    sp.dma_start(OT[a][:, :], heads[:, 0:HD, :]).then_inc(loaded[a], 16)
                    for r in range(HD):
                        sp.dma_start(DN[a][r:P:HD, :], heads[:, HD, :]).then_inc(loaded[a], 16)

        @block.vector
        def _(dve):
            dve.sem_inc(added, 2)
            with dve.Fori(0, BATCH) as b:
                for a in range(2):
                    c = 2 * b + a
                    dve.wait_ge(loaded[a], b * (16 * (HD + 1)) + 16 * (HD + 1))
                    nc.vector.reciprocal(DN[a][:, :], DN[a][:, :]).then_inc(inverted, 1)
                    dve.wait_ge(inverted, c + 1)
                    nc.vector.tensor_tensor(OT[a][:, :], OT[a][:, :], DN[a][:, :], ALU.mult).then_inc(divided, 1)
                    dve.wait_ge(projected, c + 1)
                    xs = T.X[:, bass.ds(c * CT, CT), :]
                    nc.vector.tensor_tensor(xs, ps[a][:, :].rearrange("p (t d) -> p t d", d=D), xs, ALU.add).then_inc(added, 1)

        @block.tensor
        def _(pe):
            pe.wait_ge(weights, 16)
            with pe.Fori(0, BATCH) as b:
                for a in range(2):
                    c = 2 * b + a
                    pe.wait_ge(divided, c + 1)
                    for k in range(CT):
                        ins = nc.tensor.matmul(ps[a][:, k * D:(k + 1) * D], OT[a][:, k * P:(k + 1) * P], wo[:, :],
                                               start=(k == 0), stop=(k == CT - 1), skip_group_check=True)
                    ins.then_inc(projected, 1)


def gate_stage(nc, T, I, S):
    N, E = TILES, EXPERTS
    with ExitStack() as st:
        gate_no[0] += 1
        tag = f"gate{gate_no[0]}"
        sem = lambda n: st.enter_context(nc.semaphore(f"{tag}_{n}"))
        logged, copied, turned, unturned, shifted, exped, masked, placed, weighed, chain, wdone, stored = map(
            sem, ("logged", "copied", "turned", "unturned", "shifted", "exped", "masked", "placed", "weighed",
                  "chain", "wdone", "stored"))
        sb = lambda n, shape: st.enter_context(nc.sbuf_tensor(f"{tag}_{n}", shape, F32))
        LG = sb("lg", [E, TOKENS])
        L, G, K2, EQ, W = (sb(n, [P, N, E]) for n in ("l", "g", "k2", "eq", "w"))
        M = sb("m", [P, N, 2, E])
        KEEP = sb("keep", [P, N, 2, E])
        A, B, POS = (sb(n, [P, N, 2, E]) for n in ("a", "b", "pos"))
        top, tot, den = sb("top", [P, N]), sb("tot", [P, N]), sb("den", [P, N])
        cnt = sb("cnt", [P, E])
        psl = ring(st, nc.psum_tensor, f"{tag}_psl", 4, [P, CH], F32)
        pst, psa, psb = (st.enter_context(nc.psum_tensor(f"{tag}_{n}", [P, CH], F32)) for n in ("pst", "psa", "psb"))
        block = st.enter_context(nc.Block())

        @block.tensor
        def _(pe):
            for c in range(CHUNKS):
                if c >= 4:
                    pe.wait_ge(copied, c - 3)
                nc.tensor.matmul(psl[c % 4][0:E, :], T.rw[:, :], T.XT[:, c * CH:(c + 1) * CH],
                                 start=True, stop=True).then_inc(logged, 1)
            pe.wait_ge(copied, CHUNKS)
            for t in range(N):
                ins = nc.tensor.transpose(pst[:, t * E:(t + 1) * E], LG[:, t * P:(t + 1) * P], T.ident[0:E, 0:E])
            ins.then_inc(turned, 1)
            pe.wait_ge(masked, 1)
            m = M[:, :, :, :].rearrange("p t k e -> p (t k e)")
            nc.tensor.matmul(psa[:, :], T.upper[:, :], m, start=True, stop=True)
            nc.tensor.matmul(psb[:, :], T.ones[:, :], m, start=True, stop=True).then_inc(placed, 1)
            pe.wait_ge(weighed, 1)
            for c in range(CHUNKS):
                if c >= 4:
                    pe.wait_ge(wdone, c - 3)
                for k in range(CT):
                    ins = nc.tensor.transpose(psl[c % 4][0:E, k * P:(k + 1) * P], W[:, c * CT + k, :], T.ident[:, :])
                ins.then_inc(unturned, 1)

        @block.scalar
        def _(act):
            for c in range(CHUNKS):
                act.wait_ge(logged, c + 1)
                nc.scalar.copy(LG[:, c * CH:(c + 1) * CH], psl[c % 4][0:E, :]).then_inc(copied, 1)
            act.wait_ge(shifted, 1)
            nc.scalar.activation(G[:, :, :], L[:, :, :], ACT.Exp).then_inc(exped, 1)
            for c in range(CHUNKS):
                act.wait_ge(unturned, c + 1)
                nc.scalar.copy(T.WT[:, c * CH:(c + 1) * CH], psl[c % 4][0:E, :]).then_inc(wdone, 1)
            act.wait_ge(wdone, CHUNKS)
            act.dma_start(S.wt, T.WT[:, :]).then_inc(stored, 16)
            act.wait_ge(stored, 16)

        @block.vector
        def _(dve):
            link = Count(dve, chain)
            wide = lambda a: a.unsqueeze(2).to_broadcast([P, N, E])
            rank = T.rank[:, :].unsqueeze(1).to_broadcast([P, N, E])

            def step(ins):
                link.mark(ins)
                link.settle()

            def first_best(out, key, best):
                step(nc.vector.tensor_tensor(EQ[:, :, :], key, wide(best), ALU.is_equal))
                step(nc.vector.tensor_tensor(EQ[:, :, :], EQ[:, :, :], rank, ALU.mult))
                step(nc.vector.tensor_reduce(top[:, :], EQ[:, :, :], AX.X, ALU.max))
                step(nc.vector.tensor_tensor(out, EQ[:, :, :], wide(top[:, :]), ALU.is_equal))

            dve.wait_ge(turned, 1)
            lg = pst[:, 0:N * E].rearrange("p (t e) -> p t e", e=E)
            step(nc.vector.tensor_reduce(top[:, :], lg, AX.X, ALU.max))
            nc.vector.tensor_tensor(L[:, :, :], lg, wide(top[:, :]), ALU.subtract).then_inc(shifted, 1)
            dve.wait_ge(shifted, 1)
            step(nc.vector.memset(den[:, :], 0.0))
            first_best(M[:, :, 0, :], L[:, :, :], den[:, :])
            step(nc.vector.tensor_scalar(K2[:, :, :], L[:, :, :], FLOOR, None, ALU.max))
            step(nc.vector.tensor_scalar(EQ[:, :, :], M[:, :, 0, :], FLOOR, None, ALU.mult))
            step(nc.vector.tensor_tensor(K2[:, :, :], K2[:, :, :], EQ[:, :, :], ALU.add))
            step(nc.vector.tensor_reduce(den[:, :], K2[:, :, :], AX.X, ALU.max))
            first_best(M[:, :, 1, :], K2[:, :, :], den[:, :])
            nc.vector.tensor_copy(EQ[:, :, :], M[:, :, 1, :]).then_inc(masked, 1)
            dve.wait_ge(exped, 1)
            step(nc.vector.tensor_reduce(tot[:, :], G[:, :, :], AX.X, ALU.add))
            step(nc.vector.reciprocal(tot[:, :], tot[:, :]))
            step(nc.vector.tensor_tensor(G[:, :, :], G[:, :, :], wide(tot[:, :]), ALU.mult))
            dve.wait_ge(placed, 1)
            a3 = lambda x: x[:, :, :, :].rearrange("p t k e -> p t (k e)")
            pb = psb[:, :].rearrange("p (t q) -> p t q", q=2 * E)
            step(nc.vector.tensor_copy(a3(A), pb))
            src, dst, s = A, B, 1
            while s < N:
                step(nc.vector.tensor_tensor(a3(dst)[:, s:N, :], a3(src)[:, s:N, :], a3(src)[:, 0:N - s, :], ALU.add))
                step(nc.vector.tensor_copy(a3(dst)[:, 0:s, :], a3(src)[:, 0:s, :]))
                src, dst, s = dst, src, 2 * s
            step(nc.vector.tensor_scalar(cnt[:, :], src[:, N - 1, 0, :], float(CAP), None, ALU.min))
            step(nc.vector.tensor_tensor(a3(POS), a3(src), pb, ALU.subtract))
            step(nc.vector.tensor_tensor(a3(POS), psa[:, :].rearrange("p (t q) -> p t q", q=2 * E), a3(POS), ALU.add))
            step(nc.vector.tensor_tensor(POS[:, :, 1, :], POS[:, :, 1, :],
                                         cnt[:, :].unsqueeze(1).to_broadcast([P, N, E]), ALU.add))
            step(nc.vector.tensor_scalar(a3(KEEP), a3(POS), float(CAP), None, ALU.is_lt))
            step(nc.vector.tensor_tensor(a3(KEEP), a3(KEEP), a3(M), ALU.mult))
            step(nc.vector.tensor_tensor(EQ[:, :, :], KEEP[:, :, 0, :], KEEP[:, :, 1, :], ALU.add))
            step(nc.vector.tensor_tensor(G[:, :, :], G[:, :, :], EQ[:, :, :], ALU.mult))
            step(nc.vector.tensor_reduce(tot[:, :], G[:, :, :], AX.X, ALU.add))
            step(nc.vector.tensor_scalar(tot[:, :], tot[:, :], GATE_EPS, None, ALU.max))
            step(nc.vector.reciprocal(tot[:, :], tot[:, :]))
            nc.vector.tensor_tensor(W[:, :, :], G[:, :, :], wide(tot[:, :]), ALU.mult).then_inc(weighed, 1)


gate_no = [0]


def experts_stage(nc, T, S, tag):
    NE = EXPERTS + 1
    NS = EXPERTS - 1
    with ExitStack() as st:
        sem = lambda n: st.enter_context(nc.semaphore(f"{tag}_{n}"))
        first, silued, second, scaled, summed, finished = map(
            sem, ("first", "silued", "second", "scaled", "summed", "finished"))
        wloaded = [sem("wloaded0"), sem("wloaded1")]
        WB = ring(st, nc.sbuf_tensor, f"{tag}_wb", 2, [P, EXPERTS, CH], F32)
        hid = ring(st, nc.sbuf_tensor, f"{tag}_hid", 2, [P, FT, CH], F32)
        tmp = ring(st, nc.sbuf_tensor, f"{tag}_tmp", 2, [P, CH], F32)
        acc = ring(st, nc.sbuf_tensor, f"{tag}_acc", 2, [P, CH], F32)
        ps1 = ring(st, nc.psum_tensor, f"{tag}_ps1", 4, [P, CH], F32)
        ps2 = ring(st, nc.psum_tensor, f"{tag}_ps2", 2, [P, CH], F32)
        block = st.enter_context(nc.Block())

        @block.sync
        def _(sp):
            with sp.Fori(0, CHUNKS // 2) as i:
                for a in range(2):
                    sp.wait_ge(scaled, NE * (2 * i + a) + NE)
                    sp.dma_start(WB[a][:, :, :], S.wt[:, bass.ds(i * (2 * CH) + a * CH, CH)].partition_broadcast(P)
                                 ).then_inc(wloaded[a], 16)

        @block.tensor
        def _(pe):
            def up(c, e, cols):
                for f in range(FT):
                    pe.wait_ge(silued, (c * NE + e) * FT + f + 1)
                    w = T.w1[:, e, f * P:(f + 1) * P] if e < EXPERTS else T.sw1[:, f * P:(f + 1) * P]
                    nc.tensor.matmul(ps1[f][:, :], w, T.XT[:, cols], start=True, stop=True).then_inc(first, 1)

            def down(c, a, e):
                k = (a * NE + e) % 2
                pe.wait_ge(scaled, c * NE + e + 2 * NE - 1)
                for f in range(FT):
                    pe.wait_ge(silued, (c * NE + e) * FT + f + 1 + FT)
                    w = T.w2[:, e, f, :] if e < EXPERTS else T.sw2[:, f, :]
                    ins = nc.tensor.matmul(ps2[k][:, :], w, hid[k][:, f, :], start=(f == 0), stop=(f == FT - 1))
                ins.then_inc(second, 1)

            with pe.Fori(0, CHUNKS // 2) as i:
                for a in range(2):
                    c = 2 * i + a
                    cols = bass.ds(i * (2 * CH) + a * CH, CH)
                    up(c, 0, cols)
                    for e in range(1, NE):
                        up(c, e, cols)
                        down(c, a, e - 1)
                    down(c, a, NE - 1)

        @block.scalar
        def _(act):
            act.sem_inc(silued, FT)
            act.sem_inc(second, 2)
            with act.Fori(0, CHUNKS // 2) as i:
                for a in range(2):
                    c = 2 * i + a
                    for e in range(NE):
                        k = (a * NE + e) % 2
                        act.wait_ge(second, c * NE + e + 1)
                        for f in range(FT):
                            act.wait_ge(first, (c * NE + e) * FT + f + 1)
                            nc.scalar.activation(hid[k][:, f, :], ps1[f][:, :], ACT.Silu,
                                                 bias=T.b1[:, e * FT + f:e * FT + f + 1]).then_inc(silued, 1)

        @block.vector
        def _(dve):
            dve.sem_inc(scaled, 2 * NE)
            dve.sem_inc(finished, 1)
            with dve.Fori(0, CHUNKS // 2) as i:
                for a in range(2):
                    c = 2 * i + a
                    dve.wait_ge(wloaded[a], 16 * i + 16)
                    for e in range(NE):
                        k = (a * NE + e) % 2
                        dve.wait_ge(second, c * NE + e + 3)
                        if e >= 2:
                            dve.wait_ge(summed, c * NS + max(e - 2, 1) + 2)
                        elif e == 0:
                            dve.wait_ge(finished, c + 1)
                        if e < EXPERTS:
                            nc.vector.scalar_tensor_tensor(out=tmp[k][:, :], in0=ps2[k][:, :], scalar=T.b2[:, e:e + 1],
                                                           in1=WB[a][:, e, :], op0=ALU.add, op1=ALU.mult).then_inc(scaled, 1)
                        else:
                            nc.vector.tensor_scalar(tmp[k][:, :], ps2[k][:, :], T.b2[:, e:e + 1], SHARED,
                                                    ALU.add, ALU.mult).then_inc(scaled, 1)
                    dve.wait_ge(scaled, (c + 1) * NE + 2 * NE)
                    dve.wait_ge(summed, c * NS + NS + 2)
                    nc.vector.tensor_tensor(T.ACC[:, bass.ds(i * (2 * CH) + a * CH, CH)], acc[a][:, :], tmp[k][:, :],
                                            ALU.add).then_inc(finished, 1)

        @block.gpsimd
        def _(pool):
            pool.sem_inc(summed, 2)
            with pool.Fori(0, CHUNKS // 2) as i:
                for a in range(2):
                    c = 2 * i + a
                    for e in range(1, EXPERTS):
                        k = (a * NE + e) % 2
                        pool.wait_ge(scaled, c * NE + e + 1 + 2 * NE)
                        if e > 1:
                            pool.wait_ge(summed, c * NS + e + 1)
                        pool.tensor_tensor(acc[a][:, :], tmp[1 - k][:, :] if e == 1 else acc[a][:, :], tmp[k][:, :],
                                           ALU.add).then_inc(summed, 1)


def add_back_stage(nc, T, tag):
    with ExitStack() as st:
        sem = lambda n: st.enter_context(nc.semaphore(f"{tag}_{n}"))
        fetched, turned, added = map(sem, ("fetched", "turned", "added"))
        buf = ring(st, nc.sbuf_tensor, f"{tag}_buf", 2, [P, CH], F32)
        ps = ring(st, nc.psum_tensor, f"{tag}_ps", 2, [P, CH], F32)
        block = st.enter_context(nc.Block())

        @block.scalar
        def _(act):
            act.sem_inc(turned, 2)
            with act.Fori(0, CHUNKS // 2) as i:
                for a in range(2):
                    act.wait_ge(turned, 2 * i + a + 1)
                    nc.scalar.copy(buf[a][:, :], T.ACC[:, bass.ds(i * (2 * CH) + a * CH, CH)]).then_inc(fetched, 1)

        @block.tensor
        def _(pe):
            with pe.Fori(0, CHUNKS // 2) as i:
                for a in range(2):
                    pe.wait_ge(fetched, 2 * i + a + 1)
                    pe.wait_ge(added, 2 * i + a + 1)
                    for k in range(CT):
                        ins = nc.tensor.transpose(ps[a][:, k * P:(k + 1) * P], buf[a][:, k * P:(k + 1) * P], T.ident[:, :])
                    ins.then_inc(turned, 1)

        @block.vector
        def _(dve):
            dve.sem_inc(added, 2)
            with dve.Fori(0, CHUNKS // 2) as i:
                for a in range(2):
                    dve.wait_ge(turned, 2 * i + a + 3)
                    xs = T.X[:, bass.ds(i * (2 * CT) + a * CT, CT), :]
                    nc.vector.tensor_tensor(xs, ps[a][:, :].rearrange("p (t d) -> p t d", d=D), xs, ALU.add).then_inc(added, 1)


def retention_stage(nc, T, I):
    NT = SEQ // RL
    HT = NT // 2
    TURNS = 4 + 3 * NT + 2
    WIDES = 6 + NT
    with ExitStack() as st:
        sem = lambda n: st.enter_context(nc.semaphore(f"rt_{n}"))
        (x_ready, turned, t_kept, projected, q_read, v_kept, decayed_qk, scored, masked, y_done, y_read,
         outered, m_free, wide, wide_kept, var_ready, rooted, yn_ready, gated, x_plus, chain, blank) = map(sem, (
             "x_ready", "turned", "t_kept", "projected", "q_read", "v_kept", "decayed_qk", "scored", "masked",
             "y_done", "y_read", "outered", "m_free", "wide", "wide_kept", "var_ready", "rooted", "yn_ready",
             "gated", "x_plus", "chain", "blank"))
        rotated = sem("rotated")
        loaded = sem("loaded")
        sb = lambda n, shape: st.enter_context(nc.sbuf_tensor(f"rt_{n}", shape, F32))
        wqkv, wff1, wg, wp, wff2 = sb("wqkv", [P, 3 * D]), sb("wff1", [P, 2, D]), sb("wg", [P, D]), sb("wp", [P, D]), sb("wff2", [P, 2, D])
        cols, bp = sb("cols", [P, 5]), sb("bp", [P, D])
        cosn, sinn = sb("cos", [P, NT, 2, D]), sb("sin", [P, NT, 2, D])
        mask = sb("mask", [P, 4, 4, RL])
        qg, kg, diag = sb("qg", [P, D]), sb("kg", [P, D]), sb("diag", [P, D])
        XH, XR = sb("xh", [P, NT, D]), sb("xr", [P, NT, D])
        XHT, XRT = sb("xht", [P, SEQ]), sb("xrt", [P, SEQ])
        GATE, GT = sb("gate", [P, SEQ]), sb("gt", [P, 2, SEQ])
        T1, T2 = sb("t1", [P, 2, D]), sb("t2", [P, 2, D])
        PAD = ring(st, nc.sbuf_tensor, "rt_pad", 2, [P, 2, HEADS, 32], F32)
        QD, KD = (ring(st, nc.sbuf_tensor, f"rt_{n}", r, [P, D], F32) for n, r in (("qd", 2), ("kd", 4)))
        VS = ring(st, nc.sbuf_tensor, "rt_vs", 4, [P, HEADS, 32], F32)
        QT = [T.XT[:, e * 4 * CH:(e + 1) * 4 * CH].rearrange("p (i j t) -> p i j t", i=4, j=4) for e in range(2)]
        KTr = ring(st, nc.sbuf_tensor, "rt_kt", 2, [P, 4, RL], F32)
        QDT = ring(st, nc.sbuf_tensor, "rt_qdt", 3, [P, RL], F32)
        YP = sb("yp", [P, 4, RL])
        pick = T.ident[:, :].rearrange("p (j e) -> p j e", e=32)[:, :, 0:HD]
        SM = ring(st, nc.sbuf_tensor, "rt_sm", 2, [P, 4, 4, RL], F32)
        STATE, UM = sb("state", [P, D]), sb("um", [P, D])
        YC, YN = sb("yc", [P, HT * HEADS, HD]), sb("yn", [P, HT * HEADS, HD])
        YT, GY = sb("yt", [P, CH]), sb("gy", [P, CH])
        mu, var = sb("mu", [P, HT * HEADS]), sb("var", [P, HT * HEADS])
        pt = ring(st, nc.psum_tensor, "rt_pt", 2, [P, CH], F32)
        pss = ring(st, nc.psum_tensor, "rt_ps", 2, [P, CH], F32)
        pq, py, pw, pm = (st.enter_context(nc.psum_tensor(f"rt_{n}", [P, CH], F32)) for n in ("pq", "py", "pw", "pm"))
        block = st.enter_context(nc.Block())
        LOADS = 13

        def kept_after_tile(k):
            return 4 + 3 * (k + 1)

        def use_of_widen(n):
            return max(2 * n - 1, 0)

        def use_of_values(k):
            return 2 * k + 2 if k < 5 else 6 + k

        @block.sync
        def _(sp):
            for d, s in ((wqkv[:, :], I["r_wqkv"]), (wff1[:, :, :], I["r_wff1"]), (wg[:, :], I["r_wg"]), (wp[:, :], I["r_wp"]),
                         (wff2[:, :, :], I["r_wff2"]), (cols[:, :], I["r_cols"]), (bp[:, :], I["r_bp"].partition_broadcast(P)),
                         (cosn[:, :, :, :], I["r_cos"]), (sinn[:, :, :, :], I["r_sin"]), (mask[:, :, :, :], I["r_mask"]),
                         (qg[:, :], I["r_qg"]), (kg[:, :], I["r_kg"]), (diag[:, :], I["r_diag"])):
                sp.dma_start(d, s).then_inc(loaded, 16)
            sp.wait_ge(loaded, 16 * LOADS)

        @block.tensor
        def _(pe):
            pe.wait_ge(loaded, 16 * LOADS)
            with pe.Fori(0, BATCH) as b:
                uses = [0]

                def turn_into(rows, src):
                    n = uses[0]
                    pe.wait_ge(t_kept, b * TURNS + n + 1)
                    for k, piece in enumerate(src):
                        ins = nc.tensor.transpose(pt[n % 2][0:rows, k * P:(k + 1) * P], piece, T.ident[:, :])
                    ins.then_inc(turned, 1)
                    uses[0] += 1

                def project(k):
                    pe.wait_ge(q_read, b * NT + k + 1)
                    pe.wait_ge(v_kept, b * NT + k + 1)
                    pe.wait_ge(t_kept, b * TURNS + 2 + (2 if k < HT else 4))
                    nc.tensor.matmul(pq[:, 0:3 * D], XRT[:, k * RL:(k + 1) * RL], wqkv[:, :],
                                     start=True, stop=True).then_inc(projected, 1)

                def turn_qk(k):
                    pe.wait_ge(rotated, b * NT + k + 1)
                    for w in range(2):
                        turn_into(P, [PAD[k % 2][:, w, 4 * i:4 * i + 4, :].rearrange("p h d -> p (h d)") for i in range(4)])
                    pe.wait_ge(decayed_qk, b * NT + k + 1)
                    turn_into(P, [QD[k % 2][:, :]])

                def score(k, i):
                    pe.wait_ge(masked, (b * NT + k) * 4 + i + 1)
                    if i == 0:
                        pe.wait_ge(t_kept, b * TURNS + 2 + kept_after_tile(k))
                    nc.tensor.matmul(pss[i % 2][:, :], KTr[k % 2][:, i, :], QT[k % 2][:, i, :, :],
                                     start=True, stop=True).then_inc(scored, 1)

                def values(k):
                    pe.wait_ge(wide_kept, b * WIDES + use_of_values(k) + 1)
                    pe.wait_ge(v_kept, b * NT + k + 2)
                    for i in range(4):
                        pe.wait_ge(masked, (b * NT + k) * 4 + i + 3)
                        for j in range(4):
                            ins = nc.tensor.matmul(pw[32 * j:32 * (j + 1), i * RL:(i + 1) * RL], VS[k % 4][:, 4 * i + j, :],
                                                   SM[k % 2][:, i, j, :], start=True, stop=True,
                                                   tile_position=(0, 32 * j), skip_group_check=True)
                    ins.then_inc(wide, 1)

                def gather(k):
                    o = k % HT * D
                    if k % HT == 0:
                        pe.wait_ge(y_read, b * 2 + k // HT + 1)
                    if k:
                        pe.wait_ge(m_free, b * (NT + 1) + k + 1)
                        nc.tensor.matmul(py[:, o:o + D], QDT[k % 3][:, :], STATE[:, :], start=True, stop=False,
                                         skip_group_check=True)
                    pe.wait_ge(wide_kept, b * WIDES + use_of_values(k) + 2)
                    for i in range(4):
                        ins = nc.tensor.matmul(py[:, o + i * 32:o + (i + 1) * 32], YP[:, i, :], pick,
                                               start=(k == 0 and i == 0), stop=(i == 3), skip_group_check=True)
                    ins.then_inc(y_done, 1)

                def outer(k):
                    pe.wait_ge(m_free, b * (NT + 1) + k + 1)
                    pe.wait_ge(decayed_qk, b * NT + k + 1)
                    nc.tensor.matmul(pm[:, 0:D], KD[k % 4][:, :], VS[k % 4][:, :, 0:HD], start=True, stop=True).then_inc(outered, 1)

                def widen(n):
                    pe.wait_ge(wide_kept, b * WIDES + use_of_widen(n) + 1)
                    w, x = (wg[:, :], XHT) if n < 2 else (wff1[:, (n - 2) // 2, :], XRT)
                    pe.wait_ge(t_kept, b * TURNS + 6)
                    nc.tensor.matmul(pw[:, :], w, x[:, n % 2 * CH:(n % 2 + 1) * CH], start=True, stop=True).then_inc(wide, 1)

                def finish(half):
                    pe.wait_ge(gated, b * 2 + half + 1)
                    pe.wait_ge(wide_kept, b * WIDES + use_of_widen(5) + 2)
                    pe.wait_ge(m_free, b * (NT + 1) + NT + half)
                    for k in range(HT):
                        out = pm[:, k * D:(k + 1) * D]
                        for f in range(2):
                            nc.tensor.matmul(out, GT[:, f, half * CH + k * P:half * CH + (k + 1) * P], wff2[:, f, :],
                                             start=(k == 0 and f == 0), stop=False, skip_group_check=True)
                        ins = nc.tensor.matmul(out, GY[:, k * P:(k + 1) * P], wp[:, :], start=False, stop=(k == HT - 1),
                                               skip_group_check=True)
                    ins.then_inc(outered, 1)

                def turn_y(half):
                    pe.wait_ge(yn_ready, b * 2 + half + 1)
                    turn_into(P, [YN[:, k * HEADS:(k + 1) * HEADS, :].rearrange("p h d -> p (h d)") for k in range(HT)])

                for n in range(4):
                    pe.wait_ge(x_ready, b * 4 + n + 1)
                    src = (XH, XR)[n % 2]
                    turn_into(P, [src[:, n // 2 * HT + k, :] for k in range(HT)])
                project(0)
                project(1)
                turn_qk(0)
                for k in range(NT + 1):
                    if k < NT:
                        if k < 6:
                            widen(k)
                        score(k, 0)
                        score(k, 1)
                    if k >= 1:
                        values(k - 1)
                    if k < NT:
                        score(k, 2)
                    if k + 1 < NT:
                        turn_qk(k + 1)
                    if k < NT:
                        score(k, 3)
                    if k + 2 < NT:
                        project(k + 2)
                    if k >= 1:
                        gather(k - 1)
                        if k < NT:
                            outer(k - 1)
                    if k == 6:
                        turn_y(0)
                    if k == NT:
                        finish(0)
                turn_y(1)
                finish(1)
                assert uses[0] == TURNS

        @block.scalar
        def _(act):
            act.sem_inc(t_kept, 2)
            act.sem_inc(v_kept, 1)
            act.sem_inc(wide_kept, 1)
            act.wait_ge(loaded, 16 * LOADS)
            with act.Fori(0, BATCH) as b:
                uses = [0]

                def keep(out, cols=CH, **how):
                    n = uses[0]
                    act.wait_ge(turned, b * TURNS + n + 1)
                    nc.scalar.activation(out, pt[n % 2][:, 0:cols], ACT.Identity, **how).then_inc(t_kept, 1)
                    uses[0] += 1

                def keep_v(k):
                    act.wait_ge(q_read, b * NT + k + 2)
                    nc.scalar.copy(VS[k % 4][:, :, 0:HD], pq[:, 2 * D:3 * D].rearrange("p (h e) -> p h e", e=HD)
                                   ).then_inc(v_kept, 1)

                def keep_qk(k):
                    n = uses[0]
                    act.wait_ge(turned, b * TURNS + n + 1)
                    for j in range(4):
                        rows = slice(32 * j, 32 * (j + 1))
                        ins = nc.scalar.copy(QT[k % 2][rows, :, j, :], pt[n % 2][rows, :].rearrange("p (i t) -> p i t", t=RL))
                    ins.then_inc(t_kept, 1)
                    uses[0] += 1
                    keep(KTr[k % 2][:, :, :].rearrange("p i t -> p (i t)"))
                    keep(QDT[k % 3][:, :], RL)

                def keep_values(k):
                    act.wait_ge(wide, b * WIDES + use_of_values(k) + 1)
                    nc.scalar.copy(YP[:, :, :].rearrange("p i t -> p (i t)"), pw[:, :]).then_inc(wide_kept, 1)

                def keep_wide(n):
                    act.wait_ge(wide, b * WIDES + use_of_widen(n) + 1)
                    if n < 2:
                        nc.scalar.activation(GATE[:, n * CH:(n + 1) * CH], pw[:, :], ACT.Silu, bias=cols[:, 3:4]).then_inc(wide_kept, 1)
                    else:
                        nc.scalar.activation(GT[:, (n - 2) // 2, n % 2 * CH:(n % 2 + 1) * CH], pw[:, :], ACT.Gelu).then_inc(wide_kept, 1)

                def root(half):
                    act.wait_ge(var_ready, b * 2 + half + 1)
                    nc.scalar.activation(var[:, :], var[:, :], ACT.Sqrt).then_inc(rooted, 1)

                def keep_y():
                    keep(YT[:, :], scale=cols[:, 1:2], bias=cols[:, 2:3])

                for n in range(4):
                    half = slice(n // 2 * CH, (n // 2 + 1) * CH)
                    if n % 2:
                        keep(XRT[:, half], scale=cols[:, 0:1])
                    else:
                        keep(XHT[:, half])
                keep_v(0)
                keep_v(1)
                keep_qk(0)
                for k in range(NT + 1):
                    if k < 6:
                        keep_wide(k)
                    if k >= 1:
                        keep_values(k - 1)
                    if k + 1 < NT:
                        keep_qk(k + 1)
                    if k + 2 < NT:
                        keep_v(k + 2)
                    if k == 5:
                        root(0)
                    if k == 6:
                        keep_y()
                root(1)
                keep_y()

        @block.vector
        def _(dve):
            dve.sem_inc(q_read, 1)
            dve.sem_inc(masked, 2)
            dve.sem_inc(y_read, 1)
            dve.sem_inc(m_free, 1)
            dve.wait_ge(loaded, 16 * LOADS)
            dve.wait_ge(blank, 5 + 4)
            with dve.Fori(0, BATCH) as b:
                CHAIN = NT * 2 + (NT - 2) + 2 * 6
                link = Count(dve, chain, b, CHAIN)

                def step(ins):
                    link.mark(ins)
                    link.settle()

                def normalise(n):
                    half, dst, inv = n // 2, (XH, XR)[n % 2], (T.rs, T.ri)[n % 2]
                    for k in range(half * HT, (half + 1) * HT):
                        t = b * NT + k
                        ins = nc.vector.tensor_scalar(dst[:, k, :], T.X[:, bass.ds(t, 1), :].rearrange("p t d -> p (t d)"),
                                                      T.mv[:, bass.ds(t, 1), 0:1].rearrange("p t s -> p (t s)"),
                                                      inv[:, bass.ds(t, 1)], ALU.subtract, ALU.mult)
                    ins.then_inc(x_ready, 1)

                def rotate(k):
                    dve.wait_ge(projected, b * NT + k + 1)
                    if k >= 2:
                        dve.wait_ge(decayed_qk, b * NT + k - 1)
                    qk = pq[:, 0:2 * D].rearrange("p (w d) -> p w d", w=2)
                    link.mark(nc.vector.tensor_tensor(T1[:, :, :], qk, cosn[:, k, :, :], ALU.mult))
                    link.mark(nc.vector.tensor_tensor(T2[:, :, 0:D:2], qk[:, :, 1:D:2], sinn[:, k, :, 0:D:2], ALU.mult))
                    nc.vector.tensor_tensor(T2[:, :, 1:D:2], qk[:, :, 0:D:2], sinn[:, k, :, 1:D:2], ALU.mult).then_inc(q_read, 1)
                    link.settle()
                    dve.wait_ge(q_read, b * NT + k + 2)
                    v = lambda a: a[:, :, :].rearrange("p w (h d) -> p w h d", d=HD)
                    nc.vector.tensor_tensor(PAD[k % 2][:, :, :, 0:HD], v(T1), v(T2), ALU.add).then_inc(rotated, 1)
                    dve.wait_ge(rotated, b * NT + k + 1)

                def decay_scores(k, i):
                    dve.wait_ge(scored, (b * NT + k) * 4 + i + 1)
                    nc.vector.tensor_tensor(SM[k % 2][:, i, :, :], pss[i % 2][:, :].rearrange("p (j t) -> p j t", t=RL),
                                            mask[:, i, :, :], ALU.mult).then_inc(masked, 1)

                def carry(k):
                    dve.wait_ge(outered, b * (NT + 1) + k + 1)
                    if k == 0:
                        nc.vector.tensor_tensor(STATE[:, :], pm[:, 0:D], diag[:, :], ALU.mult).then_inc(m_free, 1)
                        return
                    step(nc.vector.tensor_tensor(UM[:, :], pm[:, 0:D], diag[:, :], ALU.mult))
                    dve.wait_ge(m_free, b * (NT + 1) + k + 1)
                    nc.vector.scalar_tensor_tensor(out=STATE[:, :], in0=STATE[:, :], scalar=cols[:, 4:5], in1=UM[:, :],
                                                   op0=ALU.mult, op1=ALU.add).then_inc(m_free, 1)

                def group_norm_a(half):
                    dve.wait_ge(y_done, b * NT + (half + 1) * HT)
                    y = py[:, :].rearrange("p (h d) -> p h d", d=HD)
                    step(nc.vector.tensor_reduce(mu[:, :], y, AX.X, ALU.add))
                    step(nc.vector.tensor_scalar(mu[:, :], mu[:, :], 1.0 / HD, None, ALU.mult))
                    nc.vector.tensor_tensor(YC[:, :, :], y, mu[:, :].unsqueeze(2).to_broadcast([P, HT * HEADS, HD]),
                                            ALU.subtract).then_inc(y_read, 1)
                    dve.wait_ge(y_read, b * 2 + half + 2)
                    step(nc.vector.tensor_tensor(YN[:, :, :], YC[:, :, :], YC[:, :, :], ALU.mult))
                    step(nc.vector.tensor_reduce(var[:, :], YN[:, :, :], AX.X, ALU.add))
                    nc.vector.tensor_scalar(var[:, :], var[:, :], 1.0 / HD, GN_EPS, ALU.mult, ALU.add).then_inc(var_ready, 1)

                def group_norm_b(half):
                    dve.wait_ge(rooted, b * 2 + half + 1)
                    step(nc.vector.reciprocal(mu[:, :], var[:, :]))
                    nc.vector.tensor_tensor(YN[:, :, :], YC[:, :, :], mu[:, :].unsqueeze(2).to_broadcast([P, HT * HEADS, HD]),
                                            ALU.mult).then_inc(yn_ready, 1)

                def add(half):
                    dve.wait_ge(x_plus, b * 2 + half + 1)
                    xs = T.X[:, bass.ds(b * NT + half * HT, HT), :]
                    step(nc.vector.tensor_tensor(xs, xs, XH[:, half * HT:(half + 1) * HT, :], ALU.add))
                    dve.wait_ge(outered, b * (NT + 1) + NT + half)
                    nc.vector.tensor_tensor(xs, pm[:, :].rearrange("p (t d) -> p t d", d=D), xs, ALU.add).then_inc(m_free, 1)

                for n in range(4):
                    normalise(n)
                rotate(0)
                rotate(1)
                for k in range(NT):
                    decay_scores(k, 0)
                    if k == 5:
                        group_norm_a(0)
                    decay_scores(k, 1)
                    if k >= 2:
                        carry(k - 2)
                    decay_scores(k, 2)
                    if k + 2 < NT:
                        rotate(k + 2)
                    decay_scores(k, 3)
                    if k == 6:
                        group_norm_b(0)
                carry(NT - 2)
                add(0)
                group_norm_a(1)
                group_norm_b(1)
                add(1)
                assert link.n == CHAIN

        @block.gpsimd
        def _(pool):
            for e in range(2):
                pool.memset(PAD[e][:, :, :, :], 0.0).then_inc(blank, 1)
            pool.memset(STATE[:, :], 0.0).then_inc(blank, 1)
            for e in range(2):
                pool.memset(QT[e], 0.0).then_inc(blank, 1)
            for e in range(4):
                pool.memset(VS[e][:, :, :], 0.0).then_inc(blank, 1)
            pool.wait_ge(loaded, 16 * LOADS)
            with pool.Fori(0, BATCH) as b:
                def decay_qk(k):
                    pool.wait_ge(rotated, b * NT + k + 1)
                    h = lambda a: a[:, :].rearrange("p (h d) -> p h d", d=HD)
                    pool.tensor_tensor(h(KD[k % 4]), PAD[k % 2][:, 1, :, 0:HD], h(kg), ALU.mult)
                    pool.tensor_tensor(h(QD[k % 2]), PAD[k % 2][:, 0, :, 0:HD], h(qg), ALU.mult).then_inc(decayed_qk, 1)

                def plus(half):
                    pool.wait_ge(turned, b * TURNS + 2 * half + 1)
                    xs = XH[:, half * HT:(half + 1) * HT, :]
                    pool.tensor_tensor(xs, xs, bp[:, :].unsqueeze(1).to_broadcast([P, HT, D]), ALU.add).then_inc(x_plus, 1)

                def gate(half):
                    pool.wait_ge(t_kept, b * TURNS + 2 + TURNS - 1 + half)
                    pool.wait_ge(wide_kept, b * WIDES + 2 + use_of_widen(half))
                    pool.tensor_tensor(GY[:, :], YT[:, :], GATE[:, half * CH:(half + 1) * CH], ALU.mult).then_inc(gated, 1)

                decay_qk(0)
                decay_qk(1)
                for k in range(NT):
                    if k in (0, 1):
                        plus(k)
                    if k == 6:
                        gate(0)
                    if k + 2 < NT:
                        decay_qk(k + 2)
                gate(1)


def block_kernel(nc, I, out, upto=99):
    T, S = Buffers(), Buffers()
    with ExitStack() as st:
        sb = lambda n, shape, dt=F32: st.enter_context(nc.sbuf_tensor(n, shape, dt))
        T.X, T.XT = sb("X", [P, TILES, D]), sb("XT", [P, TOKENS])
        T.V = sb("V", [P, GROUPS + 1, KT, JH * HD])
        T.ACC = T.V[:, 0:GROUPS, :, :].rearrange("p g t e -> p (g t e)")
        T.ident, T.ones, T.upper, T.bo = (sb(n, [P, P]) for n in ("ident", "ones", "upper", "bo"))
        T.rank = sb("rank", [P, EXPERTS])
        T.mv, T.sd, T.rs, T.ri = sb("mv", [P, TILES, 2]), sb("sd", [P, TILES]), sb("rs", [P, TILES]), sb("ri", [P, TILES])
        T.w1, T.w2 = sb("w1", [P, EXPERTS, FF]), sb("w2", [P, EXPERTS, FT, D])
        T.sw1, T.sw2, T.rw = sb("sw1", [P, FF]), sb("sw2", [P, FT, D]), sb("rw", [P, EXPERTS])
        T.b1, T.b2 = sb("b1", [P, (EXPERTS + 1) * FT]), sb("b2", [P, EXPERTS + 1])
        dr = lambda n, shape, dt=F32: nc.dram_tensor(n, shape, dt, kind="Internal").ap()
        S.q, S.k = (dr(n, [GROUPS + 2, JH, QROWS, SEQ], BF16) for n in ("s_q", "s_k"))
        S.low = dr("s_low", [GROUPS + 1, JH, 3, SEQ], BF16)
        S.o = dr("s_o", [GROUPS + 1, JH, HD + 1, SEQ])
        S.wt = dr("s_wt", [EXPERTS, TOKENS])

        load_stage(nc, T, I)
        if upto >= 1:
            norm_stage(nc, T, "ln1")
            qkv_stage(nc, T, I, S)
            attention_stage(nc, T, S)
            output_stage(nc, T, I, S)

        def mixture(n):
            norm_stage(nc, T, f"ln{n}")
            with nc.sbuf_tensor(f"WT{n}", [EXPERTS, TOKENS], F32) as T.WT:
                gate_stage(nc, T, I, S)
            experts_stage(nc, T, S, f"ex{n}")
            add_back_stage(nc, T, f"ab{n}")
        if upto >= 2:
            mixture(2)
        if upto >= 3:
            norm_stage(nc, T, "ln3", turn=False)
            retention_stage(nc, T, I)
        if upto >= 4:
            mixture(4)
        with nc.semaphore("written") as written, nc.Block() as block:
            @block.sync
            def _(sp):
                xo = out.rearrange("b (t p) d -> p (b t) d", p=P)
                for c in range(CHUNKS):
                    sp.dma_start(xo[:, CT * c:CT * (c + 1), :], T.X[:, CT * c:CT * (c + 1), :]).then_inc(written, 16)
                sp.wait_ge(written, 16 * CHUNKS)


def _arrange(v):
    import numpy as np
    g = {k: np.asarray(a) for k, a in v.items()}
    a, b, f = "L0_attn_a_", "L0_attn_b_", "L0_ffn_"
    w = g[a + "W_qkv"].reshape(HEADS, 3, HD, D)
    o = {
        "x": g[a + "x"],
        "w_qkv": w.transpose(3, 1, 0, 2).reshape(D, 3, D),
        "b_qkv": g[a + "b_qkv"].reshape(HEADS, 3, HD).transpose(0, 2, 1).reshape(D, 3),
        "w_out": g[a + "W_out"].T, "b_out": g[a + "b_out"],
        "rw": g[f + "router_w"], "w1": g[f + "w1"], "w2": g[f + "w2"], "sw1": g[f + "sw1"], "sw2": g[f + "sw2"],
        "b1cols": np.concatenate([g[f + "b1"], g[f + "sb1"][None]]).reshape(-1, P).T,
        "b2cols": np.concatenate([g[f + "b2"], g[f + "sb2"][None]]).T,
        "upper": np.triu(np.ones((P, P), np.float32), 1),
        "rank": np.arange(EXPERTS, 0, -1).astype(np.float32),
    }
    wq = g[b + "w_qkvff"]
    half = D // 2
    f32 = np.float32
    scale_vec = (np.arange(0, D, 2, dtype=f32) + f32(0.4 * D)) / f32(1.4 * D)
    power = np.arange(-(SEQ // 2), SEQ // 2, dtype=f32) / f32(64)
    scale = (scale_vec[None, :] ** power[:, None]).astype(f32)
    inv_freq = (f32(1.0) / f32(10000.0) ** (np.arange(half, dtype=f32) / f32(half))).astype(f32)
    angle = (np.arange(SEQ, dtype=f32)[:, None] * inv_freq[None, :]).astype(f32)
    sin, cos = np.sin(angle), np.cos(angle)
    both = np.stack([scale, f32(1.0) / scale])
    sign = np.tile(np.array([-1.0, 1.0], f32), half)
    cosn = np.repeat(cos * both, 2, axis=-1)
    sinn = np.repeat(sin * both, 2, axis=-1) * sign
    lay = lambda t: t.reshape(2, SEQ // P, P, D).transpose(2, 1, 0, 3)
    gamma = 1.0 - 2.0 ** (-5.0 - np.arange(HEADS, dtype=np.float64))
    at = np.arange(RL)
    diff = at[None, :] - at[:, None]
    mask = np.where(diff >= 0, gamma[:, None, None] ** np.maximum(diff, 0), 0.0) * HD ** -0.5
    head = np.repeat(np.arange(HEADS), HD)
    o.update({
        "r_wqkv": wq[:3 * D].T, "r_wff1": wq[3 * D:].T.reshape(D, 2, D), "r_wg": g[b + "w_gated"].T,
        "r_wp": g[b + "w_proj"].T, "r_wff2": g[b + "w_ff"].T.reshape(2, D, D).transpose(1, 0, 2),
        "r_cols": np.stack([g[b + "rms_w"], g[b + "gn_w"], g[b + "gn_b"], g[b + "b_gated"],
                            (gamma[head] ** RL).astype(f32)], axis=1),
        "r_bp": g[b + "b_proj"], "r_cos": lay(cosn), "r_sin": lay(sinn),
        "r_mask": mask.astype(f32).reshape(4, 4, RL, RL).transpose(2, 0, 1, 3),
        "r_qg": (gamma[head][None, :] ** at[:, None] * HD ** -0.5).astype(f32),
        "r_kg": (gamma[head][None, :] ** (RL - at)[:, None]).astype(f32),
        "r_diag": (head[:, None] == head[None, :]).astype(f32),
    })
    return {k: np.ascontiguousarray(x) for k, x in o.items()}


def build(nc, arrays, upto=99):
    I = {}
    for name, x in arrays.items():
        I[name] = nc.dram_tensor(f"in_{name}", x.shape, mybir.dt.from_np(x.dtype), kind="ExternalInput").ap()
    out = nc.dram_tensor("out_x", (BATCH, SEQ, D), F32, kind="ExternalOutput").ap()
    block_kernel(nc, I, out, upto)


def kernel(**inputs):
    import concourse.bacc as bacc
    from concourse.bass_utils import run_bass_kernel_spmd

    arrays = _arrange(inputs)
    nc = bacc.Bacc("TRN2", target_bir_lowering=False, num_devices=1)
    build(nc, arrays)
    r = run_bass_kernel_spmd(nc, [{f"in_{k}": v for k, v in arrays.items()}], core_ids=[0])
    return r.results[0]["out_x"]
```

```python
from contextlib import ExitStack

import concourse.bass as bass
from concourse import mybir

F32 = mybir.dt.float32
BF16 = mybir.dt.bfloat16
ALU = mybir.AluOpType
ACT = mybir.ActivationFunctionType
AX = mybir.AxisListType

P = 128
D = 128
BATCH, SEQ = 4, 1024
TOKENS = BATCH * SEQ
TILES = TOKENS // P
CH = 512
CT = CH // P
CHUNKS = TOKENS // CH
HEADS = 16
HD = D // HEADS
LN_EPS = 1e-5

JH = 4
GROUPS = BATCH * HEADS // JH
QROWS = 6 * HD
AROWS = QROWS + 3
KT = SEQ // P
VW = 32

U32 = mybir.dt.uint32
EXPERTS = 8
FF = 512
FT = FF // P
CAP = 1280
SLOTS = EXPERTS * CAP
MARKS = {2: 1.0, 4: 16385.0}
ROW = 136
PARTS = (4, 4, 2)
FLOOR = -103.0
GATE_EPS = 1.1920929e-07
SHARED = 0.1

RL = 128
GN_EPS = 1e-5


class Count:

    def __init__(self, eng, sem, turn=0, each=0):
        self.eng, self.sem, self.turn, self.each, self.n = eng, sem, turn, each, 0

    def mark(self, ins, by=1):
        ins.then_inc(self.sem, by)
        self.n += by

    def settle(self, eng=None):
        (eng or self.eng).wait_ge(self.sem, self.turn * self.each + self.n)


class Buffers:
    pass


def ring(stack, make, name, n, shape, dt):
    return [stack.enter_context(make(f"{name}{i}", shape, dt)) for i in range(n)]


def token_stats(nc, T, t):
    return nc.vector.bn_stats(T.bn[:, t, :], T.X[:, t, :])


def load_stage(nc, T, I, S):
    with ExitStack() as st:
        loaded = st.enter_context(nc.semaphore("ld_loaded"))
        weights = st.enter_context(nc.semaphore("ld_weights"))
        blank = st.enter_context(nc.semaphore("ld_blank"))
        zeroed = st.enter_context(nc.semaphore("ld_zeroed"))
        x_loaded = [st.enter_context(nc.semaphore(f"ld_x{c}")) for c in range(CHUNKS // 2)]
        block = st.enter_context(nc.Block())
        xt = I["x"].rearrange("b (t p) d -> p (b t) d", p=P)

        @block.sync
        def _(sp):
            for c in range(CHUNKS):
                sp.dma_start(T.X[:, CT * c:CT * (c + 1), :], xt[:, CT * c:CT * (c + 1), :]).then_inc(x_loaded[c // 2], 16)
            sp.dma_start(T.upper[:, :], I["upper"]).then_inc(loaded, 16)
            sp.dma_start(T.rank[:, :], I["rank"].partition_broadcast(P)).then_inc(loaded, 16)
            sp.dma_start(T.bo[:, :], I["b_out"].partition_broadcast(P)).then_inc(loaded, 16)
            sp.dma_start(T.sb2[:, :], I["b2"][EXPERTS, :].partition_broadcast(P)).then_inc(loaded, 16)
            sp.dma_start(T.places[:, :], I["places"]).then_inc(loaded, 16)
            sp.dma_start(T.token[:, :], I["token"]).then_inc(loaded, 16)
            sp.dma_start(T.slot[:, :], I["slot"]).then_inc(loaded, 16)
            sp.wait_ge(zeroed, 1)
            for e in range(EXPERTS + 1):
                sp.dma_start(S.xe[e * CAP:(e + 1) * CAP, :].rearrange("(p t) d -> p (t d)", p=P),
                             T.spare[0][:, 0:CAP // P * ROW]).then_inc(T.filled, 16)
            sp.wait_ge(loaded, 16 * 7)

        @block.scalar
        def _(act):
            act.dma_start(T.sw1[:, :], I["w1"][EXPERTS, :, :]).then_inc(weights, 16)
            act.dma_start(T.sw2[:, :, :], I["w2"][EXPERTS, :, :].rearrange("(c p) h -> p c h", p=P)).then_inc(weights, 16)
            act.dma_start(T.rw[:, :], I["rw"]).then_inc(weights, 16)
            act.dma_start(T.sb1[:, :], I["b1"][EXPERTS, :, :]).then_inc(weights, 16)
            act.wait_ge(weights, 16 * 4)

        @block.vector
        def _(dve):
            dve.memset(T.spare[0][:, :], 0.0).then_inc(zeroed, 1)
            for c in range(CHUNKS // 2):
                dve.wait_ge(x_loaded[c], 32)
                for t in range(2 * CT * c, 2 * CT * (c + 1)):
                    token_stats(nc, T, t)

        @block.gpsimd
        def _(pool):
            pool.memset(T.ident[:, :], 0.0).then_inc(blank, 1)
            pool.memset(T.ones[:, :], 1.0)
            pool.memset(T.spare[1][:, :], 0.0)
            for n in ("X", "mv"):
                pool.memset(T.pad[n][:, TILES:, :], 0.0)
            for n in ("rs", "ri"):
                pool.memset(T.pad[n][:, TILES:], 0.0)
            pool.wait_ge(blank, 1)
            pool.affine_select(out=T.ident[:, :], in_=T.ident[:, :], compare_op=ALU.not_equal, fill=1.0,
                               base=0, pattern=[[-1, P]], channel_multiplier=1).then_inc(blank, 1)


def norm_stage(nc, T, tag, turn=True, logits=None):
    with ExitStack() as st:
        sem = lambda n: st.enter_context(nc.semaphore(f"{tag}_{n}"))
        spread, root, xh_ready, turned, copied = map(
            sem, ("spread", "root", "xh_ready", "turned", "copied"))
        pst = ring(st, nc.psum_tensor, f"{tag}_ps", 2, [P, CH], F32)
        block = st.enter_context(nc.Block())

        @block.vector
        def _(dve):
            mean, var, dif, sq = T.mv[:, :, 0], T.mv[:, :, 1], T.sd[:, :], T.rs[:, :]
            nc.vector.tensor_tensor(mean, T.bn[:, :, 1], T.bn[:, :, 4], ALU.add).then_inc(spread, 1)
            nc.vector.tensor_tensor(dif, T.bn[:, :, 1], T.bn[:, :, 4], ALU.subtract).then_inc(spread, 1)
            nc.vector.tensor_tensor(var, T.bn[:, :, 2], T.bn[:, :, 5], ALU.add).then_inc(spread, 1)
            dve.wait_ge(spread, 3)
            nc.vector.tensor_scalar(mean, mean, 0.5, None, ALU.mult).then_inc(spread, 1)
            nc.vector.tensor_tensor(sq, dif, dif, ALU.mult).then_inc(spread, 1)
            nc.vector.tensor_scalar(var, var, 1.0 / D, None, ALU.mult).then_inc(spread, 1)
            dve.wait_ge(spread, 6)
            nc.vector.scalar_tensor_tensor(out=var, in0=sq, scalar=0.25, in1=var, op0=ALU.mult, op1=ALU.add).then_inc(spread, 1)
            dve.wait_ge(spread, 7)
            nc.vector.tensor_scalar(T.sd[:, :], var, LN_EPS, None, ALU.add).then_inc(spread, 1)
            dve.wait_ge(root, 1)
            nc.vector.reciprocal(T.rs[:, :], T.sd[:, :]).then_inc(root, 1)
            dve.wait_ge(root, 2)
            if not turn:
                nc.vector.tensor_tensor(T.ri[:, :], T.ri[:, :], T.rs[:, :], ALU.mult).then_inc(root, 1)
                dve.wait_ge(root, 3)
                nc.vector.tensor_scalar(T.ri[:, :], T.ri[:, :], 1e-8, None, ALU.max).then_inc(root, 1)
                dve.wait_ge(root, 4)
                nc.vector.reciprocal(T.ri[:, :], T.ri[:, :]).then_inc(root, 1)
                dve.wait_ge(root, 5)
                nc.vector.tensor_tensor(T.ri[:, :], T.ri[:, :], T.rs[:, :], ALU.mult)
                return
            with dve.Fori(0, CHUNKS // 2) as i:
                for a in range(2):
                    for k in range(CT):
                        t = i * (2 * CT) + (a * CT + k)
                        ins = nc.vector.tensor_scalar(T.XH[:, bass.ds(t, 1), :].rearrange("p t d -> p (t d)"), T.X[:, bass.ds(t, 1), :].rearrange("p t d -> p (t d)"),
                                                      T.mv[:, bass.ds(t, 1), 0:1].rearrange("p t s -> p (t s)"),
                                                      T.rs[:, bass.ds(t, 1)], ALU.subtract, ALU.mult)
                    ins.then_inc(xh_ready, 1)

        @block.tensor
        def _(pe):
            if not turn:
                return

            def route(c):
                pe.wait_ge(copied, c + 3)
                for t in range(c * CT, (c + 1) * CT):
                    nc.tensor.matmul(logits[:, t * EXPERTS:(t + 1) * EXPERTS], T.XT[:, t * P:(t + 1) * P], T.rw[:, :],
                                     start=True, stop=True, skip_group_check=True)

            for c in range(CHUNKS):
                pe.wait_ge(xh_ready, c + 1)
                pe.wait_ge(copied, c + 1)
                for k in range(CT):
                    ins = nc.tensor.transpose(pst[c % 2][:, k * P:(k + 1) * P], T.XH[:, c * CT + k, :], T.ident[:, :])
                ins.then_inc(turned, 1)
                if logits is not None and c:
                    route(c - 1)
            if logits is not None:
                route(CHUNKS - 1)

        @block.scalar
        def _(act):
            act.sem_inc(copied, 2)
            act.wait_ge(spread, 8)
            if not turn:
                nc.scalar.activation(T.ri[:, :], T.mv[:, :, 1], ACT.Sqrt)
            nc.scalar.activation(T.sd[:, :], T.sd[:, :], ACT.Sqrt).then_inc(root, 1)
            if not turn:
                return
            with act.Fori(0, CHUNKS // 2) as i:
                for a in range(2):
                    act.wait_ge(turned, 2 * i + a + 1)
                    nc.scalar.copy(T.XT[:, bass.ds(i * (2 * CH) + a * CH, CH)], pst[a][:, :]).then_inc(copied, 1)


def qkv_stage(nc, T, I, S):
    with ExitStack() as st:
        sem = lambda n: st.enter_context(nc.semaphore(f"qkv_{n}"))
        weights, projected, evacuated, vturned, vkept, split = map(
            sem, ("weights", "projected", "evacuated", "vturned", "vkept", "split"))
        stored = [sem("stored0"), sem("stored1")]
        chain = sem("chain")
        wqkv = st.enter_context(nc.sbuf_tensor("qkv_w", [P, 3, D], F32))
        bqkv = st.enter_context(nc.sbuf_tensor("qkv_b", [P, 3], F32))
        zero = T.spare[1][0:QROWS, :].bitcast(BF16).rearrange("r (g t) -> r g t", t=SEQ)
        QK = ring(st, nc.sbuf_tensor, "qkv_qk", 2, [P, 2, CH], F32)
        R = ring(st, nc.sbuf_tensor, "qkv_r", 2, [P, 2, CH], F32)
        VT = ring(st, nc.sbuf_tensor, "qkv_vt", 2, [P, CH], F32)
        part = ring(st, nc.sbuf_tensor, "qkv_part", 2, [P, 3, 2, CH], BF16)
        ps = [ring(st, nc.psum_tensor, f"qkv_ps{w}", 2, [P, CH], F32) for w in range(3)]
        pvt = ring(st, nc.psum_tensor, "qkv_pvt", 2, [P, CH], F32)
        block = st.enter_context(nc.Block())
        PRODUCTS = ((0, 3, 0), (3, 5, 1), (5, 6, 2))
        sq = S.q.rearrange("g j (d r) t -> (g j d) r t", d=HD)
        sk = S.k.rearrange("g j (d r) t -> (g j d) r t", d=HD)

        @block.sync
        def _(sp):
            sp.dma_start(wqkv[:, :, :], I["w_qkv"]).then_inc(weights, 16)
            sp.dma_start(bqkv[:, :], I["b_qkv"]).then_inc(weights, 16)
            for s in (S.q, S.k):
                sp.dma_start(s[GROUPS:GROUPS + 2, :, :, :].rearrange("g j r t -> r (g j) t"), zero[:, :, :]).then_inc(T.filled, 16)
            for a in range(2):
                sp.sem_inc(stored[a], 16)
            with sp.Fori(0, BATCH) as b:
                for a in range(2):
                    sp.wait_ge(split, 2 * b + a + 1)
                    rows, cols = bass.ds(b * P, P), slice(a * CH, (a + 1) * CH)
                    for r0, r1, n in PRODUCTS:
                        sp.dma_start(sq[rows, r0:r1, cols],
                                     part[a][:, n, 0, :].unsqueeze(1).to_broadcast([P, r1 - r0, CH])).then_inc(stored[a], 16)
                        sp.dma_start(sk[rows, r0:r1, cols], part[a][:, 0:r1 - r0, 1, :]).then_inc(stored[a], 16)
            sp.wait_ge(weights, 32)
            sp.wait_ge(T.filled, 16 * (EXPERTS + 3))
            for a in range(2):
                sp.wait_ge(stored[a], BATCH * 6 * 16 + 16)

        @block.tensor
        def _(pe):
            pe.wait_ge(weights, 32)
            with pe.Fori(0, BATCH) as b:
                for a in range(2):
                    c = 2 * b + a
                    pe.wait_ge(evacuated, 3 * c + 3)
                    for w in (2, 0, 1):
                        nc.tensor.matmul(ps[w][a][:, :], wqkv[:, w, :], T.XT[:, bass.ds(b * SEQ + a * CH, CH)],
                                         start=True, stop=True).then_inc(projected, 1)
                    pe.wait_ge(evacuated, 3 * c + 7)
                    pe.wait_ge(vkept, c + 1)
                    for k in range(CT):
                        ins = nc.tensor.transpose(pvt[a][:, k * P:(k + 1) * P], VT[a][:, k * P:(k + 1) * P], T.ident[:, :])
                    ins.then_inc(vturned, 1)

        @block.scalar
        def _(act):
            act.sem_inc(evacuated, 6)
            act.sem_inc(vkept, 2)
            act.wait_ge(weights, 32)
            with act.Fori(0, BATCH) as b:
                for a in range(2):
                    c = 2 * b + a
                    act.wait_ge(projected, 3 * c + 1)
                    nc.scalar.activation(VT[a][:, :], ps[2][a][:, :], ACT.Identity, bias=bqkv[:, 2:3]).then_inc(evacuated, 1)
                    act.wait_ge(chain, 6 * b + 3 * a + 2)
                    for w in range(2):
                        act.wait_ge(projected, 3 * c + 2 + w)
                        nc.scalar.activation(QK[a][:, w, :], ps[w][a][:, :], ACT.Identity,
                                             bias=bqkv[:, w:w + 1]).then_inc(evacuated, 1)
                    act.wait_ge(vturned, c + 1)
                    nc.scalar.copy(T.V[:, bass.ds(b * 4, 4), CT * a:CT * (a + 1), :],
                                   pvt[a][:, :].rearrange("p (t g e) -> p g t e", t=CT, g=4)).then_inc(vkept, 1)

        @block.vector
        def _(dve):
            dve.sem_inc(chain, 6)
            with dve.Fori(0, BATCH) as b:
                link = Count(dve, chain, b, 6)
                link.n = 6
                for a in range(2):
                    dve.wait_ge(evacuated, 6 * b + 3 * a + 9)
                    dve.wait_ge(stored[a], 6 * 16 * b + 16)
                    q, r, p = QK[a][:, :, :], R[a][:, :, :], part[a]
                    link.mark(nc.vector.tensor_copy(p[:, 0, :, :], q))
                    link.settle()
                    link.mark(nc.vector.tensor_tensor(r, q, p[:, 0, :, :], ALU.subtract))
                    link.settle()
                    link.mark(nc.vector.tensor_copy(p[:, 1, :, :], r))
                    link.settle()
                    nc.vector.tensor_tensor(p[:, 2, :, :], r, p[:, 1, :, :], ALU.subtract).then_inc(split, 1)
            for e in range(2):
                dve.memset(T.XT[:, e * (TOKENS // 2):(e + 1) * (TOKENS // 2)], 0.0)

        @block.gpsimd
        def _(pool):
            pool.memset(T.V[:, GROUPS, :, :], 0.0)
            for e in range(2):
                pool.memset(T.hk[e][:, :, :].bitcast(F32), 0.0)
                pool.memset(T.eq[e][:, :, :].bitcast(F32), 0.0)
                pool.memset(T.ek[e][:, :, :], 1.0)
                pool.memset(T.vst[e][:, :, :, :], 1.0)
            with pool.Fori(0, TILES // CT) as i:
                xs = T.X[:, bass.ds(i * CT, CT), :]
                pool.tensor_tensor(xs, xs, T.bo[:, :].unsqueeze(1).to_broadcast([P, CT, D]), ALU.add)


def attention_stage(nc, T, S):
    STEPS = 16
    EXPS = 2 * STEPS
    HIGHS = JH * KT * 2
    HALF = HIGHS // 2
    with ExitStack() as st:
        sem = lambda n: st.enter_context(nc.semaphore(f"at_{n}"))
        (scored, exped, multiplied, o_kept, high_scored, high_kept, low_ready, low_turned, low_split,
         v_staged, chain) = map(sem, (
             "scored", "exped", "multiplied", "o_kept", "high_scored", "high_kept", "low_ready",
             "low_turned", "low_split", "v_staged", "chain"))
        high_loaded = [sem("high_loaded0"), sem("high_loaded1")]
        loaded = [sem("loaded0"), sem("loaded1")]
        rows_stored, rows_loaded = sem("rows_stored"), [sem("rows_loaded0"), sem("rows_loaded1")]
        o_stored = [sem("o_stored0"), sem("o_stored1")]
        free = T.XT[:, :].bitcast(BF16)
        hq = [free[:, e * JH * SEQ:(e + 1) * JH * SEQ].rearrange("p (j t) -> p j t", j=JH) for e in range(2)]
        hk, eq, ek, vst = T.hk, T.eq, T.ek, T.vst
        prob = ring(st, nc.sbuf_tensor, "at_prob", 2, [P, JH, 2, CH], F32)
        prob += [T.spare[e][:, :].rearrange("p (j k q) -> p j k q", j=JH, k=2) for e in range(2)]
        osb = ring(st, nc.sbuf_tensor, "at_o", 2, [P, CH], F32)
        hmax = ring(st, nc.sbuf_tensor, "at_hmax", 2, [P, JH * KT, 2], F32)
        low = ring(st, nc.sbuf_tensor, "at_low", 2, [P, JH * KT], F32)
        rest = ring(st, nc.sbuf_tensor, "at_rest", 2, [JH * KT, P], F32)
        lparts = ring(st, nc.sbuf_tensor, "at_lparts", 2, [JH * KT, 3, P], BF16)
        ps = ring(st, nc.psum_tensor, "at_ps", 2, [P, 2, CH], F32)
        pso = st.enter_context(nc.psum_tensor("at_pso", [P, CH], F32))
        psh = ring(st, nc.psum_tensor, "at_psh", 3, [P, CH], F32)
        block = st.enter_context(nc.Block())

        def high_banks(uses):
            return [u % 3 for u in range(uses - 1)] + [1]

        FIRST_BANKS = high_banks(HIGHS + HALF + 1)
        TURN_BANKS = high_banks(2 * (HIGHS + 1))

        def high_units(first, last):
            for n in range(first, last):
                yield n % JH, n // (2 * JH), n // JH % 2

        @block.sync
        def _(sp):
            def load_high(g, e):
                for s, d in ((S.q, hq[e]), (S.k, hk[e])):
                    for h in range(2):
                        sp.dma_start(d[64 * h:64 * h + QROWS, h:JH:2, :] if d is hq[e] else d[64 * h:64 * h + QROWS, :, :],
                                     s[bass.ds(g, 1), h:JH:2, 0:QROWS, :].rearrange("g j r t -> (g r) j t")
                                     ).then_inc(high_loaded[e], 16)

            def load_group(g, e):
                for s, d in ((S.q, eq[e]), (S.k, ek[e])):
                    for h in range(2):
                        sp.dma_start(d[64 * h:64 * h + QROWS, h:JH:2, :] if d is eq[e] else d[64 * h:64 * h + QROWS, :, :],
                                     s[bass.ds(g, 1), h:JH:2, 0:QROWS, :].rearrange("g j r t -> (g r) j t")
                                     ).then_inc(loaded[e], 16)

            def load_rows(g, e, nth):
                sp.wait_ge(low_split, nth)
                for j in range(JH):
                    sp.dma_start(S.low[bass.ds(g, 1), j, :, :].rearrange("g r (t c) -> (g t) r c", c=P),
                                 lparts[e][KT * j:KT * (j + 1), :, :]).then_inc(rows_stored, 16)
                sp.wait_ge(rows_stored, nth * JH * 16)
                for h in range(2):
                    sp.dma_start(eq[e][64 * h + QROWS:64 * h + AROWS, h:JH:2, :],
                                 S.low[bass.ds(g, 1), h:JH:2, :, :].rearrange("g j r t -> (g r) j t")
                                 ).then_inc(rows_loaded[e], 16)

            def store_o(g, qc):
                for j in range(JH):
                    sp.dma_start(S.o[bass.ds(g, 1), j, :, qc * CH:(qc + 1) * CH].rearrange("g r t -> (g r) t"),
                                 osb[qc][VW * j:VW * j + HD + 1, :]).then_inc(o_stored[qc], 16)

            for qc in range(2):
                sp.sem_inc(o_stored[qc], 16)
            load_high(0, 0)
            load_high(1, 1)
            load_group(0, 0)
            load_rows(0, 0, 1)
            with sp.Fori(0, GROUPS // 2) as turn:
                g0 = turn * 2
                for a in range(2):
                    g = g0 + a
                    sp.wait_ge(high_kept, HIGHS * g + HIGHS)
                    load_high(g + 2, a)
                    sp.wait_ge(exped, EXPS * g + 2)
                    load_group(g + 1, 1 - a)
                    sp.wait_ge(o_kept, 2 * g + 3)
                    store_o(g, 1)
                    load_rows(g + 1, 1 - a, g + 2)
                    sp.wait_ge(o_kept, 2 * g + 4)
                    store_o(g + 1, 0)
            sp.wait_ge(o_kept, 2 * GROUPS + 3)
            store_o(GROUPS, 1)
            for qc in range(2):
                sp.wait_ge(o_stored[qc], JH * 16 * (GROUPS + qc) + 16)
            for e in range(2):
                sp.wait_ge(high_loaded[e], 64 * (GROUPS // 2 + 1))
                sp.wait_ge(loaded[e], 64 * (GROUPS // 2 + 1 - e))
                sp.wait_ge(rows_loaded[e], 32 * (GROUPS // 2 + 1 - e))

        @block.gpsimd
        def _(pool):
            def stage_v(g, e):
                pool.tensor_copy(vst[e][:, :, :, 0:HD],
                                 T.V[:, bass.ds(g, 1), :, :].rearrange("p g t (j e) -> p (g t) j e", e=HD)
                                 ).then_inc(v_staged, 1)

            stage_v(0, 0)
            with pool.Fori(0, GROUPS // 2) as turn:
                g0 = turn * 2
                for a in range(2):
                    g = g0 + a
                    pool.wait_ge(multiplied, 4 + 16 * g + 3)
                    stage_v(g + 1, 1 - a)

        @block.tensor
        def _(pe):
            holder = [None] * 3
            banks, base, index = [], [0], [0]

            def free_bank():
                bank = banks.pop(0)
                kind, nth = holder[bank] or (None, 0)
                if kind == "high":
                    pe.wait_ge(high_kept, base[0] + nth + 1)
                if kind == "low":
                    pe.wait_ge(chain, nth)
                return bank

            def high(e, unit):
                j, qt, kh = unit
                bank = free_bank()
                nc.tensor.matmul(psh[bank][:, :], hq[e][:, j, qt * P:(qt + 1) * P],
                                 hk[e][:, j // 2, kh * CH:(kh + 1) * CH],
                                 start=True, stop=True).then_inc(high_scored, 1)
                holder[bank] = ("high", index[0])
                index[0] += 1

            def turn_low(e, nth):
                bank = free_bank()
                pe.wait_ge(low_ready, nth)
                nc.tensor.transpose(psh[bank][0:JH * KT, 0:P], low[e][:, :], T.ident[:, :]).then_inc(low_turned, 1)
                holder[bank] = ("low", 3 * nth - 1)

            def score(e, n, i, k):
                qc, kp, jp = n // 8, n % 8 // 2, n % 2
                ins = nc.tensor.matmul(ps[i][:, k, :], ek[e][:, jp, (2 * kp + k) * P:(2 * kp + k + 1) * P],
                                       eq[e][:, 2 * jp + i, qc * CH:(qc + 1) * CH], start=True, stop=True)
                if k == 1:
                    ins.then_inc(scored, 1)

            def multiply(e, c, k):
                kt = 2 * (c % 4) + k
                for j in range(JH):
                    ins = nc.tensor.matmul(pso[VW * j:VW * (j + 1), :], vst[e][:, kt, j, :],
                                           prob[c % 4][:, j, k, :], start=(kt == 0), stop=(kt == KT - 1))
                ins.then_inc(multiplied, 1)

            pe.sem_inc(multiplied, 4)
            for j in range(JH):
                nc.tensor.matmul(pso[VW * j:VW * (j + 1), :], vst[1][:, 0, j, :], prob[3][:, j, 0, :],
                                 start=True, stop=False)
            banks += FIRST_BANKS
            pe.wait_ge(high_loaded[0], 64)
            for n, unit in enumerate(high_units(0, HIGHS)):
                high(0, unit)
            pe.wait_ge(high_loaded[1], 64)
            for n, unit in enumerate(high_units(0, HALF)):
                high(1, unit)
                if n == 3:
                    turn_low(0, 1)
            start = HIGHS + HALF
            banks += TURN_BANKS
            index[0] = 0
            holder[:] = [("high", -4), ("high", -1), ("high", -2)]
            with pe.Fori(0, GROUPS // 2) as turn:
                g0 = turn * 2
                for a in range(2):
                    g, e = g0 + a, a
                    todo = [(1 - e, u) for u in high_units(HALF, HIGHS)] + [(e, u) for u in high_units(0, HALF)]
                    base[0] = start + HIGHS * g0
                    for n in range(STEPS):
                        if n == 0:
                            pe.wait_ge(loaded[e], g0 * 32 + 64)
                            pe.wait_ge(rows_loaded[e], g0 * 16 + 32)
                        if n == STEPS // 2:
                            pe.wait_ge(high_loaded[e], g0 * 32 + 128)
                        for i in range(2):
                            pe.wait_ge(exped, EXPS * g + 2 * n + i + 1)
                            for k in range(2):
                                score(e, n, i, k)
                                high(*todo[4 * n + 2 * i + k])
                            if i == 0:
                                if n == 3:
                                    pe.wait_ge(v_staged, g + 1)
                                if n in (3, 11):
                                    pe.wait_ge(o_kept, 2 * g + 3 + (n == 11))
                                if n < 3:
                                    multiply(1 - e, (6, 7, 7)[n], (1, 0, 1)[n])
                                else:
                                    multiply(e, (n - 3) // 2, (n - 3) % 2)
                        if n == STEPS // 2:
                            turn_low(1 - e, g + 2)
            pe.wait_ge(exped, 2 + EXPS * GROUPS)
            for c, k in ((6, 1), (7, 0), (7, 1)):
                multiply(1, c, k)

        @block.scalar
        def _(act):
            act.sem_inc(exped, 2)
            act.sem_inc(o_kept, 2)

            def keep(qc, before, done):
                act.wait_ge(multiplied, done)
                act.wait_ge(o_stored[qc], before + 16)
                nc.scalar.copy(osb[qc][:, :], pso[:, :]).then_inc(o_kept, 1)

            with act.Fori(0, GROUPS // 2) as turn:
                g0 = turn * 2
                for a in range(2):
                    g = g0 + a
                    for n in range(STEPS):
                        c = n // 2
                        if n % 2 == 0:
                            act.wait_ge(multiplied, 16 * g + 2 * c + 1)
                        for i in range(2):
                            act.wait_ge(scored, EXPS * g + 2 * n + i + 1)
                            nc.scalar.activation(prob[c % 4][:, 2 * (n % 2) + i, :, :], ps[i][:, :, :], ACT.Exp,
                                                 scale=HD ** -0.5).then_inc(exped, 1)
                            if n == 2 and i == 0:
                                keep(1, g * (JH * 16), 16 * g + 7)
                            if n == 10 and i == 0:
                                keep(0, g * (JH * 16), 16 * g + 15)
            keep(1, GROUPS * JH * 16, 16 * GROUPS + 7)

        @block.vector
        def _(dve):
            banks = []

            def take(e, unit, nth):
                j, qt, kh = unit
                dve.wait_ge(high_scored, nth)
                nc.vector.tensor_reduce(hmax[e][:, KT * j + qt, kh:kh + 1], psh[banks.pop(0)][:, :], AX.X,
                                        ALU.max).then_inc(high_kept, 1)

            def lowest(e, kept):
                dve.wait_ge(high_kept, kept)
                nc.vector.tensor_reduce(low[e][:, :], hmax[e][:, :, :], AX.X, ALU.max, negate=True).then_inc(low_ready, 1)

            def split_low(e, nth, links, rows):
                bank = psh[banks.pop(0)][0:JH * KT, 0:P]
                dve.wait_ge(low_turned, nth)
                if rows is not None:
                    dve.wait_ge(rows_stored, rows)
                nc.vector.tensor_copy(lparts[e][:, 0, :], bank).then_inc(chain, 1)
                dve.wait_ge(chain, links + 1)
                nc.vector.tensor_tensor(rest[e][:, :], bank, lparts[e][:, 0, :], ALU.subtract).then_inc(chain, 1)
                dve.wait_ge(chain, links + 2)
                nc.vector.tensor_copy(lparts[e][:, 1, :], rest[e][:, :]).then_inc(chain, 1)
                dve.wait_ge(chain, links + 3)
                nc.vector.tensor_tensor(lparts[e][:, 2, :], rest[e][:, :], lparts[e][:, 1, :],
                                        ALU.subtract).then_inc(low_split, 1)

            banks += FIRST_BANKS
            for n, unit in enumerate(high_units(0, HIGHS)):
                take(0, unit, n + 1)
            lowest(0, HIGHS)
            for n, unit in enumerate(high_units(0, HALF)):
                take(1, unit, HIGHS + n + 1)
                if n == 3:
                    split_low(0, 1, 0, None)
            start = HIGHS + HALF
            banks += TURN_BANKS
            with dve.Fori(0, GROUPS // 2) as turn:
                g0 = turn * 2
                for a in range(2):
                    g, e = g0 + a, a
                    todo = [(1 - e, u) for u in high_units(HALF, HIGHS)] + [(e, u) for u in high_units(0, HALF)]
                    for m in range(HIGHS):
                        if m == HALF:
                            lowest(1 - e, start + HIGHS * g + HALF)
                        take(*todo[m], start + HIGHS * g + m + 1)
                        if m == HALF + 3:
                            split_low(1 - e, g + 2, 3 * g + 3, g * (JH * 16) + JH * 16)


def output_stage(nc, T, I, S):
    with ExitStack() as st:
        sem = lambda n: st.enter_context(nc.semaphore(f"out_{n}"))
        weights, sums, o_loaded, inverted, stored, divided, projected, added = map(
            sem, ("weights", "sums", "o_loaded", "inverted", "stored", "divided", "projected", "added"))
        spread = [sem(f"spread{b}") for b in range(BATCH)]
        wo, total = (st.enter_context(nc.sbuf_tensor(f"out_{n}", shape, F32)) for n, shape in (("w", [P, D]), ("total", [P, CH])))
        O, INV = T.spare
        ps = ring(st, nc.psum_tensor, "out_ps", 4, [P, CH], F32)
        block = st.enter_context(nc.Block())
        heads = S.o[1:GROUPS + 1, :, :, :].rearrange("g j r t -> (g j) r t")

        @block.sync
        def _(sp):
            sp.dma_start(total[:, :], heads[:, HD, :].rearrange("h (a t) -> h a t", a=2)).then_inc(sums, 16)
            sp.dma_start(wo[:, :], I["w_out"]).then_inc(weights, 16)
            sp.wait_ge(inverted, 1)
            sp.dma_start(S.inv.rearrange("h (a t) -> h a t", a=2), total[:, :]).then_inc(stored, 16)
            sp.wait_ge(stored, 16)
            for b in range(BATCH):
                sp.dma_start(INV[:, b * SEQ:(b + 1) * SEQ],
                             S.inv[b * HEADS:(b + 1) * HEADS, :].unsqueeze(1).to_broadcast([HEADS, HD, SEQ])).then_inc(spread[b], 16)

        @block.scalar
        def _(act):
            for b in range(BATCH):
                act.dma_start(O[:, b * SEQ:(b + 1) * SEQ], heads[b * HEADS:(b + 1) * HEADS, 0:HD, :]).then_inc(o_loaded, 16)
            act.wait_ge(o_loaded, 16 * BATCH)

        @block.vector
        def _(dve):
            dve.wait_ge(sums, 16)
            nc.vector.reciprocal(total[:, :], total[:, :]).then_inc(inverted, 1)

            def add(c):
                dve.wait_ge(projected, c + 1)
                xs = T.X[:, c * CT:(c + 1) * CT, :]
                nc.vector.tensor_tensor(xs, ps[c % 4][:, :].rearrange("p (t d) -> p t d", d=D), xs, ALU.add).then_inc(added, 1)
                dve.wait_ge(added, c + 1)
                for t in range(c * CT, (c + 1) * CT):
                    token_stats(nc, T, t)

            dve.wait_ge(o_loaded, 16 * BATCH)
            for c in range(CHUNKS):
                dve.wait_ge(spread[c // 2], 16)
                cols = slice(c * CH, (c + 1) * CH)
                nc.vector.tensor_tensor(O[:, cols], O[:, cols], INV[:, cols], ALU.mult).then_inc(divided, 1)
                if c >= 2:
                    add(c - 2)
            add(CHUNKS - 2)
            add(CHUNKS - 1)

        @block.tensor
        def _(pe):
            pe.wait_ge(weights, 16)
            for c in range(CHUNKS):
                pe.wait_ge(divided, c + 1)
                if c >= 4:
                    pe.wait_ge(added, c - 3)
                for t in range(c * CT, (c + 1) * CT):
                    ins = nc.tensor.matmul(ps[c % 4][:, t % CT * D:(t % CT + 1) * D], O[:, t * P:(t + 1) * P], wo[:, :],
                                           start=True, stop=True, skip_group_check=True)
                ins.then_inc(projected, 1)


def gate_stage(nc, T, logits, mark):
    N, E = TILES, EXPERTS
    with ExitStack() as st:
        gate_no[0] += 1
        tag = f"gate{gate_no[0]}"
        sem = lambda n: st.enter_context(nc.semaphore(f"{tag}_{n}"))
        shifted, exped, masked, placed, chain, zeroed = map(sem, ("shifted", "exped", "masked", "placed", "chain", "zeroed"))
        sb = lambda n, shape: st.enter_context(nc.sbuf_tensor(f"{tag}_{n}", shape, F32))
        L, G, K2, EQ = (sb(n, [P, N, E]) for n in ("l", "g", "k2", "eq"))
        M = sb("m", [P, N, 2, E])
        KEEP = sb("keep", [P, N, 2, E])
        A, POS = (sb(n, [P, N, 2, E]) for n in ("a", "pos"))
        SUMS = ring(st, nc.sbuf_tensor, f"{tag}_sums", 2, [P, N // 2 + N, 2 * E], F32)
        top, tot, den = sb("top", [P, N]), sb("tot", [P, N]), sb("den", [P, N])
        cnt = sb("cnt", [P, E])
        place = sb("place", [P, N, 2])
        psa, psb = (st.enter_context(nc.psum_tensor(f"{tag}_{n}", [P, CH], F32)) for n in ("psa", "psb"))
        block = st.enter_context(nc.Block())

        @block.tensor
        def _(pe):
            pe.wait_ge(masked, 1)
            m = M[:, :, :, :].rearrange("p t k e -> p (t k e)")
            nc.tensor.matmul(psa[:, :], T.upper[:, :], m, start=True, stop=True)
            nc.tensor.matmul(psb[:, :], T.ones[:, :], m, start=True, stop=True).then_inc(placed, 1)

        @block.scalar
        def _(act):
            act.wait_ge(shifted, 1)
            nc.scalar.activation(G[:, :, :], L[:, :, :], ACT.Exp).then_inc(exped, 1)

        @block.vector
        def _(dve):
            link = Count(dve, chain)
            wide = lambda a: a.unsqueeze(2).to_broadcast([P, N, E])
            rank = T.rank[:, :].unsqueeze(1).to_broadcast([P, N, E])

            def step(ins):
                link.mark(ins)
                link.settle()

            def first_best(out, key, best):
                step(nc.vector.tensor_tensor(EQ[:, :, :], key, wide(best), ALU.is_equal))
                step(nc.vector.tensor_tensor(EQ[:, :, :], EQ[:, :, :], rank, ALU.mult))
                step(nc.vector.tensor_reduce(top[:, :], EQ[:, :, :], AX.X, ALU.max))
                step(nc.vector.tensor_tensor(out, EQ[:, :, :], wide(top[:, :]), ALU.is_equal))

            lg = logits[:, 0:N * E].rearrange("p (t e) -> p t e", e=E)
            step(nc.vector.tensor_reduce(top[:, :], lg, AX.X, ALU.max))
            nc.vector.tensor_tensor(L[:, :, :], lg, wide(top[:, :]), ALU.subtract).then_inc(shifted, 1)
            dve.wait_ge(shifted, 1)
            step(nc.vector.memset(den[:, :], 0.0))
            first_best(M[:, :, 0, :], L[:, :, :], den[:, :])
            step(nc.vector.tensor_scalar(K2[:, :, :], L[:, :, :], FLOOR, None, ALU.max))
            step(nc.vector.tensor_scalar(EQ[:, :, :], M[:, :, 0, :], FLOOR, None, ALU.mult))
            step(nc.vector.tensor_tensor(K2[:, :, :], K2[:, :, :], EQ[:, :, :], ALU.add))
            step(nc.vector.tensor_reduce(den[:, :], K2[:, :, :], AX.X, ALU.max))
            first_best(M[:, :, 1, :], K2[:, :, :], den[:, :])
            nc.vector.tensor_copy(EQ[:, :, :], M[:, :, 1, :]).then_inc(masked, 1)
            dve.wait_ge(exped, 1)
            step(nc.vector.tensor_reduce(tot[:, :], G[:, :, :], AX.X, ALU.add))
            step(nc.vector.reciprocal(tot[:, :], tot[:, :]))
            step(nc.vector.tensor_tensor(G[:, :, :], G[:, :, :], wide(tot[:, :]), ALU.mult))
            dve.wait_ge(placed, 1)
            dve.wait_ge(zeroed, 2)
            a3 = lambda x: x[:, :, :, :].rearrange("p t k e -> p t (k e)")
            pb = psb[:, :].rearrange("p (t q) -> p t q", q=2 * E)
            Z = N // 2
            step(nc.vector.tensor_copy(SUMS[0][:, Z:, :], pb))
            src, dst, s = *SUMS, 1
            while s < N:
                step(nc.vector.tensor_tensor(dst[:, Z:, :], src[:, Z:, :], src[:, Z - s:Z + N - s, :], ALU.add))
                src, dst, s = dst, src, 2 * s
            step(nc.vector.tensor_scalar(cnt[:, :], src[:, Z + N - 1, 0:E], float(CAP), None, ALU.min))
            step(nc.vector.tensor_tensor(a3(POS), src[:, Z:, :], pb, ALU.subtract))
            step(nc.vector.tensor_tensor(a3(POS), psa[:, :].rearrange("p (t q) -> p t q", q=2 * E), a3(POS), ALU.add))
            step(nc.vector.tensor_tensor(POS[:, :, 1, :], POS[:, :, 1, :],
                                         cnt[:, :].unsqueeze(1).to_broadcast([P, N, E]), ALU.add))
            step(nc.vector.tensor_scalar(a3(KEEP), a3(POS), float(CAP), None, ALU.is_lt))
            step(nc.vector.tensor_tensor(a3(KEEP), a3(KEEP), a3(M), ALU.mult))
            both = lambda x: x.unsqueeze(2).to_broadcast([P, N, 2, E])
            flat = lambda x: x[:, :, :, :].rearrange("p t k e -> p (t k) e")
            step(nc.vector.tensor_tensor(A[:, :, :, :], KEEP[:, :, :, :], both(G[:, :, :]), ALU.mult))
            step(nc.vector.tensor_reduce(T.weight[:, :, :].rearrange("p t k -> p (t k)"), flat(A), AX.X, ALU.add))
            step(nc.vector.tensor_tensor(tot[:, :], T.weight[:, :, 0], T.weight[:, :, 1], ALU.add))
            step(nc.vector.tensor_scalar(tot[:, :], tot[:, :], GATE_EPS, None, ALU.max))
            step(nc.vector.reciprocal(tot[:, :], tot[:, :]))
            nc.vector.tensor_tensor(T.weight[:, :, :], T.weight[:, :, :], tot[:, :].unsqueeze(2).to_broadcast([P, N, 2]), ALU.mult)
            step(nc.vector.tensor_tensor(flat(POS), flat(POS), T.places[:, 0:E].unsqueeze(1).to_broadcast([P, 2 * N, E]), ALU.add))
            step(nc.vector.tensor_tensor(a3(POS), a3(POS), a3(KEEP), ALU.mult))
            step(nc.vector.tensor_reduce(place[:, :, :].rearrange("p t k -> p (t k)"), flat(POS), AX.X, ALU.add))
            step(nc.vector.tensor_scalar(place[:, :, :], place[:, :, :], T.places[:, E:E + 1], None, ALU.add))
            nc.vector.tensor_copy(T.row[:, :, :], place[:, :, :])
            nc.vector.tensor_scalar(T.rows[:, :, D:D + 2], place[:, :, :], mark, None, ALU.add)
            nc.vector.tensor_copy(T.rows[:, :, D + 2], T.token[:, :])

        @block.gpsimd
        def _(pool):
            for sums in SUMS:
                pool.memset(sums[:, 0:N // 2, :], 0.0).then_inc(zeroed, 1)


gate_no = [0]


def experts_stage(nc, T, I, S, tag, mark, loads=(), out_x=None):
    ROUTED = 2 * len(PARTS)
    TURNS = EXPERTS // 2
    WEIGHTS = 4
    QUARTERS = 4
    QT = TILES // QUARTERS
    with ExitStack() as st:
        sem = lambda n: st.enter_context(nc.semaphore(f"{tag}_{n}"))
        first, silued, second, kept, turned, x_turned, shared_done, added, routed, out_free, zeroed = map(
            sem, ("first", "silued", "second", "kept", "turned", "x_turned", "shared_done", "added", "routed", "out_free",
                  "zeroed"))
        scattered, stored = T.scattered[tag], T.stored[tag]
        fetched, weighed = [sem(f"fetched{q}") for q in range(QUARTERS)], sem("weighed")
        ahead = sem("ahead")
        wloaded = [sem("wloaded0"), sem("wloaded1")]
        xloaded = [sem(f"xloaded{r}") for r in range(3)]
        w1 = ring(st, nc.sbuf_tensor, f"{tag}_w1", 2, [P, FF], F32)
        w2 = ring(st, nc.sbuf_tensor, f"{tag}_w2", 2, [P, FT, D], F32)
        b1 = ring(st, nc.sbuf_tensor, f"{tag}_b1", 2, [P, FT], F32)
        b2 = ring(st, nc.sbuf_tensor, f"{tag}_b2", 2, [P, D], F32)
        xin = ring(st, nc.sbuf_tensor, f"{tag}_xin", 3, [P, CT, ROW], F32)
        xt = ring(st, nc.sbuf_tensor, f"{tag}_xt", 2, [P, CH], F32)
        hid = ring(st, nc.sbuf_tensor, f"{tag}_hid", 2, [P, FT, CH], F32)
        out = ring(st, nc.sbuf_tensor, f"{tag}_out", 3, [P, CT, D], F32)
        own = st.enter_context(nc.sbuf_tensor(f"{tag}_own", [P, (EXPERTS + 1) * CAP // P], F32))
        here = st.enter_context(nc.sbuf_tensor(f"{tag}_here", [P, CT, 2], F32))
        used, to = (st.enter_context(nc.sbuf_tensor(f"{tag}_{n}", [P, CT], F32)) for n in ("used", "to"))
        goal = ring(st, nc.sbuf_tensor, f"{tag}_goal", ROUTED, [P, CT], U32)
        got = [T.spare[k][:, :].rearrange("p (t d) -> p t d", d=D) for k in range(2)]
        ps1 = ring(st, nc.psum_tensor, f"{tag}_ps1", 4, [P, CH], F32)
        ps2 = ring(st, nc.psum_tensor, f"{tag}_ps2", 2, [P, CH], F32)
        pt = ring(st, nc.psum_tensor, f"{tag}_pt", 2, [P, CH], F32)
        block = st.enter_context(nc.Block())

        def chunk(i, n):
            i, n = (i + 1, n - ROUTED) if n >= ROUTED else (i, n)
            e, part = divmod(n, len(PARTS))
            return CHUNKS + i * ROUTED + n, i * (2 * CAP) + (e * CAP + sum(PARTS[:part]) * P), PARTS[part]

        @block.sync
        def _(sp):
            def load_weights(e, a):
                sp.dma_start(w1[a][:, :], I["w1"][bass.ds(e, 1), :, :].rearrange("e h f -> h (e f)")).then_inc(wloaded[a], 16)
                sp.dma_start(w2[a][:, :, :], I["w2"][bass.ds(e, 1), :, :].rearrange("e (c p) h -> p (e c) h", p=P)
                             ).then_inc(wloaded[a], 16)
                sp.dma_start(b1[a][:, :], I["b1"][bass.ds(e, 1), :, :].rearrange("e p f -> p (e f)")).then_inc(wloaded[a], 16)
                sp.dma_start(b2[a][:, :], I["b2"][bass.ds(e, 1), :].rearrange("e h -> (e h)").partition_broadcast(P)
                             ).then_inc(wloaded[a], 16)

            def load_x(i, n):
                _, row, tiles = chunk(i, n)
                sp.dma_start(xin[n % 3][:, 0:tiles, :], S.xe[bass.ds(row, tiles * P), :].rearrange("(t p) d -> p t d", p=P)
                             ).then_inc(xloaded[n % 3], 16)

            if loads:
                sp.wait_ge(zeroed, 1)
                for k in range(2):
                    sp.dma_start(S.y[k * TOKENS:(k + 1) * TOKENS, :].rearrange("(p t) d -> p (t d)", p=P), T.spare[0][:, :]
                                 ).then_inc(ahead, 16)
            load_weights(0, 0)
            sp.wait_ge(scattered, 2 * TILES * 16)
            for n in range(3):
                load_x(0, n)
            with sp.Fori(0, TURNS) as i:
                for n in range(ROUTED):
                    c, row, tiles = chunk(i, n)
                    if n in (1, 3):
                        sp.wait_ge(kept, c + 2)
                    else:
                        sp.wait_ge(x_turned, c - CHUNKS + 3)
                    load_x(i, n + 3)
                    if n == 1:
                        load_weights(2 * i + 1, 1)
                    if n == 3:
                        load_weights(2 * i + 2, 0)
            for r in range(3):
                sp.wait_ge(xloaded[r], 16 * (2 * TURNS + 1))
            sp.wait_ge(wloaded[0], 16 * WEIGHTS * (TURNS + 1))
            if loads:
                sp.wait_ge(ahead, 16 * (len(loads) + 2))
            for r in range(3):
                sp.wait_ge(stored[r], 16 * TURNS * 2 * PARTS[r])
            for q in range(QUARTERS):
                tiles = slice(q * QT, (q + 1) * QT)
                for k in range(2):
                    row = k * TOKENS + q * QT * P
                    sp.dma_start(got[k][:, tiles, :], S.y[row:row + QT * P, :].rearrange("(t p) d -> p t d", p=P)
                                 ).then_inc(fetched[q], 16)
            if out_x is not None:
                for q in range(QUARTERS):
                    tiles = slice(q * QT, (q + 1) * QT)
                    sp.wait_ge(added, 2 * (q + 1))
                    sp.dma_start(out_x[:, tiles, :], T.X[:, tiles, :]).then_inc(ahead, 16)
                sp.wait_ge(ahead, 16 * QUARTERS)

        @block.tensor
        def _(pe):
            def up(c, w, x, cols):
                for f in range(FT):
                    pe.wait_ge(silued, c * FT + f + 1)
                    nc.tensor.matmul(ps1[f][:, 0:cols], w(f), x, start=True, stop=True).then_inc(first, 1)

            def down(c, k, w, tiles):
                pe.wait_ge(kept, c + 1)
                for f in range(FT):
                    pe.wait_ge(silued, c * FT + FT + f + 1)
                    for t in range(tiles):
                        ins = nc.tensor.matmul(ps2[k][:, t * D:(t + 1) * D], hid[k][:, f, t * P:(t + 1) * P], w(f),
                                               start=(f == 0 and t == 0), stop=(f == FT - 1 and t == tiles - 1),
                                               skip_group_check=True)
                ins.then_inc(second, 1)

            def turn(i, n):
                c, _, tiles = chunk(i, n)
                turn_no, m = (i + 1, n - ROUTED) if n >= ROUTED else (i, n)
                pe.wait_ge(xloaded[m % 3], turn_no * 32 + 16 * (m // 3) + 16)
                pe.wait_ge(x_turned, c - CHUNKS + 1)
                for t in range(tiles):
                    ins = nc.tensor.transpose(pt[m % 2][:, t * P:(t + 1) * P], xin[m % 3][:, t, 0:D], T.ident[:, :])
                ins.then_inc(turned, 1)

            shared1, shared2 = lambda f: T.sw1[:, f * P:(f + 1) * P], lambda f: T.sw2[:, f, :]
            with pe.Fori(0, CHUNKS // 4) as i:
                for a in range(4):
                    up(4 * i + a, shared1, T.XT[:, bass.ds(i * (4 * CH) + a * CH, CH)], CH)
                    if a:
                        down(4 * i + a - 1, (a - 1) % 2, shared2, CT)
                down(4 * i + 3, 1, shared2, CT)
            turn(0, 0)
            with pe.Fori(0, TURNS) as i:
                for n in range(ROUTED):
                    c, _, tiles = chunk(i, n)
                    a = n // len(PARTS)
                    turn(i, n + 1)
                    if n % len(PARTS) == 0:
                        pe.wait_ge(wloaded[a], i * (16 * WEIGHTS) + 16 * WEIGHTS)
                    pe.wait_ge(x_turned, c - CHUNKS + 3)
                    up(c, lambda f: w1[a][:, f * P:(f + 1) * P], xt[n % 2][:, 0:tiles * P], tiles * P)
                    if n:
                        p, _, before = chunk(i, n - 1)
                        down(p, (n - 1) % 2, lambda f: w2[(n - 1) // len(PARTS)][:, f, :], before)
                down(c, n % 2, lambda f: w2[a][:, f, :], tiles)

        @block.scalar
        def _(act):
            def gates(c, k, bias, cols):
                act.wait_ge(second, c + 1)
                for f in range(FT):
                    act.wait_ge(first, c * FT + f + 1)
                    nc.scalar.activation(hid[k][:, f, 0:cols], ps1[f][:, 0:cols], ACT.Silu, bias=bias[:, f:f + 1]).then_inc(silued, 1)

            act.sem_inc(silued, FT)
            act.sem_inc(second, 2)
            for buf, content in loads:
                act.dma_start(buf, content).then_inc(ahead, 16)
            with act.Fori(0, CHUNKS // 2) as i:
                for a in range(2):
                    gates(2 * i + a, a, T.sb1, CH)
            with act.Fori(0, TURNS) as i:
                for n in range(ROUTED):
                    c, _, tiles = chunk(i, n)
                    if n % len(PARTS) == 0:
                        act.wait_ge(wloaded[n // len(PARTS)], i * (16 * WEIGHTS) + 16 * WEIGHTS)
                    gates(c, n % 2, b1[n // len(PARTS)], tiles * P)
            for q in range(QUARTERS):
                act.wait_ge(fetched[q], 32)
                for t in range(q * QT, (q + 1) * QT):
                    ins = nc.scalar.activation(got[1][:, t, :], got[1][:, t, :], ACT.Identity, scale=T.weight[:, t, 1:2])
                ins.then_inc(weighed, 1)

        @block.vector
        def _(dve):
            dve.sem_inc(kept, 2)
            dve.sem_inc(x_turned, 2)
            if loads:
                dve.memset(T.spare[0][:, :], 0.0).then_inc(zeroed, 1)
            nc.vector.tensor_scalar(own[:, :], T.slot[:, :], mark, None, ALU.add).then_inc(shared_done, 1)
            with dve.Fori(0, CHUNKS // 2) as i:
                for a in range(2):
                    c = 2 * i + a
                    dve.wait_ge(second, c + 3)
                    nc.vector.tensor_tensor(out[a][:, :, :], ps2[a][:, :].rearrange("p (t d) -> p t d", d=D),
                                            T.sb2[:, :].unsqueeze(1).to_broadcast([P, CT, D]), ALU.add).then_inc(kept, 1)
                    dve.wait_ge(kept, c + 3)
                    nc.vector.tensor_scalar(out[a][:, :, :], out[a][:, :, :], SHARED, None, ALU.mult).then_inc(shared_done, 1)
                    dve.wait_ge(shared_done, 2 * c + 2)
                    xs = T.X[:, bass.ds(i * (2 * CT) + a * CT, CT), :]
                    nc.vector.tensor_tensor(xs, out[a][:, :, :], xs, ALU.add).then_inc(shared_done, 1)
            dve.wait_ge(shared_done, 2 * CHUNKS + 1)

            LINKS = 5

            def route(i, n):
                c, row, tiles = chunk(i, n)
                slot = n % ROUTED
                x = xin[n % 3]
                tile = ((i + 1) * (2 * CAP // P) if n >= ROUTED else i * (2 * CAP // P)) + \
                    (slot // len(PARTS) * (CAP // P) + sum(PARTS[:slot % len(PARTS)]))
                nowhere = T.places[:, EXPERTS:EXPERTS + 1]
                dve.wait_ge(turned, c - CHUNKS + 1)
                ops = (
                    lambda: nc.vector.tensor_tensor(here[:, 0:tiles, :], own[:, bass.ds(tile, tiles)].unsqueeze(2)
                                                    .to_broadcast([P, tiles, 2]), x[:, 0:tiles, D:D + 2], ALU.is_equal),
                    lambda: nc.vector.tensor_tensor(used[:, 0:tiles], here[:, 0:tiles, 0], here[:, 0:tiles, 1], ALU.add),
                    lambda: nc.vector.scalar_tensor_tensor(out=to[:, 0:tiles], in0=x[:, 0:tiles, D + 2], scalar=nowhere,
                                                           in1=used[:, 0:tiles], op0=ALU.subtract, op1=ALU.mult),
                    lambda: nc.vector.scalar_tensor_tensor(out=to[:, 0:tiles], in0=here[:, 0:tiles, 1], scalar=float(TOKENS),
                                                           in1=to[:, 0:tiles], op0=ALU.mult, op1=ALU.add),
                    lambda: nc.vector.tensor_scalar(goal[slot][:, 0:tiles], to[:, 0:tiles], nowhere, None, ALU.add))
                for k, op in enumerate(ops):
                    op().then_inc(routed, 1)
                    dve.wait_ge(routed, (c - CHUNKS) * LINKS + k + 1)

            def keep_x(i, n):
                c, _, tiles = chunk(i, n)
                dve.wait_ge(turned, c - CHUNKS + 1)
                nc.vector.tensor_copy(xt[n % 2][:, 0:tiles * P], pt[n % 2][:, 0:tiles * P]).then_inc(x_turned, 1)

            def keep_out(i, n):
                c, _, tiles = chunk(i, n)
                dve.wait_ge(second, c + 3)
                dve.wait_ge(out_free, c - CHUNKS + 1)
                nc.vector.tensor_tensor(out[n % 3][:, 0:tiles, :], ps2[n % 2][:, 0:tiles * D].rearrange("p (t d) -> p t d", d=D),
                                        b2[n // len(PARTS)][:, :].unsqueeze(1).to_broadcast([P, tiles, D]), ALU.add
                                        ).then_inc(kept, 1)

            dve.sem_inc(out_free, 3)
            route(0, 0)
            keep_x(0, 0)
            with dve.Fori(0, TURNS) as i:
                for n in range(ROUTED):
                    route(i, n + 1)
                    keep_x(i, n + 1)
                    if n:
                        keep_out(i, n - 1)
                keep_out(i, ROUTED - 1)

            if loads:
                dve.memset(T.XT[:, :], 0.0)
            for q in range(QUARTERS):
                dve.wait_ge(fetched[q], 32)
                for t in range(q * QT, (q + 1) * QT):
                    ins = nc.vector.scalar_tensor_tensor(out=T.X[:, t, :], in0=got[0][:, t, :], scalar=T.weight[:, t, 0:1],
                                                         in1=T.X[:, t, :], op0=ALU.mult, op1=ALU.add)
                ins.then_inc(added, 1)
                dve.wait_ge(weighed, q + 1)
                dve.wait_ge(added, 2 * q + 1)
                tiles = slice(q * QT, (q + 1) * QT)
                nc.vector.tensor_tensor(T.X[:, tiles, :], T.X[:, tiles, :], got[1][:, tiles, :], ALU.add).then_inc(added, 1)
                if out_x is None and q:
                    for t in range((q - 1) * QT, q * QT):
                        token_stats(nc, T, t)
            dve.wait_ge(added, 2 * QUARTERS)
            if out_x is None:
                for t in range((QUARTERS - 1) * QT, TILES):
                    token_stats(nc, T, t)

        @block.gpsimd
        def _(pool):
            for g in range(2 * TILES):
                pool.indirect_dma_start(out=S.xe, out_offset=bass.IndirectOffsetOnAxis(ap=T.row[:, g // 2, g % 2:g % 2 + 1], axis=0),
                                        in_=T.rows[:, g // 2, :], in_offset=None, bounds_check=SLOTS - 1, oob_is_err=False
                                        ).then_inc(scattered, 16)
            sent = [0, 0, 0]
            for m in range(TURNS * ROUTED):
                slot, r = m % ROUTED, m % 3
                pool.wait_ge(kept, CHUNKS + m + 3)
                for t in range(PARTS[r]):
                    pool.indirect_dma_start(out=S.y, out_offset=bass.IndirectOffsetOnAxis(ap=goal[slot][:, t:t + 1], axis=0),
                                            in_=out[r][:, t, :], in_offset=None, bounds_check=2 * TOKENS - 1, oob_is_err=False
                                            ).then_inc(stored[r], 16)
                sent[r] += 16 * PARTS[r]
                if m:
                    pool.wait_ge(stored[(m - 1) % 3], sent[(m - 1) % 3])
                    pool.sem_inc(out_free, 1)


RETENTION = {"r_wqkv": [P, 3 * D], "r_wff1": [P, 2, D], "r_wg": [P, D], "r_wp": [P, D], "r_wff2": [P, 2, D], "r_cols": [P, 5],
             "r_bp": [P, D], "r_cos": [P, SEQ // P, 2, D], "r_sin": [P, SEQ // P, 2, D], "r_mask": [P, 4, 4, RL],
             "r_qg": [P, D], "r_kg": [P, D], "r_diag": [P, D]}


def retention_stage(nc, T, I):
    NT = SEQ // RL
    HT = NT // 2
    TURNS = 4 + 3 * NT + 2
    AHEAD = 4 + 3
    Y_USES = (AHEAD + 3 * (NT - 1), TURNS + AHEAD - 1)
    X_USE = Y_USES[0] + 1
    WIDES = 6 + NT
    with ExitStack() as st:
        sem = lambda n: st.enter_context(nc.semaphore(f"rt_{n}"))
        (x_ready, turned, t_kept, projected, q_read, v_kept, decayed_qk, scored, masked, y_done, y_read,
         outered, m_free, wide, wide_kept, var_ready, rooted, yn_ready, gated, x_plus, chain, blank) = map(sem, (
             "x_ready", "turned", "t_kept", "projected", "q_read", "v_kept", "decayed_qk", "scored", "masked",
             "y_done", "y_read", "outered", "m_free", "wide", "wide_kept", "var_ready", "rooted", "yn_ready",
             "gated", "x_plus", "chain", "blank"))
        rotated = sem("rotated")
        sb = lambda n, shape: st.enter_context(nc.sbuf_tensor(f"rt_{n}", shape, F32))
        wqkv, wff1, wg, wp, wff2, cols, bp, cosn, sinn, mask, qg, kg, diag = (T.constants[n] for n in RETENTION)
        XH, XR = sb("xh", [P, NT, D]), sb("xr", [P, NT, D])
        XHT, XRT = sb("xht", [P, SEQ]), sb("xrt", [P, SEQ])
        GATE, GT = sb("gate", [P, SEQ]), sb("gt", [P, 2, SEQ])
        T1, T2 = sb("t1", [P, 2, D]), sb("t2", [P, 2, D])
        PAD = ring(st, nc.sbuf_tensor, "rt_pad", 2, [P, 2, HEADS, 32], F32)
        QD, KD = (ring(st, nc.sbuf_tensor, f"rt_{n}", r, [P, D], F32) for n, r in (("qd", 2), ("kd", 4)))
        VS = ring(st, nc.sbuf_tensor, "rt_vs", 4, [P, HEADS, 32], F32)
        QT = [T.XT[:, e * 4 * CH:(e + 1) * 4 * CH].rearrange("p (i j t) -> p i j t", i=4, j=4) for e in range(2)]
        KTr = ring(st, nc.sbuf_tensor, "rt_kt", 2, [P, 4, RL], F32)
        QDT = ring(st, nc.sbuf_tensor, "rt_qdt", 3, [P, RL], F32)
        YP = sb("yp", [P, 4, RL])
        pick = T.ident[:, :].rearrange("p (j e) -> p j e", e=32)[:, :, 0:HD]
        SM = ring(st, nc.sbuf_tensor, "rt_sm", 2, [P, 4, 4, RL], F32)
        STATE, UM = sb("state", [P, D]), sb("um", [P, D])
        YC, YN = sb("yc", [P, HT * HEADS, HD]), sb("yn", [P, HT * HEADS, HD])
        YT, GY = sb("yt", [P, CH]), sb("gy", [P, CH])
        mu, var = sb("mu", [P, HT * HEADS]), sb("var", [P, HT * HEADS])
        pt = ring(st, nc.psum_tensor, "rt_pt", 2, [P, CH], F32)
        pss = ring(st, nc.psum_tensor, "rt_ps", 2, [P, CH], F32)
        pq, py, pw, pm = (st.enter_context(nc.psum_tensor(f"rt_{n}", [P, CH], F32)) for n in ("pq", "py", "pw", "pm"))
        block = st.enter_context(nc.Block())

        def kept_after_tile(k):
            return 4 + 3 * (k + 1)

        def use_of_widen(n):
            return max(2 * n - 1, 0)

        def use_of_values(k):
            return 2 * k + 2 if k < 5 else 6 + k

        @block.tensor
        def _(pe):
            b = 0
            uses = [0]

            def turn_into(rows, src):
                n = uses[0]
                pe.wait_ge(t_kept, b * TURNS + n + 1)
                for k, piece in enumerate(src):
                    ins = nc.tensor.transpose(pt[n % 2][0:rows, k * P:(k + 1) * P], piece, T.ident[:, :])
                ins.then_inc(turned, 1)
                uses[0] += 1

            def project(s, k):
                pe.wait_ge(q_read, s * NT + k + 1)
                pe.wait_ge(v_kept, s * NT + k + 1)
                nc.tensor.matmul(pq[:, 0:3 * D], XRT[:, k * RL:(k + 1) * RL], wqkv[:, :],
                                 start=True, stop=True).then_inc(projected, 1)

            def turn_qk(s, k):
                pe.wait_ge(rotated, s * NT + k + 1)
                padded = lambda w: [PAD[k % 2][:, w, 4 * i:4 * i + 4, :].rearrange("p h d -> p (h d)") for i in range(4)]
                turn_into(P, padded(1))
                pe.wait_ge(decayed_qk, s * NT + k + 1)
                turn_into(P, [QD[k % 2][:, :]])
                turn_into(P, padded(0))

            def score(k, i):
                pe.wait_ge(masked, (b * NT + k) * 4 + i + 1)
                if i == 0:
                    pe.wait_ge(t_kept, b * TURNS + 2 + kept_after_tile(k))
                nc.tensor.matmul(pss[i % 2][:, :], KTr[k % 2][:, i, :], QT[k % 2][:, i, :, :],
                                 start=True, stop=True).then_inc(scored, 1)

            def values(k):
                pe.wait_ge(wide_kept, b * WIDES + use_of_values(k) + 1)
                pe.wait_ge(v_kept, b * NT + k + 2)
                for i in range(4):
                    pe.wait_ge(masked, (b * NT + k) * 4 + i + 3)
                    for j in range(4):
                        ins = nc.tensor.matmul(pw[32 * j:32 * (j + 1), i * RL:(i + 1) * RL], VS[k % 4][:, 4 * i + j, :],
                                               SM[k % 2][:, i, j, :], start=True, stop=True,
                                               tile_position=(0, 32 * j), skip_group_check=True)
                ins.then_inc(wide, 1)

            def gather(k):
                o = k % HT * D
                if k % HT == 0:
                    pe.wait_ge(y_read, b * 2 + k // HT + 1)
                if k:
                    pe.wait_ge(m_free, b * (NT + 1) + k + 1)
                    nc.tensor.matmul(py[:, o:o + D], QDT[k % 3][:, :], STATE[:, :], start=True, stop=False,
                                     skip_group_check=True)
                pe.wait_ge(wide_kept, b * WIDES + use_of_values(k) + 2)
                for i in range(4):
                    ins = nc.tensor.matmul(py[:, o + i * 32:o + (i + 1) * 32], YP[:, i, :], pick,
                                           start=(k == 0 and i == 0), stop=(i == 3), skip_group_check=True)
                ins.then_inc(y_done, 1)

            def outer(k):
                pe.wait_ge(m_free, b * (NT + 1) + k + 1)
                pe.wait_ge(decayed_qk, b * NT + k + 1)
                nc.tensor.matmul(pm[:, 0:D], KD[k % 4][:, :], VS[k % 4][:, :, 0:HD], start=True, stop=True).then_inc(outered, 1)

            def widen(n):
                pe.wait_ge(wide_kept, b * WIDES + use_of_widen(n) + 1)
                w, x = (wg[:, :], XHT) if n < 2 else (wff1[:, (n - 2) // 2, :], XRT)
                nc.tensor.matmul(pw[:, :], w, x[:, n % 2 * CH:(n % 2 + 1) * CH], start=True, stop=True).then_inc(wide, 1)

            def finish(half):
                pe.wait_ge(gated, b * 2 + half + 1)
                pe.wait_ge(wide_kept, b * WIDES + use_of_widen(5) + 2)
                pe.wait_ge(m_free, b * (NT + 1) + NT + half)
                for k in range(HT):
                    out = pm[:, k * D:(k + 1) * D]
                    for f in range(2):
                        nc.tensor.matmul(out, GT[:, f, half * CH + k * P:half * CH + (k + 1) * P], wff2[:, f, :],
                                         start=(k == 0 and f == 0), stop=False, skip_group_check=True)
                    ins = nc.tensor.matmul(out, GY[:, k * P:(k + 1) * P], wp[:, :], start=False, stop=(k == HT - 1),
                                           skip_group_check=True)
                ins.then_inc(outered, 1)

            def turn_y(half):
                pe.wait_ge(yn_ready, b * 2 + half + 1)
                turn_into(P, [YN[:, k * HEADS:(k + 1) * HEADS, :].rearrange("p h d -> p (h d)") for k in range(HT)])

            def turn_x(s, n):
                pe.wait_ge(x_ready, s * 4 + n + 1)
                src = (XH, XR)[n % 2]
                turn_into(P, [src[:, n // 2 * HT + k, :] for k in range(HT)])

            for n in range(4):
                turn_x(0, n)
            pe.wait_ge(t_kept, 2 + 4)
            project(0, 0)
            project(0, 1)
            turn_qk(0, 0)
            with pe.Fori(0, BATCH) as b:
                uses = [AHEAD]
                for k in range(NT):
                    if k < 6:
                        widen(k)
                    score(k, 0)
                    score(k, 1)
                    if k:
                        values(k - 1)
                    score(k, 2)
                    if k + 1 < NT:
                        turn_qk(b, k + 1)
                    else:
                        turn_x(b + 1, 0)
                        turn_x(b + 1, 1)
                    score(k, 3)
                    if k + 2 < NT:
                        project(b, k + 2)
                    if k:
                        gather(k - 1)
                        outer(k - 1)
                    if k == 6:
                        turn_y(0)
                turn_x(b + 1, 2)
                turn_x(b + 1, 3)
                values(NT - 1)
                pe.wait_ge(t_kept, b * TURNS + 2 + X_USE + 4)
                project(b + 1, 0)
                gather(NT - 1)
                project(b + 1, 1)
                finish(0)
                turn_qk(b + 1, 0)
                turn_y(1)
                finish(1)
                assert uses[0] == TURNS + AHEAD

        @block.scalar
        def _(act):
            act.sem_inc(t_kept, 2)
            act.sem_inc(v_kept, 1)
            act.sem_inc(wide_kept, 1)
            b = 0
            uses = [0]

            def keep(out, cols=CH, **how):
                n = uses[0]
                act.wait_ge(turned, b * TURNS + n + 1)
                nc.scalar.activation(out, pt[n % 2][:, 0:cols], ACT.Identity, **how).then_inc(t_kept, 1)
                uses[0] += 1

            def keep_v(s, k):
                act.wait_ge(q_read, s * NT + k + 2)
                nc.scalar.copy(VS[k % 4][:, :, 0:HD], pq[:, 2 * D:3 * D].rearrange("p (h e) -> p h e", e=HD)
                               ).then_inc(v_kept, 1)

            def keep_qk(k):
                keep(KTr[k % 2][:, :, :].rearrange("p i t -> p (i t)"))
                keep(QDT[k % 3][:, :], RL)
                n = uses[0]
                act.wait_ge(turned, b * TURNS + n + 1)
                for j in range(4):
                    rows = slice(32 * j, 32 * (j + 1))
                    ins = nc.scalar.copy(QT[k % 2][rows, :, j, :], pt[n % 2][rows, :].rearrange("p (i t) -> p i t", t=RL))
                ins.then_inc(t_kept, 1)
                uses[0] += 1

            def keep_values(k):
                act.wait_ge(wide, b * WIDES + use_of_values(k) + 1)
                nc.scalar.copy(YP[:, :, :].rearrange("p i t -> p (i t)"), pw[:, :]).then_inc(wide_kept, 1)

            def keep_wide(n):
                act.wait_ge(wide, b * WIDES + use_of_widen(n) + 1)
                if n < 2:
                    nc.scalar.activation(GATE[:, n * CH:(n + 1) * CH], pw[:, :], ACT.Silu, bias=cols[:, 3:4]).then_inc(wide_kept, 1)
                else:
                    nc.scalar.activation(GT[:, (n - 2) // 2, n % 2 * CH:(n % 2 + 1) * CH], pw[:, :], ACT.Gelu).then_inc(wide_kept, 1)

            def root(half):
                act.wait_ge(var_ready, b * 2 + half + 1)
                nc.scalar.activation(var[:, :], var[:, :], ACT.Sqrt).then_inc(rooted, 1)

            def keep_y():
                keep(YT[:, :], scale=cols[:, 1:2], bias=cols[:, 2:3])

            def keep_x(n):
                half = slice(n // 2 * CH, (n // 2 + 1) * CH)
                if n % 2:
                    keep(XRT[:, half], scale=cols[:, 0:1])
                else:
                    keep(XHT[:, half])

            for n in range(4):
                keep_x(n)
            keep_v(0, 0)
            keep_v(0, 1)
            keep_qk(0)
            with act.Fori(0, BATCH) as b:
                uses = [AHEAD]
                for k in range(NT):
                    if k < 6:
                        keep_wide(k)
                    if k:
                        keep_values(k - 1)
                    if k + 1 < NT:
                        keep_qk(k + 1)
                    if k + 2 < NT:
                        keep_v(b, k + 2)
                    if k == 5:
                        root(0)
                    if k == 6:
                        keep_y()
                for n in range(4):
                    keep_x(n)
                keep_values(NT - 1)
                keep_v(b + 1, 0)
                keep_v(b + 1, 1)
                keep_qk(0)
                root(1)
                keep_y()

        @block.vector
        def _(dve):
            dve.sem_inc(q_read, 1)
            dve.sem_inc(masked, 2)
            dve.sem_inc(y_read, 1)
            dve.sem_inc(m_free, 1)
            dve.wait_ge(blank, 3 + 4)
            b = 0
            CHAIN = NT * 2 + (NT - 2) + 2 * 6
            link = Count(dve, chain)

            def step(ins):
                link.mark(ins)
                link.settle()

            def normalise(s, n):
                half, dst, inv = n // 2, (XH, XR)[n % 2], (T.pad["rs"], T.pad["ri"])[n % 2]
                for k in range(half * HT, (half + 1) * HT):
                    t = s * NT + k
                    ins = nc.vector.tensor_scalar(dst[:, k, :], T.pad["X"][:, bass.ds(t, 1), :].rearrange("p t d -> p (t d)"),
                                                  T.pad["mv"][:, bass.ds(t, 1), 0:1].rearrange("p t s -> p (t s)"),
                                                  inv[:, bass.ds(t, 1)], ALU.subtract, ALU.mult)
                ins.then_inc(x_ready, 1)

            def rotate(s, k):
                dve.wait_ge(projected, s * NT + k + 1)
                if k >= 2:
                    dve.wait_ge(decayed_qk, s * NT + k - 1)
                qk = pq[:, 0:2 * D].rearrange("p (w d) -> p w d", w=2)
                link.mark(nc.vector.tensor_tensor(T1[:, :, :], qk, cosn[:, k, :, :], ALU.mult))
                link.mark(nc.vector.tensor_tensor(T2[:, :, 0:D:2], qk[:, :, 1:D:2], sinn[:, k, :, 0:D:2], ALU.mult))
                nc.vector.tensor_tensor(T2[:, :, 1:D:2], qk[:, :, 0:D:2], sinn[:, k, :, 1:D:2], ALU.mult).then_inc(q_read, 1)
                link.settle()
                dve.wait_ge(q_read, s * NT + k + 2)
                v = lambda a: a[:, :, :].rearrange("p w (h d) -> p w h d", d=HD)
                nc.vector.tensor_tensor(PAD[k % 2][:, :, :, 0:HD], v(T1), v(T2), ALU.add).then_inc(rotated, 1)
                dve.wait_ge(rotated, s * NT + k + 1)

            def decay_scores(k, i):
                dve.wait_ge(scored, (b * NT + k) * 4 + i + 1)
                nc.vector.tensor_tensor(SM[k % 2][:, i, :, :], pss[i % 2][:, :].rearrange("p (j t) -> p j t", t=RL),
                                        mask[:, i, :, :], ALU.mult).then_inc(masked, 1)

            def carry(k):
                dve.wait_ge(outered, b * (NT + 1) + k + 1)
                if k == 0:
                    nc.vector.tensor_tensor(STATE[:, :], pm[:, 0:D], diag[:, :], ALU.mult).then_inc(m_free, 1)
                    return
                step(nc.vector.tensor_tensor(UM[:, :], pm[:, 0:D], diag[:, :], ALU.mult))
                dve.wait_ge(m_free, b * (NT + 1) + k + 1)
                nc.vector.scalar_tensor_tensor(out=STATE[:, :], in0=STATE[:, :], scalar=cols[:, 4:5], in1=UM[:, :],
                                               op0=ALU.mult, op1=ALU.add).then_inc(m_free, 1)

            def group_norm_a(half):
                dve.wait_ge(y_done, b * NT + (half + 1) * HT)
                y = py[:, :].rearrange("p (h d) -> p h d", d=HD)
                step(nc.vector.tensor_reduce(mu[:, :], y, AX.X, ALU.add))
                step(nc.vector.tensor_scalar(mu[:, :], mu[:, :], 1.0 / HD, None, ALU.mult))
                nc.vector.tensor_tensor(YC[:, :, :], y, mu[:, :].unsqueeze(2).to_broadcast([P, HT * HEADS, HD]),
                                        ALU.subtract).then_inc(y_read, 1)
                dve.wait_ge(y_read, b * 2 + half + 2)
                step(nc.vector.tensor_tensor(YN[:, :, :], YC[:, :, :], YC[:, :, :], ALU.mult))
                step(nc.vector.tensor_reduce(var[:, :], YN[:, :, :], AX.X, ALU.add))
                nc.vector.tensor_scalar(var[:, :], var[:, :], 1.0 / HD, GN_EPS, ALU.mult, ALU.add).then_inc(var_ready, 1)

            def group_norm_b(half):
                dve.wait_ge(rooted, b * 2 + half + 1)
                step(nc.vector.reciprocal(mu[:, :], var[:, :]))
                nc.vector.tensor_tensor(YN[:, :, :], YC[:, :, :], mu[:, :].unsqueeze(2).to_broadcast([P, HT * HEADS, HD]),
                                        ALU.mult).then_inc(yn_ready, 1)

            def absorb(half):
                dve.wait_ge(x_plus, b * 2 + half + 1)
                xs = T.X[:, bass.ds(b * NT + half * HT, HT), :]
                step(nc.vector.tensor_tensor(xs, xs, XH[:, half * HT:(half + 1) * HT, :], ALU.add))

            def add(half):
                xs = T.X[:, bass.ds(b * NT + half * HT, HT), :]
                dve.wait_ge(outered, b * (NT + 1) + NT + half)
                nc.vector.tensor_tensor(xs, pm[:, :].rearrange("p (t d) -> p t d", d=D), xs, ALU.add).then_inc(m_free, 1)
                dve.wait_ge(m_free, b * (NT + 1) + NT + half + 1)
                for k in range(half * HT, (half + 1) * HT):
                    nc.vector.bn_stats(T.bn[:, bass.ds(b * NT + k, 1), :].rearrange("p t s -> p (t s)"),
                                       T.X[:, bass.ds(b * NT + k, 1), :].rearrange("p t d -> p (t d)"))

            for n in range(4):
                normalise(0, n)
            rotate(0, 0)
            rotate(0, 1)
            with dve.Fori(0, BATCH) as b:
                link = Count(dve, chain, b, CHAIN)
                link.n = 2 * 2
                for k in range(NT):
                    decay_scores(k, 0)
                    if k == 5:
                        group_norm_a(0)
                    decay_scores(k, 1)
                    if k >= 2:
                        carry(k - 2)
                    if k in (2, 3):
                        absorb(k - 2)
                    if k == 7:
                        normalise(b + 1, 2)
                    decay_scores(k, 2)
                    if k + 2 < NT:
                        rotate(b, k + 2)
                    if k == 6:
                        group_norm_b(0)
                        normalise(b + 1, 0)
                    if k == 7:
                        normalise(b + 1, 3)
                    decay_scores(k, 3)
                    if k == 6:
                        normalise(b + 1, 1)
                carry(NT - 2)
                rotate(b + 1, 0)
                rotate(b + 1, 1)
                group_norm_a(1)
                add(0)
                group_norm_b(1)
                add(1)
                assert link.n == CHAIN + 2 * 2

        @block.gpsimd
        def _(pool):
            for e in range(2):
                pool.memset(PAD[e][:, :, :, :], 0.0).then_inc(blank, 1)
            pool.memset(STATE[:, :], 0.0).then_inc(blank, 1)
            for e in range(4):
                pool.memset(VS[e][:, :, :], 0.0).then_inc(blank, 1)
            b = 0
            def decay_qk(s, k):
                pool.wait_ge(rotated, s * NT + k + 1)
                h = lambda a: a[:, :].rearrange("p (h d) -> p h d", d=HD)
                pool.tensor_tensor(h(KD[k % 4]), PAD[k % 2][:, 1, :, 0:HD], h(kg), ALU.mult)
                pool.tensor_tensor(h(QD[k % 2]), PAD[k % 2][:, 0, :, 0:HD], h(qg), ALU.mult).then_inc(decayed_qk, 1)

            def plus(half):
                pool.wait_ge(turned, b * TURNS + AHEAD - 1)
                xs = XH[:, half * HT:(half + 1) * HT, :]
                pool.tensor_tensor(xs, xs, bp[:, :].unsqueeze(1).to_broadcast([P, HT, D]), ALU.add).then_inc(x_plus, 1)

            def gate(half):
                pool.wait_ge(t_kept, b * TURNS + 2 + Y_USES[half] + 1)
                pool.wait_ge(wide_kept, b * WIDES + 2 + use_of_widen(half))
                pool.tensor_tensor(GY[:, :], YT[:, :], GATE[:, half * CH:(half + 1) * CH], ALU.mult).then_inc(gated, 1)

            decay_qk(0, 0)
            decay_qk(0, 1)
            with pool.Fori(0, BATCH) as b:
                for k in range(NT):
                    if k in (0, 1):
                        plus(k)
                    if k == 6:
                        gate(0)
                    if k + 2 < NT:
                        decay_qk(b, k + 2)
                decay_qk(b + 1, 0)
                decay_qk(b + 1, 1)
                gate(1)


def block_kernel(nc, I, out):
    T, S = Buffers(), Buffers()
    with ExitStack() as st:
        sb = lambda n, shape, dt=F32: st.enter_context(nc.sbuf_tensor(n, shape, dt))
        T.pad = {n: sb(n, [P, TILES + SEQ // P] + more) for n, more in (("X", [D]), ("mv", [2]), ("rs", []), ("ri", []))}
        T.X, T.mv = (T.pad[n][:, 0:TILES, :] for n in ("X", "mv"))
        T.rs, T.ri = (T.pad[n][:, 0:TILES] for n in ("rs", "ri"))
        T.XT = sb("XT", [P, TOKENS])
        T.V = sb("V", [P, GROUPS + 1, KT, JH * HD])
        T.rows = T.V[:, :, :, :].rearrange("p g t e -> p (g t e)").rearrange("p (t r) -> p t r", r=ROW)
        T.XH = T.rows[:, :, 0:D]
        T.ident, T.ones, T.upper, T.bo = (sb(n, [P, P]) for n in ("ident", "ones", "upper", "bo"))
        T.rank = sb("rank", [P, EXPERTS])
        T.bn, T.sd = sb("bn", [P, TILES, 6]), sb("sd", [P, TILES])
        T.spare = [sb(f"spare{e}", [P, TOKENS]) for e in range(2)]
        T.sw1, T.sw2, T.rw = sb("sw1", [P, FF]), sb("sw2", [P, FT, D]), sb("rw", [P, EXPERTS])
        T.sb1, T.sb2, T.places = sb("sb1", [P, FT]), sb("sb2", [P, D]), sb("places", [P, EXPERTS + 1])
        T.token, T.slot = sb("token", [P, TILES]), sb("slot", [P, (EXPERTS + 1) * CAP // P])
        T.weight, T.row = sb("weight", [P, TILES, 2]), sb("row", [P, TILES, 2], U32)
        T.filled = st.enter_context(nc.semaphore("filled"))
        T.scattered = {n: st.enter_context(nc.semaphore(f"{n}_scattered")) for n in ("ex2", "ex4")}
        T.stored = {n: [st.enter_context(nc.semaphore(f"{n}_stored{r}")) for r in range(3)] for n in ("ex2", "ex4")}
        dr = lambda n, shape, dt=F32: nc.dram_tensor(n, shape, dt, kind="Internal").ap()
        S.q, S.k = (dr(n, [GROUPS + 2, JH, QROWS, SEQ], BF16) for n in ("s_q", "s_k"))
        S.low = dr("s_low", [GROUPS + 1, JH, 3, SEQ], BF16)
        S.o = dr("s_o", [GROUPS + 1, JH, HD + 1, SEQ])
        S.inv = dr("s_inv", [BATCH * HEADS, SEQ])
        S.xe = dr("s_xe", [(EXPERTS + 1) * CAP, ROW])
        S.y = dr("s_y", [2 * TOKENS, D])

        load_stage(nc, T, I, S)
        norm_stage(nc, T, "ln1")
        with ExitStack() as own:
            T.hk, T.eq, T.ek = (ring(own, nc.sbuf_tensor, f"at_{n}", 2, [P, rows, SEQ], BF16)
                                for n, rows in (("hk", 2), ("eq", JH), ("ek", 2)))
            T.vst = ring(own, nc.sbuf_tensor, "at_v", 2, [P, KT, JH, VW], F32)
            qkv_stage(nc, T, I, S)
            attention_stage(nc, T, S)
        output_stage(nc, T, I, S)

        def mixture(n, **more):
            with nc.psum_tensor(f"logits{n}", [P, CH], F32) as logits:
                norm_stage(nc, T, f"ln{n}", logits=logits)
                gate_stage(nc, T, logits, MARKS[n])
            experts_stage(nc, T, I, S, f"ex{n}", MARKS[n], **more)
        with ExitStack() as own:
            T.constants = {n: own.enter_context(nc.sbuf_tensor(n, shape, F32)) for n, shape in RETENTION.items()}
            whole = lambda buf: buf[(slice(None),) * len(buf.shape)]
            mixture(2, loads=[(whole(T.constants[n]), I[n].partition_broadcast(P) if n == "r_bp" else I[n]) for n in RETENTION])
            norm_stage(nc, T, "ln3", turn=False)
            retention_stage(nc, T, I)
        mixture(4, out_x=out.rearrange("b (t p) d -> p (b t) d", p=P))


def _arrange(v):
    import numpy as np
    g = {k: np.asarray(a) for k, a in v.items()}
    a, b, f = "L0_attn_a_", "L0_attn_b_", "L0_ffn_"
    w = g[a + "W_qkv"].reshape(HEADS, 3, HD, D)
    o = {
        "x": g[a + "x"],
        "w_qkv": w.transpose(3, 1, 0, 2).reshape(D, 3, D),
        "b_qkv": g[a + "b_qkv"].reshape(HEADS, 3, HD).transpose(0, 2, 1).reshape(D, 3),
        "w_out": g[a + "W_out"].T, "b_out": g[a + "b_out"],
        "rw": g[f + "router_w"], 
        "w1": np.concatenate([g[f + "w1"], g[f + "sw1"][None]]), "w2": np.concatenate([g[f + "w2"], g[f + "sw2"][None]]),
        "b1": np.concatenate([g[f + "b1"], g[f + "sb1"][None]]).reshape(EXPERTS + 1, FT, P).transpose(0, 2, 1),
        "b2": np.concatenate([g[f + "b2"], g[f + "sb2"][None]]),
        "places": np.concatenate([np.arange(EXPERTS)[None] * CAP - SLOTS - np.arange(P)[:, None],
                                  SLOTS + np.arange(P)[:, None]], axis=1).astype(np.float32),
        "token": np.arange(TOKENS).reshape(TILES, P).T.astype(np.float32),
        "slot": np.arange((EXPERTS + 1) * CAP).reshape(-1, P).T.astype(np.float32),
        "upper": np.triu(np.ones((P, P), np.float32), 1),
        "rank": np.arange(EXPERTS, 0, -1).astype(np.float32),
    }
    wq = g[b + "w_qkvff"]
    half = D // 2
    f32 = np.float32
    scale_vec = (np.arange(0, D, 2, dtype=f32) + f32(0.4 * D)) / f32(1.4 * D)
    power = np.arange(-(SEQ // 2), SEQ // 2, dtype=f32) / f32(64)
    scale = (scale_vec[None, :] ** power[:, None]).astype(f32)
    inv_freq = (f32(1.0) / f32(10000.0) ** (np.arange(half, dtype=f32) / f32(half))).astype(f32)
    angle = (np.arange(SEQ, dtype=f32)[:, None] * inv_freq[None, :]).astype(f32)
    sin, cos = np.sin(angle), np.cos(angle)
    both = np.stack([scale, f32(1.0) / scale])
    sign = np.tile(np.array([-1.0, 1.0], f32), half)
    cosn = np.repeat(cos * both, 2, axis=-1)
    sinn = np.repeat(sin * both, 2, axis=-1) * sign
    lay = lambda t: t.reshape(2, SEQ // P, P, D).transpose(2, 1, 0, 3)
    gamma = 1.0 - 2.0 ** (-5.0 - np.arange(HEADS, dtype=np.float64))
    at = np.arange(RL)
    diff = at[None, :] - at[:, None]
    mask = np.where(diff >= 0, gamma[:, None, None] ** np.maximum(diff, 0), 0.0) * HD ** -0.5
    head = np.repeat(np.arange(HEADS), HD)
    o.update({
        "r_wqkv": wq[:3 * D].T, "r_wff1": wq[3 * D:].T.reshape(D, 2, D), "r_wg": g[b + "w_gated"].T,
        "r_wp": g[b + "w_proj"].T, "r_wff2": g[b + "w_ff"].T.reshape(2, D, D).transpose(1, 0, 2),
        "r_cols": np.stack([g[b + "rms_w"], g[b + "gn_w"], g[b + "gn_b"], g[b + "b_gated"],
                            (gamma[head] ** RL).astype(f32)], axis=1),
        "r_bp": g[b + "b_proj"], "r_cos": lay(cosn), "r_sin": lay(sinn),
        "r_mask": mask.astype(f32).reshape(4, 4, RL, RL).transpose(2, 0, 1, 3),
        "r_qg": (gamma[head][None, :] ** at[:, None] * HD ** -0.5).astype(f32),
        "r_kg": (gamma[head][None, :] ** (RL - at)[:, None]).astype(f32),
        "r_diag": (head[:, None] == head[None, :]).astype(f32),
    })
    return {k: np.ascontiguousarray(x) for k, x in o.items()}


def build(nc, arrays):
    I = {}
    for name, x in arrays.items():
        I[name] = nc.dram_tensor(f"in_{name}", x.shape, mybir.dt.from_np(x.dtype), kind="ExternalInput").ap()
    out = nc.dram_tensor("out_x", (BATCH, SEQ, D), F32, kind="ExternalOutput").ap()
    block_kernel(nc, I, out)


def kernel(**inputs):
    import concourse.bacc as bacc
    from concourse.bass_utils import run_bass_kernel_spmd

    arrays = _arrange(inputs)
    nc = bacc.Bacc("TRN2", target_bir_lowering=False, num_devices=1)
    build(nc, arrays)
    r = run_bass_kernel_spmd(nc, [{f"in_{k}": v for k, v in arrays.items()}], core_ids=[0])
    return r.results[0]["out_x"]
```
